# Optimizing a Trainium2 kernel written in Bass

```python
import numpy as np
import jax
import jax.numpy as jnp

def _softmax(x, axis=-1):
    return jax.nn.softmax(x, axis=axis)

def _gelu(x):
    return jax.nn.gelu(x, approximate=True)

def _silu(x):
    return jax.nn.silu(x)

def _sigmoid(x):
    return jax.nn.sigmoid(x)

def _layernorm(x, axis=-1, eps=1e-05):
    m = jnp.mean(x, axis=axis, keepdims=True)
    v = jnp.var(x, axis=axis, keepdims=True)
    return (x - m) / jnp.sqrt(v + eps)

def _scatter_add(tgt, idx, src, axis=0):
    return tgt.at[idx].add(src)

def _segment_sum(src, seg, n):
    return jax.ops.segment_sum(src, seg, n)
kernel_name = 'mk_flamingo_gated_d2_seqx_r8_8a6340'

def setup_inputs(seed: int=0):
    np.random.seed(seed)
    _w = jnp.asarray

    def _rec_inputs():
        import jax
        import jax.numpy as jnp
        _rk = jax.random.key(seed)
        x = -0.000125 + 0.9999 * jax.random.normal(jax.random.fold_in(_rk, 1), (32, 128, 128), jnp.float32)
        _lenS = 128 - jax.random.randint(jax.random.fold_in(_rk, 7), (32,), 0, max(1, 128 // 4) + 1, jnp.int32)
        _lenS2 = 120 - jax.random.randint(jax.random.fold_in(_rk, 8), (32,), 0, max(1, 120 // 4) + 1, jnp.int32)
        _ctx_768P = jax.random.normal(jax.random.fold_in(_rk, 11), (32, 16, 96), jnp.float32)
        _ctx_768c = jax.random.dirichlet(jax.random.fold_in(_rk, 511), 0.3 * jnp.ones((16,), jnp.float32), (32, 120))
        _ctx_768t = jnp.einsum('bsk,bkd->bsd', _ctx_768c, _ctx_768P)
        _ctx_768t = _ctx_768t * jax.lax.rsqrt(jnp.mean(jnp.square(_ctx_768t)) + 1e-12) * 0.953939
        ctx_768 = 0.00243539 + 0.99952 * (_ctx_768t + 0.3 * jax.random.normal(jax.random.fold_in(_rk, 611), (32, 120, 96), jnp.float32))
        _g = jax.random.normal(jax.random.fold_in(_rk, 9001), (2, 2), jnp.float32)
        _g = jnp.sign(_g) * jnp.maximum(jnp.abs(_g), 1.0) + (_g == 0) * 1.0
        g_xattn = _g[0]
        g_ffn = _g[1]
        return (x, ctx_768, g_xattn, g_ffn)
    x, ctx_768, g_xattn, g_ffn = _rec_inputs()

    def _L0_xattn_setup():
        import jax, jax.numpy as jnp
        import numpy as np
        HEADS = 16
        DIM_HEAD = 64
        RANK = 32
        LORA_W = 1.0
        IPA_SCALE = 1.0
        IPA_TOKENS = 4
        SCALE = DIM_HEAD ** (-0.5)

        def _split_heads(t):
            b, n, _ = t.shape
            return t.reshape(b, n, HEADS, DIM_HEAD).transpose(0, 2, 1, 3)

        def _merge_heads(t):
            b, h, n, d = t.shape
            return t.transpose(0, 2, 1, 3).reshape(b, n, h * d)

        def _attention(q_in, k_in, v_in):
            q = _split_heads(q_in)
            k = _split_heads(k_in)
            v = _split_heads(v_in)
            s = jnp.einsum('bhid,bhjd->bhij', q, k) * SCALE
            p = jax.nn.softmax(s, axis=-1)
            o = jnp.einsum('bhij,bhjd->bhid', p, v)
            return _merge_heads(o)

        def _lora(t, down, up, alpha):
            return t @ down @ up * (LORA_W * alpha[0] / RANK)
        key = jax.random.key(seed)
        ks = jax.random.split(key, 20)
        B, N, QD, CD, ID = (8, 512, 128, 96, HEADS * DIM_HEAD)
        CTX = 77 + IPA_TOKENS
        s = 0.02
        return {'x': jax.random.normal(ks[0], (B, N, QD), jnp.float32), 'context': jax.random.normal(ks[1], (B, CTX, CD), jnp.float32), 'Wq': jax.random.normal(ks[2], (QD, ID), jnp.float32) * s, 'Wk': jax.random.normal(ks[3], (CD, ID), jnp.float32) * s, 'Wv': jax.random.normal(ks[4], (CD, ID), jnp.float32) * s, 'Wo': jax.random.normal(ks[5], (ID, QD), jnp.float32) * s, 'bo': jnp.zeros((QD,), jnp.float32), 'q_down': jax.random.normal(ks[6], (QD, RANK), jnp.float32) * s, 'q_up': jax.random.normal(ks[7], (RANK, ID), jnp.float32) * s, 'q_alpha': jnp.ones((1,), jnp.float32) * RANK, 'k_down': jax.random.normal(ks[8], (CD, RANK), jnp.float32) * s, 'k_up': jax.random.normal(ks[9], (RANK, ID), jnp.float32) * s, 'k_alpha': jnp.ones((1,), jnp.float32) * RANK, 'v_down': jax.random.normal(ks[10], (CD, RANK), jnp.float32) * s, 'v_up': jax.random.normal(ks[11], (RANK, ID), jnp.float32) * s, 'v_alpha': jnp.ones((1,), jnp.float32) * RANK, 'o_down': jax.random.normal(ks[12], (ID, RANK), jnp.float32) * s, 'o_up': jax.random.normal(ks[13], (RANK, QD), jnp.float32) * s, 'o_alpha': jnp.ones((1,), jnp.float32) * RANK, 'Wk_ipa': jax.random.normal(ks[14], (CD, ID), jnp.float32) * s, 'Wv_ipa': jax.random.normal(ks[15], (CD, ID), jnp.float32) * s}
    _L0_xattn_all = _L0_xattn_setup()
    _L0_xattn_in = {k: v for k, v in _L0_xattn_all.items() if k in ('Wq', 'Wk', 'Wv', 'Wo', 'bo', 'q_down', 'q_up', 'q_alpha', 'k_down', 'k_up', 'k_alpha', 'v_down', 'v_up', 'v_alpha', 'o_down', 'o_up', 'o_alpha', 'Wk_ipa', 'Wv_ipa')}
    del _L0_xattn_all

    def _L0_ffn_setup():
        import jax, jax.numpy as jnp
        import numpy as np
        H = 128
        E = 8
        FFN = 512
        TOP_K = 2
        key = jax.random.key(seed)
        ks = jax.random.split(key, 6)
        s_h = 1.0 / np.sqrt(H)
        s_f = 1.0 / np.sqrt(FFN)
        return {'hidden_states': jax.random.normal(ks[0], (4, 128, H), dtype=jnp.float32), 'router_w': jax.random.uniform(ks[1], (E, H), jnp.float32, -s_h, s_h), 'w1': jax.random.uniform(ks[2], (E, FFN, H), jnp.float32, -s_h, s_h), 'b1': jax.random.uniform(ks[3], (E, FFN), jnp.float32, -s_h, s_h), 'w2': jax.random.uniform(ks[4], (E, H, FFN), jnp.float32, -s_f, s_f), 'b2': jax.random.uniform(ks[5], (E, H), jnp.float32, -s_f, s_f)}
    _L0_ffn_all = _L0_ffn_setup()
    _L0_ffn_in = {k: v for k, v in _L0_ffn_all.items() if k in ('router_w', 'w1', 'b1', 'w2', 'b2')}
    del _L0_ffn_all

    def _L1_xattn_setup():
        import jax, jax.numpy as jnp
        import numpy as np
        IMG_DIM, TXT_DIM, HID = (128, 96, 128)
        B, LQ, LK = (8, 256, 256)
        key = jax.random.key(seed)
        ks = jax.random.split(key, 8)
        s_img = 1.0 / np.sqrt(IMG_DIM)
        s_txt = 1.0 / np.sqrt(TXT_DIM)
        return {'image_features': jax.random.normal(ks[0], (B, LQ, IMG_DIM), jnp.float32), 'text_features': jax.random.normal(ks[1], (B, LK, TXT_DIM), jnp.float32), 'Wq': jax.random.uniform(ks[2], (IMG_DIM, HID), jnp.float32, -s_img, s_img), 'bq': jax.random.uniform(ks[3], (HID,), jnp.float32, -s_img, s_img), 'Wk': jax.random.uniform(ks[4], (TXT_DIM, HID), jnp.float32, -s_txt, s_txt), 'bk': jax.random.uniform(ks[5], (HID,), jnp.float32, -s_txt, s_txt), 'Wv': jax.random.uniform(ks[6], (TXT_DIM, HID), jnp.float32, -s_txt, s_txt), 'bv': jax.random.uniform(ks[7], (HID,), jnp.float32, -s_txt, s_txt)}
    _L1_xattn_all = _L1_xattn_setup()
    _L1_xattn_in = {k: v for k, v in _L1_xattn_all.items() if k in ('Wq', 'bq', 'Wk', 'bk', 'Wv', 'bv')}
    del _L1_xattn_all

    def _L1_ffn_setup():
        import jax, jax.numpy as jnp
        import numpy as np
        BITS = 8
        LORA_RANK = 16
        LORA_ALPHA = 32
        SCALING = LORA_ALPHA / LORA_RANK

        def fake_quant_weight(w, bits=BITS):
            qmax = 2.0 ** (bits - 1) - 1
            scale = jnp.max(jnp.abs(w)) / qmax
            wq = jnp.clip(jnp.round(w / scale), -qmax - 1, qmax) * scale
            return w + jax.lax.stop_gradient(wq - w)

        def qat_lora_linear(x, W, b, A, B):
            Wq = fake_quant_weight(W)
            base = jnp.einsum('bsi,oi->bso', x, Wq) + b
            lora = jnp.einsum('bsr,or->bso', jnp.einsum('bsi,ri->bsr', x, A), B)
            return base + SCALING * lora
        key = jax.random.key(seed)
        ks = jax.random.split(key, 9)
        d, f = (128, 512)
        s_in = 1.0 / np.sqrt(d)
        s_ff = 1.0 / np.sqrt(f)
        return {'hidden_states': jax.random.normal(ks[0], (4, 256, d), jnp.float32), 'W_fc': jax.random.normal(ks[1], (f, d), jnp.float32) * s_in, 'b_fc': jnp.zeros((f,), jnp.float32), 'A_fc': jax.random.normal(ks[2], (LORA_RANK, d), jnp.float32) * s_in, 'B_fc': jnp.zeros((f, LORA_RANK), jnp.float32), 'W_proj': jax.random.normal(ks[3], (d, f), jnp.float32) * s_ff, 'b_proj': jnp.zeros((d,), jnp.float32), 'A_proj': jax.random.normal(ks[4], (LORA_RANK, f), jnp.float32) * s_ff, 'B_proj': jnp.zeros((d, LORA_RANK), jnp.float32)}
    _L1_ffn_all = _L1_ffn_setup()
    _L1_ffn_in = {k: v for k, v in _L1_ffn_all.items() if k in ('W_fc', 'b_fc', 'A_fc', 'B_fc', 'W_proj', 'b_proj', 'A_proj', 'B_proj')}
    del _L1_ffn_all
    return {'x': x, 'ctx_768': ctx_768, 'g_xattn': g_xattn, 'g_ffn': g_ffn, 'L0_xattn_Wq': _L0_xattn_in['Wq'], 'L0_xattn_Wk': _L0_xattn_in['Wk'], 'L0_xattn_Wv': _L0_xattn_in['Wv'], 'L0_xattn_Wo': _L0_xattn_in['Wo'], 'L0_xattn_bo': _L0_xattn_in['bo'], 'L0_xattn_q_down': _L0_xattn_in['q_down'], 'L0_xattn_q_up': _L0_xattn_in['q_up'], 'L0_xattn_q_alpha': _L0_xattn_in['q_alpha'], 'L0_xattn_k_down': _L0_xattn_in['k_down'], 'L0_xattn_k_up': _L0_xattn_in['k_up'], 'L0_xattn_k_alpha': _L0_xattn_in['k_alpha'], 'L0_xattn_v_down': _L0_xattn_in['v_down'], 'L0_xattn_v_up': _L0_xattn_in['v_up'], 'L0_xattn_v_alpha': _L0_xattn_in['v_alpha'], 'L0_xattn_o_down': _L0_xattn_in['o_down'], 'L0_xattn_o_up': _L0_xattn_in['o_up'], 'L0_xattn_o_alpha': _L0_xattn_in['o_alpha'], 'L0_xattn_Wk_ipa': _L0_xattn_in['Wk_ipa'], 'L0_xattn_Wv_ipa': _L0_xattn_in['Wv_ipa'], 'L0_ffn_router_w': _L0_ffn_in['router_w'], 'L0_ffn_w1': _L0_ffn_in['w1'], 'L0_ffn_b1': _L0_ffn_in['b1'], 'L0_ffn_w2': _L0_ffn_in['w2'], 'L0_ffn_b2': _L0_ffn_in['b2'], 'L1_xattn_Wq': _L1_xattn_in['Wq'], 'L1_xattn_bq': _L1_xattn_in['bq'], 'L1_xattn_Wk': _L1_xattn_in['Wk'], 'L1_xattn_bk': _L1_xattn_in['bk'], 'L1_xattn_Wv': _L1_xattn_in['Wv'], 'L1_xattn_bv': _L1_xattn_in['bv'], 'L1_ffn_W_fc': _L1_ffn_in['W_fc'], 'L1_ffn_b_fc': _L1_ffn_in['b_fc'], 'L1_ffn_A_fc': _L1_ffn_in['A_fc'], 'L1_ffn_B_fc': _L1_ffn_in['B_fc'], 'L1_ffn_W_proj': _L1_ffn_in['W_proj'], 'L1_ffn_b_proj': _L1_ffn_in['b_proj'], 'L1_ffn_A_proj': _L1_ffn_in['A_proj'], 'L1_ffn_B_proj': _L1_ffn_in['B_proj']}

def reference(x, ctx_768, g_xattn, g_ffn, L0_xattn_Wq, L0_xattn_Wk, L0_xattn_Wv, L0_xattn_Wo, L0_xattn_bo, L0_xattn_q_down, L0_xattn_q_up, L0_xattn_q_alpha, L0_xattn_k_down, L0_xattn_k_up, L0_xattn_k_alpha, L0_xattn_v_down, L0_xattn_v_up, L0_xattn_v_alpha, L0_xattn_o_down, L0_xattn_o_up, L0_xattn_o_alpha, L0_xattn_Wk_ipa, L0_xattn_Wv_ipa, L0_ffn_router_w, L0_ffn_w1, L0_ffn_b1, L0_ffn_w2, L0_ffn_b2, L1_xattn_Wq, L1_xattn_bq, L1_xattn_Wk, L1_xattn_bk, L1_xattn_Wv, L1_xattn_bv, L1_ffn_W_fc, L1_ffn_b_fc, L1_ffn_A_fc, L1_ffn_B_fc, L1_ffn_W_proj, L1_ffn_b_proj, L1_ffn_A_proj, L1_ffn_B_proj):
    import jax
    import jax.numpy as jnp

    def _L0_xattn_ref(x, context, Wq, Wk, Wv, Wo, bo, q_down, q_up, q_alpha, k_down, k_up, k_alpha, v_down, v_up, v_alpha, o_down, o_up, o_alpha, Wk_ipa, Wv_ipa):
        import jax, jax.numpy as jnp
        import numpy as np
        HEADS = 16
        DIM_HEAD = 64
        RANK = 32
        LORA_W = 1.0
        IPA_SCALE = 1.0
        IPA_TOKENS = 4
        SCALE = DIM_HEAD ** (-0.5)

        def _split_heads(t):
            b, n, _ = t.shape
            return t.reshape(b, n, HEADS, DIM_HEAD).transpose(0, 2, 1, 3)

        def _merge_heads(t):
            b, h, n, d = t.shape
            return t.transpose(0, 2, 1, 3).reshape(b, n, h * d)

        def _attention(q_in, k_in, v_in):
            q = _split_heads(q_in)
            k = _split_heads(k_in)
            v = _split_heads(v_in)
            s = jnp.einsum('bhid,bhjd->bhij', q, k) * SCALE
            p = jax.nn.softmax(s, axis=-1)
            o = jnp.einsum('bhij,bhjd->bhid', p, v)
            return _merge_heads(o)

        def _lora(t, down, up, alpha):
            return t @ down @ up * (LORA_W * alpha[0] / RANK)
        q_in = x @ Wq + _lora(x, q_down, q_up, q_alpha)
        end = context.shape[1] - IPA_TOKENS
        org_ctx = context[:, :end, :]
        ipa_ctx = context[:, end:, :]
        k_in = org_ctx @ Wk + _lora(org_ctx, k_down, k_up, k_alpha)
        v_in = org_ctx @ Wv + _lora(org_ctx, v_down, v_up, v_alpha)
        out = _attention(q_in, k_in, v_in)
        ipa_k = ipa_ctx @ Wk_ipa
        ipa_v = ipa_ctx @ Wv_ipa
        out_ipa = _attention(q_in, ipa_k, ipa_v)
        out = out + IPA_SCALE * out_ipa
        return out @ Wo + bo + _lora(out, o_down, o_up, o_alpha)

    def _L0_ffn_ref(hidden_states, router_w, w1, b1, w2, b2):
        import jax, jax.numpy as jnp
        import numpy as np
        H = 128
        E = 8
        FFN = 512
        TOP_K = 2
        B, S, _ = hidden_states.shape
        x = hidden_states.reshape(-1, H)
        T = x.shape[0]
        logits = x @ router_w.T
        top_v, top_i = jax.lax.top_k(logits, TOP_K)
        rw = jax.nn.softmax(top_v, axis=-1)
        combine = jnp.zeros((T, E), x.dtype).at[jnp.arange(T)[:, None], top_i].add(rw)
        h = jax.nn.gelu(jnp.einsum('th,efh->etf', x, w1) + b1[:, None, :], approximate=False)
        y = jnp.einsum('etf,ehf->eth', h, w2) + b2[:, None, :]
        out = jnp.einsum('eth,te->th', y, combine)
        return out.reshape(B, S, H)

    def _L1_xattn_ref(image_features, text_features, Wq, bq, Wk, bk, Wv, bv):
        import jax, jax.numpy as jnp
        import numpy as np
        IMG_DIM, TXT_DIM, HID = (128, 96, 128)
        B, LQ, LK = (8, 256, 256)
        query = jnp.einsum('bqi,ih->bqh', image_features, Wq) + bq
        key = jnp.einsum('bkt,th->bkh', text_features, Wk) + bk
        value = jnp.einsum('bkt,th->bkh', text_features, Wv) + bv
        scale = 1.0 / jnp.sqrt(jnp.asarray(HID, query.dtype))
        scores = jnp.einsum('bqh,bkh->bqk', query, key) * scale
        weights = jax.nn.softmax(scores, axis=-1)
        attended = jnp.einsum('bqk,bkh->bqh', weights, value)
        return attended

    def _L1_ffn_ref(hidden_states, W_fc, b_fc, A_fc, B_fc, W_proj, b_proj, A_proj, B_proj):
        import jax, jax.numpy as jnp
        import numpy as np
        BITS = 8
        LORA_RANK = 16
        LORA_ALPHA = 32
        SCALING = LORA_ALPHA / LORA_RANK

        def fake_quant_weight(w, bits=BITS):
            qmax = 2.0 ** (bits - 1) - 1
            scale = jnp.max(jnp.abs(w)) / qmax
            wq = jnp.clip(jnp.round(w / scale), -qmax - 1, qmax) * scale
            return w + jax.lax.stop_gradient(wq - w)

        def qat_lora_linear(x, W, b, A, B):
            Wq = fake_quant_weight(W)
            base = jnp.einsum('bsi,oi->bso', x, Wq) + b
            lora = jnp.einsum('bsr,or->bso', jnp.einsum('bsi,ri->bsr', x, A), B)
            return base + SCALING * lora
        h = qat_lora_linear(hidden_states, W_fc, b_fc, A_fc, B_fc)
        h = jax.nn.gelu(h, approximate=False)
        h = qat_lora_linear(h, W_proj, b_proj, A_proj, B_proj)
        return h
    x = x + jnp.tanh(g_xattn[0]) * _L0_xattn_ref(_layernorm(x, axis=-1), ctx_768, L0_xattn_Wq, L0_xattn_Wk, L0_xattn_Wv, L0_xattn_Wo, L0_xattn_bo, L0_xattn_q_down, L0_xattn_q_up, L0_xattn_q_alpha, L0_xattn_k_down, L0_xattn_k_up, L0_xattn_k_alpha, L0_xattn_v_down, L0_xattn_v_up, L0_xattn_v_alpha, L0_xattn_o_down, L0_xattn_o_up, L0_xattn_o_alpha, L0_xattn_Wk_ipa, L0_xattn_Wv_ipa)
    x = x + jnp.tanh(g_ffn[0]) * _L0_ffn_ref(_layernorm(x, axis=-1), L0_ffn_router_w, L0_ffn_w1, L0_ffn_b1, L0_ffn_w2, L0_ffn_b2)
    x = x + jnp.tanh(g_xattn[1]) * _L1_xattn_ref(_layernorm(x, axis=-1), ctx_768, L1_xattn_Wq, L1_xattn_bq, L1_xattn_Wk, L1_xattn_bk, L1_xattn_Wv, L1_xattn_bv)
    x = x + jnp.tanh(g_ffn[1]) * _L1_ffn_ref(_layernorm(x, axis=-1), L1_ffn_W_fc, L1_ffn_b_fc, L1_ffn_A_fc, L1_ffn_B_fc, L1_ffn_W_proj, L1_ffn_b_proj, L1_ffn_A_proj, L1_ffn_B_proj)
    return x

_drawn_inputs = setup_inputs


def setup_inputs(seed=0):
    import zlib

    import numpy as np

    out = dict(_drawn_inputs(seed))
    spreads = {'g_ffn': (-1.0, 0.2),
     'L0_xattn_bo': (0.0, 0.1),
     'L1_ffn_b_fc': (0.0, 0.1),
     'L1_ffn_B_fc': (0.0, 0.1),
     'L1_ffn_b_proj': (0.0, 0.1),
     'L1_ffn_B_proj': (0.0, 0.1)}
    factors = {'L0_xattn_Wq': 8.0,
     'L0_xattn_Wk': 8.0,
     'L0_xattn_q_down': 8.0,
     'L0_xattn_q_up': 8.0,
     'L0_xattn_k_down': 8.0,
     'L0_xattn_k_up': 8.0,
     'L0_xattn_v_down': 7.088,
     'L0_xattn_v_up': 7.12,
     'L0_xattn_o_down': 4.788,
     'L0_xattn_o_up': 4.647,
     'L0_xattn_Wk_ipa': 8.0,
     'L0_ffn_b1': 5.95,
     'L0_ffn_b2': 4.179,
     'L1_xattn_bq': 34.787,
     'L1_xattn_bk': 64.0,
     'L1_xattn_Wq': 2.889}
    for name, (base, spread) in spreads.items():
        noise = np.random.default_rng([zlib.crc32(name.encode()), seed]).standard_normal(out[name].shape)
        drawn = base * np.exp(spread * noise) if base else spread * noise
        out[name] = jnp.asarray(drawn.astype(out[name].dtype))
    for name, factor in factors.items():
        out[name] = (out[name] * factor).astype(out[name].dtype)
    return out
```

```python
from contextlib import ExitStack

import concourse.bass as bass
from concourse import mybir

F32 = mybir.dt.float32
F32R = mybir.dt.float32r
ALU = mybir.AluOpType
ACT = mybir.ActivationFunctionType
AX = mybir.AxisListType

P = 128
BATCH, TOK, DIM = 32, 128, 128
CTX, CDIM = 120, 96
HEADS, DHEAD = 16, 64
INNER = HEADS * DHEAD
RANK = 32
IPA = 4
ORG = CTX - IPA
GB = 4
GROUPS = BATCH // GB
GTOK = GB * TOK
QH = 4
QUADS = HEADS // QH
UNITS = QUADS * GB
QCOLS = QH * CTX
CHUNKS = INNER // P
EPS = 1e-5
SCALE = DHEAD ** -0.5


class Taken:

    def __init__(self, eng):
        self.eng, self.count = eng, {}

    def next(self, sem, n=1):
        self.count[sem.name] = (sem, self.count.get(sem.name, (sem, 0))[1] + n)
        return self.count[sem.name][1]

    def give_back(self):
        for sem, n in self.count.values():
            self.eng.sem_inc(sem, -n)
        self.count = {}


def bcast(ap, n):
    return ap.unsqueeze(2).to_broadcast([ap.shape[0], ap.shape[1], n])


def item(step, ahead, last, count=UNITS):
    i = step + ahead
    if i < 0 or (last and i >= count):
        return None
    return i // count, i % count


def head_attention(nc, d, x, w1_raw, w2_raw, raw_in):
    with ExitStack() as ctx:
        def sb(name, shape, dt=F32):
            return ctx.enter_context(nc.sbuf_tensor(name, shape, dt))

        def sem(name):
            return ctx.enter_context(nc.semaphore(name))

        ident = sb("ident", [P, P])
        ctx_hi, ctx_lo = (sb(n, [CDIM, BATCH, CTX], F32R) for n in ("ctx_hi", "ctx_lo"))
        a_hi, a_lo, b_hi, b_lo = (sb(n, [CDIM, HEADS * P], F32R) for n in ("a_hi", "a_lo", "b_hi", "b_lo"))
        kipa_hi, kipa_lo = (sb(n, [P, HEADS, BATCH, IPA], F32R) for n in ("kipa_hi", "kipa_lo"))
        bias_hi, bias_lo = (sb(n, [1, GB, DIM], F32R) for n in ("bias_hi", "bias_lo"))
        ones = sb("ones", [1, P], F32R)
        vipa_dram = nc.dram_tensor("vipa_scratch", [BATCH * IPA, HEADS * DIM], F32, kind="Internal").ap()

        with ExitStack() as ws:
            def st(name, shape, dt=F32):
                return ws.enter_context(nc.sbuf_tensor(name, shape, dt))

            def ps(name):
                return ws.enter_context(nc.psum_tensor(name, [P, 512], F32))

            wqT = st("wqT", [P, CHUNKS, DIM])
            wkT, wvT, wkiT, wviT = (st(n, [P, CHUNKS, CDIM]) for n in ("wkT", "wvT", "wkiT", "wviT"))
            wo = st("wo", [P, CHUNKS, DIM])
            q_up, k_up, v_up, o_downT = (st(n, [RANK, INNER]) for n in ("q_up", "k_up", "v_up", "o_downT"))
            q_downT = st("q_downT", [RANK, DIM])
            k_downT, v_downT = (st(n, [RANK, CDIM]) for n in ("k_downT", "v_downT"))
            o_up = st("o_up", [RANK, DIM])
            scal = st("scal", [P, 5])
            lora = st("lora", [P, 4])
            gate = st("gate", [P, 1])
            bo = st("bo", [1, DIM])
            bog = st("bog", [1, DIM])
            a_ipa, b_ipa = (st(n, [CDIM, HEADS * P]) for n in ("a_ipa", "b_ipa"))
            stage = st("stage", [P, BATCH * CTX])
            ctx_raw = stage[0:CDIM, :].rearrange("c (b t) -> c b t", b=BATCH)
            ctx_ipa = st("ctx_ipa", [CDIM, BATCH, IPA])
            vipa = stage[:, 0:HEADS * DIM]
            banks = [ps(f"setup{i}") for i in range(8)]

            loaded = ws.enter_context(nc.semaphore("weights_loaded"))
            xin = ws.enter_context(nc.semaphore("x_loaded"))
            cin = ws.enter_context(nc.semaphore("ctx_loaded"))
            ident0 = ws.enter_context(nc.semaphore("ident_zeroed"))
            ready = ws.enter_context(nc.semaphore("scalars_ready"))
            gated = ws.enter_context(nc.semaphore("gate_ready"))
            split = ws.enter_context(nc.semaphore("ctx_high_part"))
            gathered = ws.enter_context(nc.semaphore("ctx_ipa_gathered"))
            chunk_mm = ws.enter_context(nc.semaphore("chunk_products"))
            chunk_ok = ws.enter_context(nc.semaphore("chunks_added"))
            fold_mm = ws.enter_context(nc.semaphore("fold_products"))
            fold_hi = ws.enter_context(nc.semaphore("fold_high_parts"))
            fold_lo = ws.enter_context(nc.semaphore("fold_low_parts"))
            fold_f32 = ws.enter_context(nc.semaphore("folds_whole"))
            ipa_mm = ws.enter_context(nc.semaphore("ipa_products"))
            ipa_hi = ws.enter_context(nc.semaphore("ipa_high_parts"))
            ipa_ok = ws.enter_context(nc.semaphore("ipa_stored"))
            vipa_mm = ws.enter_context(nc.semaphore("vipa_products"))
            vipa_ok = ws.enter_context(nc.semaphore("vipa_ready"))
            spilled = ws.enter_context(nc.semaphore("vipa_spilled"))
            boh = ws.enter_context(nc.semaphore("bias_steps"))

            loads = [
                (q_up[:, :], d["q_up"]), (q_downT[:, :], d["q_downT"]), (k_up[:, :], d["k_up"]),
                (k_downT[:, :], d["k_downT"]), (v_up[:, :], d["v_up"]), (v_downT[:, :], d["v_downT"]),
                (o_downT[:, :], d["o_downT"]), (o_up[:, :], d["o_up"]),
                (wqT[:, :, :], d["wqT"].rearrange("(c p) d -> p c d", p=P)),
                (wkT[:, :, :], d["wkT"].rearrange("(c p) d -> p c d", p=P)),
                (wo[:, :, :], d["wo"].rearrange("(c p) d -> p c d", p=P)),
                (wvT[:, :, :], d["wvT"].rearrange("(c p) d -> p c d", p=P)),
                (wkiT[:, :, :], d["wkiT"].rearrange("(c p) d -> p c d", p=P)),
                (wviT[:, :, :], d["wviT"].rearrange("(c p) d -> p c d", p=P)),
                (bo[:, :], d["bo"].rearrange("(a n) -> a n", a=1)),
            ]
            scalars = [d["q_alpha"], d["k_alpha"], d["v_alpha"], d["o_alpha"], d["g_xattn"][0:1]]
            N_LOADS = 16 * (len(loads) + len(scalars))
            LORAS = [(wqT, q_up, q_downT, DIM), (wkT, k_up, k_downT, CDIM),
                     (wo, o_downT, o_up, DIM), (wvT, v_up, v_downT, CDIM)]
            LORA_SCALAR = [0, 1, 3, 2]
            FOLDS = [(wkT, wqT, a_hi, a_lo), (wvT, wo, b_hi, b_lo), (wkiT, wqT, a_ipa, None), (wviT, wo, b_ipa, None)]
            FBANKS = HEADS // 4

            with nc.Block() as block:
                @block.sync
                def _(sp):
                    for out, in_ in loads:
                        sp.dma_start(out, in_).then_inc(loaded, 16)
                    for i, s in enumerate(scalars):
                        sp.dma_start(scal[:, i:i + 1], s.partition_broadcast(P)).then_inc(loaded, 16)
                    for i in range(4):
                        sp.wait_ge(vipa_ok, i + 1)
                        sp.dma_start(vipa_dram[:, i * 512:i * 512 + 512],
                                     vipa[:, i * 512:i * 512 + 512]).then_inc(spilled, 16)
                    sp.wait_ge(spilled, 64)
                    sp.wait_ge(xin, 16)

                @block.scalar
                def _(act):
                    act.dma_start(ctx_raw[:, :, :], d["ctxT"].rearrange("c (b t) -> c b t", b=BATCH)).then_inc(cin, 16)
                    act.dma_start(x[:, :, :], d["x"].rearrange("b t d -> t b d")).then_inc(xin, 16)
                    act.wait_ge(loaded, N_LOADS)
                    nc.scalar.activation(gate[:, :], scal[:, 4:5], ACT.Tanh).then_inc(gated, 1)
                    act.wait_ge(cin, 16)
                    nc.scalar.activation(ctx_hi[:, :, :], ctx_raw[:, :, :], ACT.Copy).then_inc(split, 1)
                    n = 0
                    for f, (_, _, hi, lo) in enumerate(FOLDS):
                        scale = SCALE if f in (0, 2) else 1.0
                        for k in range(FBANKS):
                            act.wait_ge(fold_mm, n + 1)
                            nc.scalar.activation(fold_view(hi, k), banks[n % 8][0:CDIM, :].rearrange("c (h d) -> c h d", h=4),
                                                 ACT.Copy, scale=scale).then_inc(fold_hi if lo is not None else fold_f32, 1)
                            n += 1
                    for i in range(4):
                        act.wait_ge(ipa_mm, i + 1)
                        nc.scalar.activation(kipa_hi[:, 4 * i:4 * i + 4, :, :].rearrange("p h b t -> p (h b t)"),
                                             banks[i][:, :], ACT.Copy).then_inc(ipa_hi, 1)
                    for i in range(4):
                        act.wait_ge(vipa_mm, i + 1)
                        nc.scalar.activation(vipa[:, i * 512:i * 512 + 512], banks[4 + i][:, :],
                                             ACT.Copy).then_inc(vipa_ok, 1)

                @block.gpsimd
                def _(pool):
                    nc.gpsimd.memset(ident[:, :], 0.0).then_inc(ident0, 1)
                    pool.wait_ge(ident0, 1)
                    nc.gpsimd.affine_select(out=ident[:, :], in_=ident[:, :], compare_op=ALU.not_equal, fill=1.0,
                                            base=0, pattern=[[-1, P]], channel_multiplier=1)

                @block.tensor
                def _(pe):
                    pe.wait_ge(loaded, N_LOADS)
                    n = 0
                    for w, left, right, cols in LORAS:
                        for k in range(2):
                            for c in range(4):
                                mm = nc.tensor.matmul(banks[n][:, c * cols:(c + 1) * cols],
                                                      left[:, (4 * k + c) * P:(4 * k + c + 1) * P], right[:, :],
                                                      start=True, stop=True)
                            mm.then_inc(chunk_mm, 1)
                            n += 1
                    n = 0
                    for f, (left, right, hi, lo) in enumerate(FOLDS):
                        pe.wait_ge(chunk_ok, 4 if f % 2 == 0 else 8)
                        for k in range(FBANKS):
                            if n >= 8:
                                pe.wait_ge(fold_lo, n - 7)
                            half, first = k % 2, 4 * (k // 2)
                            for c in range(4):
                                mm = nc.tensor.matmul(banks[n % 8][0:CDIM, c * P:(c + 1) * P],
                                                      left[64 * half:64 * half + 64, first + c, :],
                                                      right[64 * half:64 * half + 64, first + c, :],
                                                      start=True, stop=True)
                            mm.then_inc(fold_mm, 1)
                            n += 1
                    pe.wait_ge(fold_f32, 8)
                    pe.wait_ge(gathered, 1)
                    for i in range(4):
                        for h in range(4):
                            mm = nc.tensor.matmul(banks[i][:, h * P:(h + 1) * P],
                                                  a_ipa[:, (4 * i + h) * P:(4 * i + h + 1) * P],
                                                  ctx_ipa[:, :, :].rearrange("c b t -> c (b t)"), start=True, stop=True)
                        mm.then_inc(ipa_mm, 1)
                    for i in range(4):
                        nc.tensor.matmul(banks[4 + i][:, :], ctx_ipa[:, :, :].rearrange("c b t -> c (b t)"),
                                         b_ipa[:, i * 512:(i + 1) * 512], start=True, stop=True).then_inc(vipa_mm, 1)

                @block.vector
                def _(dve):
                    dve.wait_ge(loaded, N_LOADS)
                    nc.vector.tensor_scalar(lora[:, :], scal[:, 0:4], 1.0 / RANK, None, ALU.mult).then_inc(ready, 1)
                    dve.wait_ge(ready, 1)
                    dve.wait_ge(gated, 1)
                    n = 0
                    for (w, _, _, cols), s in zip(LORAS, LORA_SCALAR):
                        for k in range(2):
                            dve.wait_ge(chunk_mm, n + 1)
                            part = w[:, 4 * k:4 * k + 4, :]
                            op = nc.vector.scalar_tensor_tensor(
                                out=part, in0=banks[n][:, 0:4 * cols].rearrange("p (c d) -> p c d", c=4),
                                scalar=lora[:, s:s + 1], in1=part, op0=ALU.mult, op1=ALU.add)
                            if w is wo:
                                op.then_inc(ready, 1)
                            else:
                                op.then_inc(chunk_ok, 1)
                            n += 1
                    dve.wait_ge(ready, 3)
                    nc.vector.tensor_scalar(wo[:, :, :], wo[:, :, :], gate[:, 0:1], None, ALU.mult).then_inc(chunk_ok, 2)
                    dve.wait_ge(cin, 16)
                    dve.wait_ge(split, 1)
                    nc.vector.tensor_tensor(ctx_lo[:, :, :], ctx_raw[:, :, :], ctx_hi[:, :, :], ALU.subtract)
                    nc.vector.tensor_copy(ctx_ipa[:, :, :], ctx_raw[:, :, ORG:CTX]).then_inc(gathered, 1)
                    n = 0
                    for f, (_, _, hi, lo) in enumerate(FOLDS):
                        if lo is None:
                            continue
                        scale = SCALE if f == 0 else 1.0
                        for k in range(FBANKS):
                            dve.wait_ge(fold_hi, n + 1)
                            nc.vector.scalar_tensor_tensor(
                                out=fold_view(lo, k), in0=banks[n][0:CDIM, :].rearrange("c (h d) -> c h d", h=4),
                                scalar=scale, in1=fold_view(hi, k), op0=ALU.mult, op1=ALU.subtract).then_inc(fold_lo, 1)
                            n += 1
                    for i in range(4):
                        dve.wait_ge(ipa_hi, i + 1)
                        out = kipa_lo[:, 4 * i:4 * i + 4, :, :].rearrange("p h b t -> p (h b t)")
                        hi = kipa_hi[:, 4 * i:4 * i + 4, :, :].rearrange("p h b t -> p (h b t)")
                        nc.vector.tensor_tensor(out, banks[i][:, :], hi, ALU.subtract).then_inc(ipa_ok, 1)
                    nc.vector.tensor_scalar(bog[:, :], bo[:, :], gate[0:1, 0:1], None, ALU.mult).then_inc(boh, 1)
                    nc.vector.memset(ones[:, :].bitcast(F32), 1.0)
                    dve.wait_ge(boh, 1)
                    for b in range(GB):
                        op = nc.vector.tensor_copy(bias_hi[:, b, :], bog[:, :])
                    op.then_inc(boh, 1)
                    dve.wait_ge(boh, 2)
                    for b in range(GB):
                        nc.vector.tensor_tensor(bias_lo[:, b, :], bog[:, :], bias_hi[:, b, :], ALU.subtract)

        def pb(name, shape=(P, 512)):
            return ctx.enter_context(nc.psum_tensor(name, list(shape), F32))

        ctxg_hi, ctxg_lo = (sb(n, [CDIM, GB, CTX], F32R) for n in ("ctxg_hi", "ctxg_lo"))
        xn = sb("xn", [P, GB, DIM])
        xn_hi, xn_lo = (sb(n, [P, GTOK], F32R) for n in ("xnT_hi", "xnT_lo"))
        stats = sb("stats", [P, GB, 6])
        mv = sb("mean_var", [P, GB, 2])
        veps = sb("var_eps", [P, GB])
        rstd = sb("rstd", [P, GB])
        neg_half = sb("neg_half", [P, GB])
        keys_hi = [sb(f"keys_hi{i}", [P, GB, QH, CTX], F32R) for i in range(2)]
        keys_lo = [sb(f"keys_lo{i}", [P, GB, QH, CTX], F32R) for i in range(2)]
        vals = [sb(f"vals{i}", [CTX, QH * DIM]) for i in range(2)]
        shifted = [sb(f"shifted{i}", [P, QH, CTX]) for i in range(2)]
        expd = [sb(f"expd{i}", [P, QH, CTX]) for i in range(2)]
        prob = [sb(f"prob{i}", [P, QH, CTX]) for i in range(2)]
        probT = sb("probT", [CTX, QH * TOK])
        top = sb("top", [P, 2, 2, QH])
        total = sb("total", [P, 2, 2, QH])
        inv = sb("inv", [P, 2, 2, QH])

        score_ps = [pb(f"score_ps{i}") for i in range(2)]
        key_ps, val_ps, probT_ps, xnT_ps, acc = (pb(n) for n in ("key_ps", "val_ps", "probT_ps", "xnT_ps", "acc"))

        norm_ready = sem("norm_ready")
        probT_ready = sem("probT_ready")
        vals_ready = sem("vals_ready")
        keys_lo_ready = sem("keys_lo_ready")
        xn_ready = sem("xn_ready")
        xnT_ready = sem("xnT_ready")
        ctxg_ready = sem("ctxg_ready")
        vipa_in = [sem(f"vipa_in{i}") for i in range(2)]
        acc_free = sem("acc_free")
        probT_mm, vals_mm, keys_mm, xnT_mm = (sem(n) for n in ("probT_mm", "vals_mm", "keys_mm", "xnT_mm"))
        shift_ready = sem("shift_ready")
        score_mm, acc_mm = sem("score_mm"), sem("acc_mm")
        keys_hi_ready, exp_ready, xn_hi_ready = (sem(n) for n in ("keys_hi_ready", "exp_ready", "xn_hi_ready"))
        rstd_ready = sem("rstd_ready")
        d_max, d_sum, d_stat = (sem(n) for n in ("d_max", "d_sum", "d_stat"))
        inv_ready, var_ready = sem("inv_ready"), sem("var_ready")
        p_var, p_half = sem("p_var"), sem("p_half")
        vals_slot = sem("vals_slot")

        def segs(t):
            return [(t[:, :, 0:ORG], ORG, 0), (t[:, :, ORG:CTX], IPA, 1)]

        with nc.Block() as block:
            @block.tensor
            def _(pe):
                taken = Taken(pe)

                def transpose_x():
                    pe.wait_ge(xn_ready, taken.next(xn_ready))
                    for b in range(GB):
                        mm = nc.tensor.transpose(xnT_ps[:, b * TOK:(b + 1) * TOK], xn[:, b, :], ident[:, :])
                    mm.then_inc(xnT_mm, 1)

                def three(out, a, b, hi, lo):
                    nc.tensor.matmul(out, a[0], b[0], start=True, stop=False)
                    nc.tensor.matmul(out, a[0], b[1], start=False, stop=False)
                    return nc.tensor.matmul(out, a[1], b[0], start=False, stop=True)

                def step(s, g, last):
                    if s >= 0:
                        pe.wait_ge(norm_ready, taken.next(norm_ready))
                        for h in range(QH):
                            mm = nc.tensor.transpose(probT_ps[0:CTX, h * TOK:(h + 1) * TOK], prob[s % 2][:, h, :], ident[:, :])
                            if h == 0:
                                mm.then_inc(vals_slot, 1)
                        mm.then_inc(probT_mm, 1)
                    if it := item(s, 2, last):
                        _, u = it
                        q, b = divmod(u, GB)
                        if u == 0:
                            pe.wait_ge(xnT_ready, taken.next(xnT_ready))
                        rhs = [t[q % 2][:, b, :, :].rearrange("p h k -> p (h k)") for t in (keys_hi, keys_lo)]
                        three(score_ps[u % 2][:, 0:QCOLS], [t[:, b * TOK:(b + 1) * TOK] for t in (xn_hi, xn_lo)], rhs,
                              None, None).then_inc(score_mm, 1)
                    if s >= 0:
                        pe.wait_ge(vals_ready, taken.next(vals_ready))
                    if it := item(s, 1, last):
                        dg, u = it
                        q, b = divmod(u, GB)
                        if u == 0:
                            pe.wait_ge(ctxg_ready, taken.next(ctxg_ready))
                        three(val_ps[0:CTX, :], [t[:, b, :] for t in (ctxg_hi, ctxg_lo)],
                              [t[:, q * QH * DIM:(q + 1) * QH * DIM] for t in (b_hi, b_lo)], None, None).then_inc(vals_mm, 1)
                    if item(s, 6, last) is not None and s > -7 + 0:
                        pe.wait_ge(keys_lo_ready, taken.next(keys_lo_ready))
                    if it := item(s, 7, last):
                        dg, h = it
                        grp = bass.ds(g * GB + dg * GB, GB) if not isinstance(g, int) else slice((g + dg) * GB, (g + dg + 1) * GB)
                        three(key_ps[:, 0:GB * ORG].rearrange("p (b k) -> p b k", b=GB),
                              [t[:, h * P:(h + 1) * P] for t in (a_hi, a_lo)],
                              [t[:, grp, 0:ORG] for t in (ctx_hi, ctx_lo)], None, None).then_inc(keys_mm, 1)
                    if s >= 0:
                        q, b = divmod(s, GB)
                        if s == 0:
                            pe.wait_ge(acc_free, taken.next(acc_free))
                            for n, part in enumerate((bias_hi, bias_lo)):
                                nc.tensor.matmul(acc[:, :], ones[:, :], part[:, :, :].rearrange("p b d -> p (b d)"),
                                                 start=(n == 0), stop=False, skip_group_check=True)
                        pe.wait_ge(probT_ready, taken.next(probT_ready))
                        pe.wait_ge(vipa_in[s % 2], taken.next(vipa_in[s % 2], 16))
                        for h in range(QH):
                            mm = nc.tensor.matmul(acc[:, b * DIM:(b + 1) * DIM], probT[:, h * TOK:(h + 1) * TOK],
                                                  vals[s % 2][:, h * DIM:(h + 1) * DIM],
                                                  start=False, stop=(q == QUADS - 1 and h == QH - 1), skip_group_check=True)
                        if s == UNITS - 1:
                            mm.then_inc(acc_mm, 1)
                        if s == 9 and not last:
                            transpose_x()

                transpose_x()
                for s in range(-7, 0):
                    step(s, 0, False)
                taken.give_back()
                with pe.Fori(0, GROUPS - 1) as g:
                    for s in range(UNITS):
                        step(s, g, False)
                    taken.give_back()
                for s in range(UNITS):
                    step(s, GROUPS - 1, True)

            @block.scalar
            def _(act):
                taken = Taken(act)

                def copy_ctx(grp):
                    nc.scalar.activation(ctxg_hi[:, :, :], ctx_hi[:, grp, :], ACT.Copy)
                    nc.scalar.activation(ctxg_lo[:, :, :], ctx_lo[:, grp, :], ACT.Copy).then_inc(ctxg_ready, 1)

                def split_x():
                    act.wait_ge(xnT_mm, taken.next(xnT_mm))
                    nc.scalar.activation(xn_hi[:, :], xnT_ps[:, :], ACT.Copy).then_inc(xn_hi_ready, 1)

                def step(s, g, last):
                    if s >= 0:
                        act.wait_ge(probT_mm, taken.next(probT_mm))
                        nc.scalar.activation(probT[:, :], probT_ps[0:CTX, :], ACT.Copy).then_inc(probT_ready, 1)
                    if it := item(s, 1, last):
                        _, u = it
                        act.wait_ge(vals_mm, taken.next(vals_mm))
                        nc.scalar.activation(vals[u % 2][0:ORG, :], val_ps[0:ORG, :], ACT.Copy).then_inc(vals_ready, 1)
                    if s == 13 and not last:
                        split_x()
                    if s == 14 and not last:
                        copy_ctx(bass.ds(g * GB + GB, GB))
                    if it := item(s, 7, last):
                        _, k = it
                        q, h = divmod(k, QH)
                        act.wait_ge(keys_mm, taken.next(keys_mm))
                        nc.scalar.activation(keys_hi[q % 2][:, :, h, 0:ORG],
                                             key_ps[:, 0:GB * ORG].rearrange("p (b k) -> p b k", b=GB),
                                             ACT.Copy).then_inc(keys_hi_ready, 1)
                    if it := item(s, 2, last):
                        _, u = it
                        act.wait_ge(shift_ready, taken.next(shift_ready))
                        nc.scalar.activation(expd[u % 2][:, :, :], shifted[u % 2][:, :, :], ACT.Exp).then_inc(exp_ready, 1)

                act.dma_start(w1_raw[:, :, :], d["w1T"].rearrange("e h f -> h e f")).then_inc(raw_in, 16)
                act.dma_start(w2_raw[:, :, :, :], d["w2T"].rearrange("e (c p) h -> p e c h", p=P)).then_inc(raw_in, 16)
                copy_ctx(slice(0, GB))
                split_x()
                for s in range(-7, 0):
                    step(s, 0, False)
                taken.give_back()
                with act.Fori(0, GROUPS - 1) as g:
                    for s in range(UNITS):
                        step(s, g, False)
                    taken.give_back()
                for s in range(UNITS):
                    step(s, GROUPS - 1, True)

            @block.vector
            def _(dve):
                taken = Taken(dve)

                def stat(b, xb, last_one):
                    op = nc.vector.bn_stats(stats[:, b, :], xb)
                    if last_one:
                        op.then_inc(d_stat, 1)

                def aggregate():
                    dve.wait_ge(d_stat, taken.next(d_stat))
                    for b in range(GB):
                        op = nc.vector.bn_aggr(mv[:, b, :], stats[:, b, :])
                    op.then_inc(var_ready, 1)

                def normalise(xg):
                    dve.wait_ge(rstd_ready, taken.next(rstd_ready))
                    for b in range(GB):
                        op = nc.vector.tensor_scalar(xn[:, b, :], xg(b), mv[:, b, 0:1], rstd[:, b:b + 1],
                                                     ALU.subtract, ALU.mult)
                    op.then_inc(xn_ready, 1)

                def split_x():
                    dve.wait_ge(xn_hi_ready, taken.next(xn_hi_ready))
                    nc.vector.tensor_tensor(xn_lo[:, :], xnT_ps[:, :], xn_hi[:, :], ALU.subtract).then_inc(xnT_ready, 1)

                def step(s, g, last):
                    if it := item(s, 1, last):
                        _, u = it
                        dve.wait_ge(exp_ready, taken.next(exp_ready))
                        for part, _, seg in segs(expd[u % 2]):
                            op = nc.vector.tensor_reduce(total[:, u % 2, seg, :], part, AX.X, ALU.add)
                        op.then_inc(d_sum, 1)
                        dve.wait_ge(d_sum, taken.next(d_sum))
                        nc.vector.reciprocal(inv[:, u % 2, :, :], total[:, u % 2, :, :]).then_inc(inv_ready, 1)
                    if it := item(s, 2, last):
                        _, u = it
                        score = score_ps[u % 2][:, 0:QCOLS].rearrange("p (h k) -> p h k", h=QH)
                        dve.wait_ge(score_mm, taken.next(score_mm))
                        for part, _, seg in segs(score):
                            op = nc.vector.tensor_reduce(top[:, u % 2, seg, :], part, AX.X, ALU.max)
                        op.then_inc(d_max, 1)
                        dve.wait_ge(d_max, taken.next(d_max))
                        for (part, n, seg), (out, _, _) in zip(segs(score), segs(shifted[u % 2])):
                            op = nc.vector.tensor_tensor(out, part, bcast(top[:, u % 2, seg, :], n), ALU.subtract)
                        op.then_inc(shift_ready, 1)
                    if s == 13 and not last:
                        split_x()
                    if it := item(s, 7, last):
                        _, k = it
                        q, h = divmod(k, QH)
                        dve.wait_ge(keys_hi_ready, taken.next(keys_hi_ready))
                        nc.vector.tensor_tensor(keys_lo[q % 2][:, :, h, 0:ORG],
                                                key_ps[:, 0:GB * ORG].rearrange("p (b k) -> p b k", b=GB),
                                                keys_hi[q % 2][:, :, h, 0:ORG], ALU.subtract).then_inc(keys_lo_ready, 1)
                    if s >= 0 and not last:
                        if s < GB:
                            stat(s, x[:, bass.ds(g * GB + GB + s, 1), :].rearrange("p a d -> p (a d)"), s == GB - 1)
                        if s == GB:
                            aggregate()
                        if s == 7:
                            normalise(lambda b: x[:, bass.ds(g * GB + GB + b, 1), :].rearrange("p a d -> p (a d)"))
                    if s == UNITS - 1:
                        xg = x[:, bass.ds(g * GB, GB), :] if not isinstance(g, int) else x[:, g * GB:(g + 1) * GB, :]
                        dve.wait_ge(acc_mm, taken.next(acc_mm))
                        nc.vector.tensor_tensor(xg, acc[:, :].rearrange("p (b d) -> p b d", b=GB), xg, ALU.add)\
                          .then_inc(acc_free, 1)

                dve.sem_inc(acc_free, 1)
                for b in range(GB):
                    stat(b, x[:, b, :], b == GB - 1)
                aggregate()
                normalise(lambda b: x[:, b, :])
                split_x()
                for s in range(-7, 0):
                    step(s, 0, False)
                taken.give_back()
                with dve.Fori(0, GROUPS - 1) as g:
                    for s in range(UNITS):
                        step(s, g, False)
                    taken.give_back()
                for s in range(UNITS):
                    step(s, GROUPS - 1, True)

            @block.gpsimd
            def _(pool):
                taken = Taken(pool)

                def ipa_keys(q, grp):
                    for slot, src in ((keys_hi, kipa_hi), (keys_lo, kipa_lo)):
                        op = nc.gpsimd.tensor_copy(slot[q % 2][:, :, :, ORG:CTX].rearrange("p b h t -> p h b t"),
                                                   src[:, q * QH:(q + 1) * QH, grp, :])
                    return op

                def rstd_of_group():
                    pool.wait_ge(var_ready, taken.next(var_ready))
                    nc.gpsimd.tensor_scalar(veps[:, :], mv[:, :, 1], EPS, None, ALU.add).then_inc(p_var, 1)
                    pool.wait_ge(p_var, taken.next(p_var))
                    nc.gpsimd.tensor_tensor(rstd[:, :], veps[:, :], neg_half[:, :], ALU.pow).then_inc(rstd_ready, 1)

                def step(s, g, last):
                    if it := item(s, 1, last):
                        _, u = it
                        pool.wait_ge(inv_ready, taken.next(inv_ready))
                        for (part, n, seg), (out, _, _) in zip(segs(expd[u % 2]), segs(prob[u % 2])):
                            op = nc.gpsimd.tensor_tensor(out, part, bcast(inv[:, u % 2, seg, :], n), ALU.mult)
                        op.then_inc(norm_ready, 1)
                    if s >= 0 and (s + 1) % GB == GB - 1 and item(s, 6, last):
                        dg, u = item(s, 6, last)
                        q = u // GB
                        ipa_keys(q, bass.ds(g * GB + dg * GB, GB) if not isinstance(g, int) else
                                 slice((g + dg) * GB, (g + dg + 1) * GB))
                    if s == 5 and not last:
                        rstd_of_group()

                nc.gpsimd.memset(neg_half[:, :], -0.5).then_inc(p_half, 1)
                pool.wait_ge(p_half, 1)
                ipa_keys(0, slice(0, GB))
                ipa_keys(1, slice(0, GB))
                rstd_of_group()
                for s in range(-7, 0):
                    step(s, 0, False)
                taken.give_back()
                with pool.Fori(0, GROUPS - 1) as g:
                    for s in range(UNITS):
                        step(s, g, False)
                    taken.give_back()
                for s in range(UNITS):
                    step(s, GROUPS - 1, True)

            @block.sync
            def _(sp):
                taken = Taken(sp)

                def fetch(u, row):
                    q = u // GB
                    sp.dma_start(vals[u % 2][ORG:CTX, :], vipa_dram[row, q * QH * DIM:(q + 1) * QH * DIM])\
                      .then_inc(vipa_in[u % 2], 16)

                def step(s, g, last):
                    sp.wait_ge(vals_slot, taken.next(vals_slot))
                    if it := item(s, 1, last):
                        dg, u = it
                        b = u % GB
                        start = (g * GB + dg * GB + b) * IPA
                        fetch(u, slice(start, start + IPA) if isinstance(g, int) else bass.ds(start, IPA))

                fetch(0, slice(0, IPA))
                with sp.Fori(0, GROUPS - 1) as g:
                    for s in range(UNITS):
                        step(s, g, False)
                    taken.give_back()
                for s in range(UNITS):
                    step(s, GROUPS - 1, True)


def fold_view(t, k):
    return t[:, :].rearrange("c (i two d) -> c two i d", two=2, d=P)[:, k % 2, 4 * (k // 2):4 * (k // 2) + 4, :]



EXPERTS, FFN = 8, 512
FCH = FFN // P
LORA_R = 16
LORA_SCALING = 2.0
QMAX = 127.0
ROUND = 1.5 * 2.0 ** 23
ISCALE = DIM ** -0.5
MLP = 7
PARTS = EXPERTS + 1
SLOTS = PARTS * FCH


def expert_of(part):
    return EXPERTS - 1 if part == EXPERTS else part


def rest(nc, d, x, w1_raw, w2_raw, raw_in, out):
    with ExitStack() as ctx:
        def sb(name, shape, dt=F32):
            return ctx.enter_context(nc.sbuf_tensor(name, shape, dt))

        def sem(name):
            return ctx.enter_context(nc.semaphore(name))

        ident = sb("ident2", [P, P])
        w1_hi, w1_lo = (sb(n, [P, EXPERTS, FFN], F32R) for n in ("w1_hi", "w1_lo"))
        w2_hi, w2_lo = (sb(n, [P, EXPERTS, FCH, DIM], F32R) for n in ("w2_hi", "w2_lo"))
        fc_hi, fc_lo = (sb(n, [P, FFN], F32R) for n in ("fc_hi", "fc_lo"))
        pj_hi, pj_lo = (sb(n, [P, FCH, DIM], F32R) for n in ("pj_hi", "pj_lo"))
        q_hi, q_lo = (sb(n, [DIM, DIM], F32R) for n in ("wq1_hi", "wq1_lo"))
        wk, wv = (sb(n, [CDIM, DIM]) for n in ("wk1", "wv1"))
        b1 = sb("b1", [P, EXPERTS, FCH])
        b_fc = sb("b_fc", [P, FCH])
        bq, bk, b_pj = (sb(n, [P, 1]) for n in ("bq", "bk", "b_pj"))
        b2 = sb("b2", [EXPERTS, DIM])
        routerT = sb("routerT", [DIM, EXPERTS])
        gates = sb("gates", [P, 4])
        neg_gate = sb("neg_gate", [P, 1])
        bv_hi, bv_lo = (sb(n, [1, GB, DIM], F32R) for n in ("bv_hi", "bv_lo"))
        ones = sb("ones1", [1, P], F32R)
        neg_half = sb("neg_half1", [P, GB])
        iota = sb("iota8", [P, EXPERTS])
        comb_dram = nc.dram_tensor("comb_scratch", [GROUPS, EXPERTS, GTOK], F32, kind="Internal").ap()

        with ExitStack() as ws:
            def st(name, shape, dt=F32):
                return ws.enter_context(nc.sbuf_tensor(name, shape, dt))

            def wsem(name):
                return ws.enter_context(nc.semaphore(name))

            quant = st("quant", [P, 2, FFN])
            work = st("work", [P, 2, FFN])
            most = st("most", [P, 2])
            most_all = st("most_all", [P, 2])
            qscale = st("qscale", [P, 2])
            qinv = st("qinv", [P, 2])
            a_fc, bT_fc = st("a_fc", [LORA_R, DIM]), st("bT_fc", [LORA_R, FFN])
            a_pj, bT_pj = st("a_pj", [LORA_R, FFN]), st("bT_pj", [LORA_R, DIM])
            wq = st("wq1", [DIM, DIM])
            bv = st("bv", [1, DIM])
            bvg = st("bvg", [1, DIM])
            scal = st("scal1", [P, 3])
            lora_ps = [ws.enter_context(nc.psum_tensor(f"lora_ps{i}", [P, FFN], F32)) for i in range(2)]
            small_in, tanh_ok, quant_in = wsem("small_in"), wsem("tanh_ok"), wsem("quant_in")
            w_hi_ok, q_step, most_ok, all_ok, lora_mm = (wsem(n) for n in ("w_hi_ok", "q_step", "most_ok", "all_ok", "lora_mm"))
            ident0, bias_step, misc_hi = wsem("ident2_zeroed"), wsem("bias_step"), wsem("misc_hi")

            smalls = [
                (a_fc[:, :], d["a_fc"]), (bT_fc[:, :], d["b_fcT"]), (a_pj[:, :], d["a_pj"]), (bT_pj[:, :], d["b_pjT"]),
                (wq[:, :], d["wq1"]), (wk[:, :], d["wk1"]), (wv[:, :], d["wv1"]),
                (b1[:, :, :].rearrange("p e c -> p (e c)"), d["b1"]), (b_fc[:, :], d["b_fc"]),
                (bq[:, :], d["bq1"].rearrange("(p a) -> p a", a=1)), (bk[:, :], d["bk1"].rearrange("(p a) -> p a", a=1)),
                (b_pj[:, :], d["b_proj"].rearrange("(p a) -> p a", a=1)),
                (bv[:, :], d["bv1"].rearrange("(a n) -> a n", a=1)), (b2[:, :], d["b2"]), (routerT[:, :], d["routerT"]),
                (scal[:, 0:1], d["g_ffn"][0:1].partition_broadcast(P)), (scal[:, 1:2], d["g_xattn"][1:2].partition_broadcast(P)),
                (scal[:, 2:3], d["g_ffn"][1:2].partition_broadcast(P)),
            ]
            N_SMALL = 16 * len(smalls)

            with nc.Block() as block:
                @block.sync
                def _(sp):
                    sp.dma_start(quant[:, 0, :], d["w_fcT"]).then_inc(quant_in, 16)
                    sp.dma_start(quant[:, 1, :].rearrange("p (c d) -> p c d", c=FCH),
                                 d["w_pjT"].rearrange("(c p) d -> p c d", p=P)).then_inc(quant_in, 16)
                    for out_, in_ in smalls:
                        sp.dma_start(out_, in_).then_inc(small_in, 16)

                @block.scalar
                def _(act):
                    act.wait_ge(raw_in, 32)
                    nc.scalar.activation(w1_hi[:, :, :], w1_raw[:, :, :], ACT.Copy).then_inc(w_hi_ok, 1)
                    nc.scalar.activation(w2_hi[:, :, :, :], w2_raw[:, :, :, :], ACT.Copy).then_inc(w_hi_ok, 1)
                    act.wait_ge(small_in, N_SMALL)
                    nc.scalar.activation(q_hi[:, :], wq[:, :], ACT.Copy).then_inc(misc_hi, 1)
                    nc.scalar.activation(gates[:, 0:3], scal[:, :], ACT.Tanh).then_inc(tanh_ok, 1)

                @block.gpsimd
                def _(pool):
                    nc.gpsimd.memset(ident[:, :], 0.0).then_inc(ident0, 1)
                    nc.gpsimd.memset(neg_half[:, :], -0.5)
                    nc.gpsimd.iota(iota[:, :], [[1, EXPERTS]], base=0, channel_multiplier=0,
                                   allow_small_or_imprecise_dtypes=True)
                    pool.wait_ge(ident0, 1)
                    nc.gpsimd.affine_select(out=ident[:, :], in_=ident[:, :], compare_op=ALU.not_equal, fill=1.0,
                                            base=0, pattern=[[-1, P]], channel_multiplier=1)
                    pool.wait_ge(most_ok, 1)
                    nc.gpsimd.partition_all_reduce(most_all[:, :], most[:, :], P, bass.bass_isa.ReduceOp.max).then_inc(all_ok, 1)

                @block.tensor
                def _(pe):
                    pe.wait_ge(small_in, N_SMALL)
                    nc.tensor.matmul(lora_ps[0][:, :], a_fc[:, :], bT_fc[:, :], start=True, stop=True)
                    for c in range(FCH):
                        mm = nc.tensor.matmul(lora_ps[1][:, c * DIM:(c + 1) * DIM], a_pj[:, c * P:(c + 1) * P], bT_pj[:, :],
                                              start=True, stop=True)
                    mm.then_inc(lora_mm, 1)

                @block.vector
                def _(dve):
                    n = [0]

                    def chained(op):
                        n[0] += 1
                        op.then_inc(q_step, 1)
                        dve.wait_ge(q_step, n[0])

                    dve.wait_ge(quant_in, 32)
                    nc.vector.tensor_reduce(most[:, :], quant[:, :, :], AX.X, ALU.max,
                                            apply_absolute_value=True).then_inc(most_ok, 1)
                    dve.wait_ge(w_hi_ok, 1)
                    nc.vector.tensor_tensor(w1_lo[:, :, :], w1_raw[:, :, :], w1_hi[:, :, :], ALU.subtract)
                    dve.wait_ge(all_ok, 1)
                    chained(nc.vector.tensor_scalar(qscale[:, :], most_all[:, :], 1.0 / QMAX, None, ALU.mult))
                    chained(nc.vector.reciprocal(qinv[:, :], qscale[:, :]))
                    for i in range(2):
                        chained(nc.vector.tensor_scalar(work[:, i, :], quant[:, i, :], qinv[:, i:i + 1], ROUND, ALU.mult, ALU.add))
                        chained(nc.vector.tensor_scalar(work[:, i, :], work[:, i, :], ROUND, QMAX, ALU.subtract, ALU.min))
                        chained(nc.vector.tensor_scalar(work[:, i, :], work[:, i, :], -QMAX - 1, qscale[:, i:i + 1], ALU.max, ALU.mult))
                    chained(nc.vector.tensor_tensor(work[:, :, :], work[:, :, :], quant[:, :, :], ALU.subtract))
                    chained(nc.vector.tensor_tensor(work[:, :, :], work[:, :, :], quant[:, :, :], ALU.add))
                    dve.wait_ge(lora_mm, 1)
                    for i in range(2):
                        op = nc.vector.scalar_tensor_tensor(out=work[:, i, :], in0=lora_ps[i][:, :], scalar=LORA_SCALING,
                                                            in1=work[:, i, :], op0=ALU.mult, op1=ALU.add)
                    chained(op)
                    flat = [fc_hi[:, :], pj_hi[:, :, :].rearrange("p c d -> p (c d)")]
                    for i in range(2):
                        op = nc.vector.tensor_copy(flat[i], work[:, i, :])
                    chained(op)
                    nc.vector.tensor_tensor(fc_lo[:, :], work[:, 0, :], fc_hi[:, :], ALU.subtract)
                    nc.vector.tensor_tensor(pj_lo[:, :, :].rearrange("p c d -> p (c d)"), work[:, 1, :], flat[1], ALU.subtract)
                    dve.wait_ge(misc_hi, 1)
                    nc.vector.tensor_tensor(q_lo[:, :], wq[:, :], q_hi[:, :], ALU.subtract)
                    nc.vector.memset(ones[:, :].bitcast(F32), 1.0)
                    dve.wait_ge(tanh_ok, 1)
                    nc.vector.tensor_scalar(gates[:, 3:4], gates[:, 0:1], 0.5, None, ALU.mult)
                    nc.vector.tensor_scalar(neg_gate[:, :], gates[:, 0:1], -0.5, None, ALU.mult)
                    nc.vector.tensor_scalar(bq[:, :], bq[:, :], ISCALE, None, ALU.mult)
                    nc.vector.tensor_scalar(b_pj[:, :], b_pj[:, :], gates[:, 2:3], None, ALU.mult)
                    chained(nc.vector.tensor_scalar(bvg[:, :], bv[:, :], gates[0:1, 1:2], None, ALU.mult))
                    for b in range(GB):
                        op = nc.vector.tensor_copy(bv_hi[:, b, :], bvg[:, :])
                    chained(op)
                    for b in range(GB):
                        nc.vector.tensor_tensor(bv_lo[:, b, :], bvg[:, :], bv_hi[:, b, :], ALU.subtract)
                    dve.wait_ge(w_hi_ok, 2)
                    nc.vector.tensor_tensor(w2_lo[:, :, :, :], w2_raw[:, :, :, :], w2_hi[:, :, :, :], ALU.subtract)

        def pb(name):
            return ctx.enter_context(nc.psum_tensor(name, [P, 512], F32))

        hid_ps = [pb(f"hid_ps{i}") for i in range(2)]
        y_ps = [pb(f"y_ps{i}") for i in range(3)]
        turn_ps, att_ps, out_ps = pb("turn_ps"), pb("att_ps"), pb("out_ps")

        hid = [sb(f"hid{i}", [P, GTOK]) for i in range(2)]
        hid_hi = [sb(f"hid_hi{i}", [P, GTOK], F32R) for i in range(2)]
        hid_lo = [sb(f"hid_lo{i}", [P, GTOK], F32R) for i in range(2)]
        part = [sb(f"part{i}", [P, GTOK]) for i in range(2)]
        y_sum = sb("y_sum", [P, GTOK])
        comb_all = sb("comb_all", [P, EXPERTS, GTOK])
        moe_hi, moe_lo = (sb(n, [P, 2, GTOK], F32R) for n in ("moe_hi", "moe_lo"))
        two_hi, two_lo = (sb(n, [P, GTOK], F32R) for n in ("two_hi", "two_lo"))
        xnT = sb("xnT_route", [P, GTOK])
        xn = sb("xn_rest", [P, GB, DIM])
        stats, mv = sb("stats1", [P, GB, 6]), sb("mean_var1", [P, GB, 2])
        veps, rstd = sb("var_eps1", [P, GB]), sb("rstd1", [P, GB])
        best = sb("best", [P, GB, 8])
        best_at = sb("best_at", [P, GB, 8], mybir.dt.uint32)
        best_f = sb("best_f", [P, GB, 2])
        lead, lead_t = sb("lead", [P, GB]), sb("lead_tanh", [P, GB])
        weight = sb("weight", [P, 2, GB])
        hot = sb("hot", [P, 2, GB, EXPERTS])
        comb = sb("comb", [P, GB, EXPERTS])
        combT_next, combT = sb("combT_next", [EXPERTS, GTOK]), sb("combT", [EXPERTS, GTOK])
        ctxg = sb("ctxg1", [CDIM, GB, CTX])
        k1 = sb("k1", [DIM, GB, CTX])
        v1 = sb("v1", [CTX, GB, DIM])
        q1 = sb("q1", [DIM, GTOK])
        s1, e1, p1 = (sb(n, [P, GB, CTX]) for n in ("att_shifted", "att_expd", "att_probs"))
        p1T = sb("att_probsT", [CTX, GTOK])
        top1, total1, inv1 = (sb(n, [P, GB]) for n in ("top1", "total1", "inv1"))
        yT = sb("mlp_outT", [P, GTOK])

        hid_ready = sem("hid_ready")
        route_x, att_x, mlp_x = (sem(n) for n in ("route_x", "att_x", "mlp_x"))
        routeT_ready = sem("routeT_ready")
        moeT_ready, attT_ready, mlpT_ready = (sem(n) for n in ("moeT_ready", "attT_ready", "mlpT_ready"))
        comb_ready = sem("comb_ready")
        y_ready = sem("y_ready")
        ctxg_in = sem("ctxg_in")
        att_act = sem("att_act")
        att_prob = sem("att_prob")
        mlp_out = sem("mlp_out")
        hid_mm, turn_mm, att_mm, mlp_mm = (sem(n) for n in ("hid_mm", "turn_mm", "att_mm", "mlp_mm"))
        att_shift, lead_ok = sem("att_shift"), sem("lead_ok")
        gelu_ready, two_hi_ok, tanh_ready, att_exp = (sem(n) for n in ("gelu_ready", "two_hi_ok", "tanh_ready", "att_exp"))
        y_mm, out_mm, logit_mm, score_mm = (sem(n) for n in ("y_mm", "out_mm", "logit_mm", "score1_mm"))
        rstd_ok, summed = sem("rstd1_ok"), sem("summed")
        comb_in = [sem(f"comb_in{e}") for e in range(EXPERTS)]
        own = sem("dve_own")
        var_ok, part_ok, inv_ok, p_own = (sem(n) for n in ("var_ok", "part_ok", "inv_ok", "pool_own"))
        comb_free, combT_ok, comb_out, ctxg_free, x_done = (sem(n) for n in ("comb_free", "combT_ok", "comb_out", "ctxg_free", "x_done"))
        stored = sem("stored")

        class Round:

            def __init__(self, r, experts, two, route):
                self.r, self.experts, self.two, self.route = r, experts, two, route
                self.loop = not isinstance(r, int)

            def has(self, u):
                if u < 0:
                    return False
                if u >= SLOTS:
                    return self.route
                return self.two if u // FCH == MLP else self.experts

            def group(self, off):
                g = self.r + off
                return bass.ds(g, 1) if self.loop else slice(g, g + 1)

            def batches(self, off):
                g = (self.r + off) * GB
                return bass.ds(g, GB) if self.loop else slice(g, g + GB)

            def batch(self, off, b):
                g = (self.r + off) * GB + b
                return bass.ds(g, 1) if self.loop else slice(g, g + 1)

            def parity(self, off):
                p = (self.r + off) % 2
                return bass.ds(p, 1) if self.loop else slice(p, p + 1)

        def rounds(eng, taken, body):
            body(Round(0, True, False, True))
            taken.give_back()
            with eng.Fori(1, GROUPS - 1) as r:
                body(Round(r, True, True, True))
                taken.give_back()
            body(Round(GROUPS - 1, True, True, False))
            taken.give_back()
            body(Round(GROUPS, False, True, False))

        def flat(ap):
            return ap.rearrange("p a b -> p (a b)")

        with nc.Block() as block:
            @block.tensor
            def _(pe):
                taken = Taken(pe)

                def three(out_, a, b):
                    nc.tensor.matmul(out_, a[0], b[0], start=True, stop=False)
                    nc.tensor.matmul(out_, a[0], b[1], start=False, stop=False)
                    return nc.tensor.matmul(out_, a[1], b[0], start=False, stop=True)

                def turn(ready):
                    pe.wait_ge(ready, taken.next(ready))
                    for b in range(GB):
                        mm = nc.tensor.transpose(turn_ps[:, b * TOK:(b + 1) * TOK], xn[:, b, :], ident[:, :])
                    mm.then_inc(turn_mm, 1)

                def up(R, u):
                    if not R.has(u):
                        return
                    k, c = divmod(u % SLOTS, FCH)
                    if k == MLP:
                        if c == 0:
                            pe.wait_ge(mlpT_ready, taken.next(mlpT_ready))
                        w, rhs = [t[:, c * P:(c + 1) * P] for t in (fc_hi, fc_lo)], [t[:, :] for t in (two_hi, two_lo)]
                    else:
                        if u % SLOTS == 0:
                            pe.wait_ge(moeT_ready, taken.next(moeT_ready))
                        e = expert_of(k)
                        w = [t[:, e, c * P:(c + 1) * P] for t in (w1_hi, w1_lo)]
                        rhs = [flat(t[:, R.parity(u // SLOTS), :]) for t in (moe_hi, moe_lo)]
                    three(hid_ps[u % 2][:, :], w, rhs).then_inc(hid_mm, 1)

                def down(R, u):
                    if not R.has(u):
                        return
                    k, c = divmod(u, FCH)
                    pe.wait_ge(hid_ready, taken.next(hid_ready))
                    if k == MLP:
                        w = [t[:, c, :] for t in (pj_hi, pj_lo)]
                    else:
                        w = [t[:, expert_of(k), c, :] for t in (w2_hi, w2_lo)]
                    h = [t[u % 2][:, :] for t in (hid_hi, hid_lo)]
                    y = y_ps[k % 3][:, :]
                    nc.tensor.matmul(y, w[0], h[0], start=(c == 0), stop=False)
                    nc.tensor.matmul(y, w[1], h[0], start=False, stop=False)
                    mm = nc.tensor.matmul(y, w[0], h[1], start=False, stop=(c == FCH - 1))
                    if c == FCH - 1:
                        mm.then_inc(mlp_mm if k == MLP else y_mm, 1)

                def body(R):
                    for s in range(SLOTS):
                        down(R, s)
                        up(R, s + 2)
                        if R.two and s == 0:
                            pe.wait_ge(ctxg_in, taken.next(ctxg_in, 16))
                            nc.tensor.matmul(att_ps[:, 0:GB * CTX], wk[:, :], flat(ctxg[:, :, :]), start=True, stop=True)\
                              .then_inc(att_mm, 1)
                        if R.two and s == 1:
                            pe.wait_ge(y_ready, taken.next(y_ready))
                            for b in range(GB):
                                nc.tensor.matmul(out_ps[:, b * DIM:(b + 1) * DIM], combT[:, b * TOK:(b + 1) * TOK], b2[:, :],
                                                 start=(b == 0), stop=False, skip_group_check=True)
                            for b in range(GB):
                                mm = nc.tensor.matmul(out_ps[:, b * DIM:(b + 1) * DIM], y_sum[:, b * TOK:(b + 1) * TOK],
                                                      ident[:, :], start=False, stop=True, skip_group_check=True)
                            mm.then_inc(out_mm, 1)
                        if R.two and s == 3:
                            pe.wait_ge(att_act, taken.next(att_act))
                            for b in range(GB):
                                mm = nc.tensor.matmul(att_ps[0:CTX, b * DIM:(b + 1) * DIM], ctxg[:, b, :], wv[:, :],
                                                      start=True, stop=True)
                                if b == 0:
                                    pass
                            mm.then_inc(att_mm, 1)
                        if R.two and s == 7:
                            turn(att_x)
                        if R.two and s == 9:
                            pe.wait_ge(attT_ready, taken.next(attT_ready))
                            pe.wait_ge(att_act, taken.next(att_act))
                            three(att_ps[:, :], [q_hi[:, :], q_lo[:, :]], [two_hi[:, :], two_lo[:, :]]).then_inc(att_mm, 1)
                        if R.two and s == 11:
                            pe.wait_ge(att_act, taken.next(att_act))
                            for b in range(GB):
                                mm = nc.tensor.matmul(att_ps[:, b * CTX:(b + 1) * CTX], q1[:, b * TOK:(b + 1) * TOK],
                                                      k1[:, b, :], start=True, stop=True)
                            mm.then_inc(score_mm, 1)
                        if R.route and s == 12:
                            turn(route_x)
                        if R.route and s == 14:
                            pe.wait_ge(routeT_ready, taken.next(routeT_ready))
                            for b in range(GB):
                                mm = nc.tensor.matmul(turn_ps[:, b * EXPERTS:(b + 1) * EXPERTS], xnT[:, b * TOK:(b + 1) * TOK],
                                                      routerT[:, :], start=True, stop=True)
                            mm.then_inc(logit_mm, 1)
                        if R.two and s == 15:
                            pe.wait_ge(att_prob, taken.next(att_prob))
                            for b in range(GB):
                                mm = nc.tensor.transpose(att_ps[0:CTX, b * TOK:(b + 1) * TOK], p1[:, b, :], ident[:, :])
                            mm.then_inc(att_mm, 1)
                        if R.two and s == 17:
                            pe.wait_ge(att_act, taken.next(att_act))
                            for n, t in enumerate((bv_hi, bv_lo)):
                                nc.tensor.matmul(out_ps[:, :], ones[:, :], flat(t[:, :, :]), start=(n == 0), stop=False,
                                                 skip_group_check=True)
                            for b in range(GB):
                                mm = nc.tensor.matmul(out_ps[:, b * DIM:(b + 1) * DIM], p1T[:, b * TOK:(b + 1) * TOK],
                                                      v1[:, b, :], start=False, stop=True, skip_group_check=True)
                            mm.then_inc(out_mm, 1)
                        if R.route and s == 20:
                            pe.wait_ge(comb_ready, taken.next(comb_ready))
                            for b in range(GB):
                                mm = nc.tensor.transpose(turn_ps[0:EXPERTS, b * TOK:(b + 1) * TOK], comb[:, b, :], ident[:, :])
                            mm.then_inc(turn_mm, 1)
                        if R.two and s == 23:
                            turn(mlp_x)
                        if R.two and s == 33:
                            pe.wait_ge(mlp_out, taken.next(mlp_out))
                            for b in range(GB):
                                mm = nc.tensor.transpose(out_ps[:, b * DIM:(b + 1) * DIM], yT[:, b * TOK:(b + 1) * TOK], ident[:, :])
                            mm.then_inc(out_mm, 1)

                turn(route_x)
                pe.wait_ge(routeT_ready, taken.next(routeT_ready))
                for b in range(GB):
                    mm = nc.tensor.matmul(turn_ps[:, b * EXPERTS:(b + 1) * EXPERTS], xnT[:, b * TOK:(b + 1) * TOK],
                                          routerT[:, :], start=True, stop=True)
                mm.then_inc(logit_mm, 1)
                R0 = Round(0, True, False, True)
                up(R0, 0)
                up(R0, 1)
                pe.wait_ge(comb_ready, taken.next(comb_ready))
                for b in range(GB):
                    mm = nc.tensor.transpose(turn_ps[0:EXPERTS, b * TOK:(b + 1) * TOK], comb[:, b, :], ident[:, :])
                mm.then_inc(turn_mm, 1)
                taken.give_back()
                rounds(pe, taken, body)

            @block.scalar
            def _(act):
                taken = Taken(act)

                def gelu(R, u):
                    if not R.has(u):
                        return
                    k, c = divmod(u % SLOTS, FCH)
                    bias = b_fc[:, c:c + 1] if k == MLP else b1[:, expert_of(k), c:c + 1]
                    act.wait_ge(hid_mm, taken.next(hid_mm))
                    op = nc.scalar.activation(hid[u % 2][:, :], hid_ps[u % 2][:, :], ACT.Gelu, bias=bias)
                    if u % 2:
                        op = nc.scalar.activation(hid_hi[u % 2][:, :], hid_ps[u % 2][:, :], ACT.Gelu, bias=bias)
                    op.then_inc(gelu_ready, 1)

                def turned(out_):
                    act.wait_ge(turn_mm, taken.next(turn_mm))
                    return nc.scalar.activation(out_, turn_ps[0:out_.shape[0], :], ACT.Copy)

                def weights():
                    act.wait_ge(lead_ok, taken.next(lead_ok))
                    nc.scalar.activation(lead_t[:, :], lead[:, :], ACT.Tanh, scale=0.5).then_inc(tanh_ready, 1)

                def body(R):
                    for s in range(SLOTS):
                        gelu(R, s + 2)
                        if R.two:
                            if s in (0, 3, 9, 15):
                                act.wait_ge(att_mm, taken.next(att_mm))
                            if s == 0:
                                nc.scalar.activation(flat(k1[:, :, :]), att_ps[:, 0:GB * CTX], ACT.Identity, bias=bk[:, 0:1])\
                                  .then_inc(att_act, 1)
                            if s == 3:
                                nc.scalar.activation(flat(v1[:, :, :]), att_ps[0:CTX, :], ACT.Copy, scale=gates[0:CTX, 1:2])\
                                  .then_inc(att_act, 1)
                            if s == 7:
                                turned(two_hi[:, :]).then_inc(two_hi_ok, 1)
                            if s == 9:
                                nc.scalar.activation(q1[:, :], att_ps[:, :], ACT.Identity, bias=bq[:, 0:1], scale=ISCALE)\
                                  .then_inc(att_act, 1)
                            if s == 12:
                                act.wait_ge(att_shift, taken.next(att_shift))
                                nc.scalar.activation(e1[:, :, :], s1[:, :, :], ACT.Exp).then_inc(att_exp, 1)
                            if s == 15:
                                nc.scalar.activation(p1T[:, :], att_ps[0:CTX, :], ACT.Copy).then_inc(att_act, 1)
                            if s == 23:
                                turned(two_hi[:, :]).then_inc(two_hi_ok, 1)
                            if s == 31:
                                act.wait_ge(mlp_mm, taken.next(mlp_mm))
                                nc.scalar.activation(yT[:, :], y_ps[MLP % 3][:, :], ACT.Identity, bias=b_pj[:, 0:1],
                                                     scale=gates[:, 2:3]).then_inc(mlp_out, 1)
                        if R.experts and s == 4:
                            nc.scalar.activation(combT[:, :], combT_next[:, :], ACT.Copy)
                        if R.route:
                            if s == 12:
                                turned(xnT[:, :]).then_inc(routeT_ready, 1)
                            if s == 16:
                                weights()
                            if s == 20:
                                turned(combT_next[:, :]).then_inc(combT_ok, 1)

                turned(xnT[:, :]).then_inc(routeT_ready, 1)
                weights()
                R0 = Round(0, True, False, True)
                gelu(R0, 0)
                gelu(R0, 1)
                turned(combT_next[:, :]).then_inc(combT_ok, 1)
                taken.give_back()
                rounds(act, taken, body)

            @block.vector
            def _(dve):
                taken = Taken(dve)

                def done(op):
                    op.then_inc(own, 1)
                    dve.wait_ge(own, taken.next(own))

                def split(R, u, free_comb):
                    if not R.has(u):
                        return
                    dve.wait_ge(gelu_ready, taken.next(gelu_ready))
                    if u % 2 == 0:
                        if free_comb:
                            nc.vector.tensor_copy(hid_hi[0][:, :], hid[0][:, :]).then_inc(comb_free, 1)
                            dve.drain()
                        else:
                            done(nc.vector.tensor_copy(hid_hi[0][:, :], hid[0][:, :]))
                    nc.vector.tensor_tensor(hid_lo[u % 2][:, :], hid[u % 2][:, :], hid_hi[u % 2][:, :], ALU.subtract)\
                      .then_inc(hid_ready, 1)

                def statistics(xb):
                    for b in range(GB):
                        op = nc.vector.bn_stats(stats[:, b, :], flat(xb(b)))
                    done(op)
                    for b in range(GB):
                        op = nc.vector.bn_aggr(mv[:, b, :], stats[:, b, :])
                    op.then_inc(var_ok, 1)

                def normalise(xb, ready):
                    dve.wait_ge(rstd_ok, taken.next(rstd_ok))
                    for b in range(GB):
                        op = nc.vector.tensor_scalar(xn[:, b, :], flat(xb(b)), mv[:, b, 0:1], rstd[:, b:b + 1],
                                                     ALU.subtract, ALU.mult)
                    op.then_inc(ready, 1)

                def two_low(ready):
                    dve.wait_ge(two_hi_ok, taken.next(two_hi_ok))
                    nc.vector.tensor_tensor(two_lo[:, :], turn_ps[:, :], two_hi[:, :], ALU.subtract).then_inc(ready, 1)

                def add_out(R, off, after=None):
                    xg = x[:, R.batches(off), :]
                    dve.wait_ge(out_mm, taken.next(out_mm))
                    op = nc.vector.tensor_tensor(xg, out_ps[:, :].rearrange("p (b d) -> p b d", b=GB), xg, ALU.add)
                    if after is None:
                        done(op)
                    else:
                        op.then_inc(after, 1)

                def top_two():
                    dve.wait_ge(logit_mm, taken.next(logit_mm))
                    logits = turn_ps[:, 0:GB * EXPERTS].rearrange("p (b e) -> p b e", b=GB)
                    for b in range(GB):
                        op = nc.vector.max(best[:, b, :], logits[:, b, :])
                    done(op)
                    nc.vector.tensor_tensor(lead[:, :], best[:, :, 0], best[:, :, 1], ALU.subtract).then_inc(lead_ok, 1)
                    for b in range(GB):
                        op = nc.vector.max_index(best_at[:, b, :], best[:, b, :], logits[:, b, :])
                    done(op)
                    done(nc.vector.tensor_copy(best_f[:, :, :], best_at[:, :, 0:2]))
                    for n in range(2):
                        op = nc.vector.tensor_tensor(hot[:, n, :, :], iota[:, :].unsqueeze(1).to_broadcast([P, GB, EXPERTS]),
                                                     bcast(best_f[:, :, n], EXPERTS), ALU.is_equal)

                def combine():
                    dve.wait_ge(tanh_ready, taken.next(tanh_ready))
                    nc.vector.tensor_scalar(weight[:, 0, :], lead_t[:, :], gates[:, 3:4], gates[:, 3:4], ALU.mult, ALU.add)
                    done(nc.vector.tensor_scalar(weight[:, 1, :], lead_t[:, :], neg_gate[:, 0:1], gates[:, 3:4], ALU.mult, ALU.add))
                    for n in range(2):
                        op = nc.vector.tensor_tensor(hot[:, n, :, :], hot[:, n, :, :], bcast(weight[:, n, :], EXPERTS), ALU.mult)
                    done(op)
                    nc.vector.tensor_tensor(comb[:, :, :], hot[:, 0, :, :], hot[:, 1, :, :], ALU.add).then_inc(comb_ready, 1)

                def moe_split(par):
                    done(nc.vector.tensor_copy(flat(moe_hi[:, par, :]), xnT[:, :]))
                    nc.vector.tensor_tensor(flat(moe_lo[:, par, :]), xnT[:, :], flat(moe_hi[:, par, :]), ALU.subtract)\
                      .then_inc(moeT_ready, 1)

                def body(R):
                    for s in range(SLOTS):
                        split(R, s + 2, (s == 0 and R.two and R.experts) or (s % FCH == 0 and 0 < s < 32 and R.experts))
                        if R.experts and s % FCH == FCH - 1 and s // FCH != MLP:
                            e = expert_of(s // FCH)
                            dve.wait_ge(y_mm, taken.next(y_mm))
                            dve.wait_ge(comb_in[e], taken.next(comb_in[e], 16))
                            if e >= 2:
                                dve.wait_ge(summed, taken.next(summed))
                            nc.vector.tensor_tensor(part[e % 2][:, :], y_ps[(s // FCH) % 3][:, :], comb_all[:, e, :],
                                                    ALU.mult).then_inc(part_ok, 1)
                        if R.two:
                            if s == 2:
                                add_out(R, -1)
                            if s == 3:
                                statistics(lambda b: x[:, R.batch(-1, b), :])
                            if s == 5:
                                normalise(lambda b: x[:, R.batch(-1, b), :], att_x)
                            if s == 7:
                                two_low(attT_ready)
                            if s == 11:
                                dve.wait_ge(score_mm, taken.next(score_mm))
                                scores = att_ps[:, 0:GB * CTX].rearrange("p (b k) -> p b k", b=GB)
                                done(nc.vector.tensor_reduce(top1[:, :], scores, AX.X, ALU.max))
                                nc.vector.tensor_tensor(s1[:, :, :], scores, bcast(top1[:, :], CTX), ALU.subtract)\
                                  .then_inc(att_shift, 1)
                            if s == 13:
                                dve.wait_ge(att_exp, taken.next(att_exp))
                                done(nc.vector.tensor_reduce(total1[:, :], e1[:, :, :], AX.X, ALU.add))
                                nc.vector.reciprocal(inv1[:, :], total1[:, :]).then_inc(inv_ok, 1)
                            if s == 17:
                                add_out(R, -1)
                            if s == 18:
                                statistics(lambda b: x[:, R.batch(-1, b), :])
                            if s == 20:
                                normalise(lambda b: x[:, R.batch(-1, b), :], mlp_x)
                            if s == 23:
                                two_low(mlpT_ready)
                            if s == 33:
                                add_out(R, -1, x_done)
                        if R.route:
                            if s == 8:
                                statistics(lambda b: x[:, R.batch(1, b), :])
                            if s == 10:
                                normalise(lambda b: x[:, R.batch(1, b), :], route_x)
                            if s == 14:
                                top_two()
                            if s == 16:
                                moe_split(R.parity(1))
                            if s == 17:
                                combine()

                statistics(lambda b: x[:, b:b + 1, :])
                normalise(lambda b: x[:, b:b + 1, :], route_x)
                top_two()
                moe_split(slice(0, 1))
                combine()
                R0 = Round(0, True, False, True)
                split(R0, 0, False)
                split(R0, 1, False)
                taken.give_back()
                rounds(dve, taken, body)

            @block.gpsimd
            def _(pool):
                taken = Taken(pool)

                def root():
                    pool.wait_ge(var_ok, taken.next(var_ok))
                    nc.gpsimd.tensor_scalar(veps[:, :], mv[:, :, 1], EPS, None, ALU.add).then_inc(p_own, 1)
                    pool.wait_ge(p_own, taken.next(p_own))
                    nc.gpsimd.tensor_tensor(rstd[:, :], veps[:, :], neg_half[:, :], ALU.pow).then_inc(rstd_ok, 1)

                def body(R):
                    for s in range(SLOTS):
                        if R.experts and s % FCH == FCH - 1 and s // FCH != MLP:
                            e = expert_of(s // FCH)
                            pool.wait_ge(part_ok, taken.next(part_ok))
                            if e == 1:
                                nc.gpsimd.tensor_tensor(y_sum[:, :], part[0][:, :], part[1][:, :], ALU.add).then_inc(summed, 1)
                            elif 1 < e < EXPERTS - 1:
                                nc.gpsimd.tensor_tensor(y_sum[:, :], y_sum[:, :], part[e % 2][:, :], ALU.add).then_inc(summed, 1)
                            elif e == EXPERTS - 1:
                                nc.gpsimd.tensor_tensor(y_sum[:, :], y_sum[:, :], part[e % 2][:, :], ALU.add).then_inc(y_ready, 1)
                        if R.two and s == 3:
                            root()
                        if R.two and s == 13:
                            pool.wait_ge(inv_ok, taken.next(inv_ok))
                            nc.gpsimd.tensor_tensor(p1[:, :, :], e1[:, :, :], bcast(inv1[:, :], CTX), ALU.mult).then_inc(att_prob, 1)
                        if R.two and s == 18:
                            root()
                        if R.route and s == 8:
                            root()

                root()
                taken.give_back()
                rounds(pool, taken, body)

            @block.sync
            def _(sp):
                taken = Taken(sp)

                def context(g):
                    sp.dma_start(ctxg[:, :, :], d["ctxT"].rearrange("c (b t) -> c b t", b=BATCH)[:, g, :]).then_inc(ctxg_in, 16)

                def spill(R, off):
                    sp.wait_ge(combT_ok, taken.next(combT_ok))
                    sp.dma_start(comb_dram[R.group(off), :, :].rearrange("a e t -> (a e) t"), combT_next[:, :]).then_inc(comb_out, 16)
                    sp.wait_ge(comb_out, taken.next(comb_out, 16))

                def fetch(R, off, e):
                    sp.dma_start(comb_all[:, e, :], comb_dram[R.group(off), e, :].rearrange("a t -> (a t)").partition_broadcast(P))\
                      .then_inc(comb_in[e], 16)

                def body(R):
                    if R.two and R.experts:
                        sp.wait_ge(comb_free, taken.next(comb_free))
                        fetch(R, 0, EXPERTS - 1)
                    if R.route:
                        spill(R, 1)
                        for e in range(EXPERTS - 1):
                            sp.wait_ge(comb_free, taken.next(comb_free))
                            fetch(R, 1, e)
                    if R.two:
                        sp.wait_ge(x_done, taken.next(x_done))
                        sp.dma_start(out.rearrange("b t d -> t b d")[:, R.batches(-1), :], x[:, R.batches(-1), :]).then_inc(stored, 16)
                    if R.experts:
                        context(R.batches(0))

                R0 = Round(0, True, False, True)
                spill(R0, 0)
                for e in range(EXPERTS):
                    fetch(R0, 0, e)
                taken.give_back()
                rounds(sp, taken, body)
                sp.wait_ge(stored, 16 * GROUPS)


def program(nc, d, out):
    with ExitStack() as ctx:
        x = ctx.enter_context(nc.sbuf_tensor("x_sb", [P, BATCH, DIM], F32))
        w1_raw = ctx.enter_context(nc.sbuf_tensor("w1_raw", [P, EXPERTS, FFN], F32))
        w2_raw = ctx.enter_context(nc.sbuf_tensor("w2_raw", [P, EXPERTS, FCH, DIM], F32))
        raw_in = ctx.enter_context(nc.semaphore("experts_in"))
        head_attention(nc, d, x, w1_raw, w2_raw, raw_in)
        rest(nc, d, x, w1_raw, w2_raw, raw_in, out)


_L0 = "L0_xattn_"
_PLAIN = {"x": "x", "g_xattn": "g_xattn", "g_ffn": "g_ffn", "q_up": _L0 + "q_up", "k_up": _L0 + "k_up", "v_up": _L0 + "v_up",
          "o_up": _L0 + "o_up", "wo": _L0 + "Wo", "bo": _L0 + "bo", "q_alpha": _L0 + "q_alpha",
          "k_alpha": _L0 + "k_alpha", "v_alpha": _L0 + "v_alpha", "o_alpha": _L0 + "o_alpha",
          "b2": "L0_ffn_b2", "wq1": "L1_xattn_Wq", "bq1": "L1_xattn_bq", "wk1": "L1_xattn_Wk", "bk1": "L1_xattn_bk",
          "wv1": "L1_xattn_Wv", "bv1": "L1_xattn_bv", "a_fc": "L1_ffn_A_fc", "a_pj": "L1_ffn_A_proj", "b_proj": "L1_ffn_b_proj"}
_TURNED = {"q_downT": _L0 + "q_down", "k_downT": _L0 + "k_down", "v_downT": _L0 + "v_down", "o_downT": _L0 + "o_down",
           "routerT": "L0_ffn_router_w", "w_fcT": "L1_ffn_W_fc", "b_fcT": "L1_ffn_B_fc", "w_pjT": "L1_ffn_W_proj",
           "b_pjT": "L1_ffn_B_proj", "wqT": _L0 + "Wq", "wkT": _L0 + "Wk", "wvT": _L0 + "Wv", "wkiT": _L0 + "Wk_ipa", "wviT": _L0 + "Wv_ipa"}


def kernel(**inputs):
    import numpy as _np
    import concourse.bacc as _bacc
    from concourse import mybir as _mybir
    from concourse.bass_utils import run_bass_kernel_spmd as _run

    given = {n: _np.ascontiguousarray(inputs[src]) for n, src in _PLAIN.items()}
    given |= {n: _np.ascontiguousarray(_np.asarray(inputs[src]).T) for n, src in _TURNED.items()}
    c = _np.asarray(inputs["ctx_768"])
    given["ctxT"] = _np.ascontiguousarray(c.reshape(-1, c.shape[-1]).T)
    for n, src in (("w1T", "L0_ffn_w1"), ("w2T", "L0_ffn_w2")):
        given[n] = _np.ascontiguousarray(_np.asarray(inputs[src]).transpose(0, 2, 1))
    for n, src in (("b1", "L0_ffn_b1"), ("b_fc", "L1_ffn_b_fc")):
        given[n] = _np.ascontiguousarray(_np.asarray(inputs[src]).reshape(-1, P).T)
    nc = _bacc.Bacc("TRN2", target_bir_lowering=False, num_devices=1)
    dram, arrays = {}, {}
    for n, a in given.items():
        arrays[f"in_{n}"] = a
        dram[n] = nc.dram_tensor(f"in_{n}", a.shape, _mybir.dt.from_np(a.dtype), kind="ExternalInput").ap()
    out = nc.dram_tensor("out_x", (BATCH, TOK, DIM), F32, kind="ExternalOutput").ap()
    program(nc, dram, out)
    r = _run(nc, [arrays], core_ids=[0])
    return r.results[0]["out_x"]
```

```python
from contextlib import ExitStack

import concourse.bass as bass
from concourse import mybir

F32 = mybir.dt.float32
F32R = mybir.dt.float32r
ALU = mybir.AluOpType
ACT = mybir.ActivationFunctionType
AX = mybir.AxisListType

P = 128
BATCH, TOK, DIM = 32, 128, 128
CTX, CDIM = 120, 96
HEADS, DHEAD = 16, 64
INNER = HEADS * DHEAD
RANK = 32
IPA = 4
ORG = CTX - IPA
GB = 4
GROUPS = BATCH // GB
GTOK = GB * TOK
QH = 4
QUADS = HEADS // QH
UNITS = QUADS * GB
QCOLS = QH * CTX
CHUNKS = INNER // P
EPS = 1e-5
SCALE = DHEAD ** -0.5


class Taken:

    def __init__(self, eng):
        self.eng, self.count = eng, {}

    def next(self, sem, n=1):
        self.count[sem.name] = (sem, self.count.get(sem.name, (sem, 0))[1] + n)
        return self.count[sem.name][1]

    def give_back(self):
        for sem, n in self.count.values():
            self.eng.sem_inc(sem, -n)
        self.count = {}


def bcast(ap, n):
    return ap.unsqueeze(2).to_broadcast([ap.shape[0], ap.shape[1], n])


def item(step, ahead, last, count=UNITS):
    i = step + ahead
    if i < 0 or (last and i >= count):
        return None
    return i // count, i % count


def head_attention(nc, d, x, raw_in, keep):
    with ExitStack() as ctx:
        def sb(name, shape, dt=F32):
            return ctx.enter_context(nc.sbuf_tensor(name, shape, dt))

        def sem(name):
            return ctx.enter_context(nc.semaphore(name))

        ident = sb("ident", [P, P])
        ctx_hi, ctx_lo = (sb(n, [CDIM, BATCH, CTX], F32R) for n in ("ctx_hi", "ctx_lo"))
        a_hi, a_lo, b_hi, b_lo = (sb(n, [CDIM, HEADS * P], F32R) for n in ("a_hi", "a_lo", "b_hi", "b_lo"))
        kipa_hi, kipa_lo = (sb(n, [P, HEADS, BATCH, IPA], F32R) for n in ("kipa_hi", "kipa_lo"))
        bias_hi, bias_lo = (sb(n, [1, GB, DIM], F32R) for n in ("bias_hi", "bias_lo"))
        ones = sb("ones", [1, P], F32R)
        xn = sb("xn", [P, GB, DIM])
        xn_hi, xn_lo = (sb(n, [P, GTOK], F32R) for n in ("xnT_hi", "xnT_lo"))
        stats = sb("stats", [P, GB, 6])
        mv = sb("mean_var", [P, GB, 2])
        veps = sb("var_eps", [P, GB])
        rstd = sb("rstd", [P, GB])
        neg_half = sb("neg_half", [P, GB])
        vipa_dram = nc.dram_tensor("vipa_scratch", [BATCH * IPA, HEADS * DIM], F32, kind="Internal").ap()

        with ExitStack() as ws:
            def st(name, shape, dt=F32):
                return ws.enter_context(nc.sbuf_tensor(name, shape, dt, side="right"))

            def ps(name):
                return ws.enter_context(nc.psum_tensor(name, [P, 512], F32))

            wqT, wo = (st(n, [P, CHUNKS, DIM]) for n in ("wqT", "wo"))
            wkT, wvT, wkiT, wviT = (st(n, [P, CHUNKS, CDIM]) for n in ("wkT", "wvT", "wkiT", "wviT"))
            ups, downs = st("lora_ups", [P, INNER]), st("lora_downs", [P, 2 * DIM + 2 * CDIM])
            scal = st("scal", [P, 5])
            lora = st("lora", [P, 4])
            gate = st("gate", [P, 1])
            bo, bog = st("bo", [1, DIM]), st("bog", [1, DIM])
            ctx_raw = st("ctx_raw", [CDIM, BATCH, CTX])
            ctx_ipa = st("ctx_ipa", [CDIM, BATCH, IPA])
            vipa = st("vipa", [P, HEADS * DIM])
            a_ipa, b_ipa = (st(n, [CDIM, HEADS * P]) for n in ("a_ipa", "b_ipa"))
            wq2, wo2 = (st(n, [P, CHUNKS, 2, DIM]) for n in ("wq2", "wo2"))
            banks = [ps(f"setup{i}") for i in range(8)]
            first, second = banks[0:4], banks[4:8]

            def wsem(name):
                return ws.enter_context(nc.semaphore(name))

            scal_in, lora_in, qk_in, ki_in, vo_in, vi_in, ctx_in, x0_in, x_in, spilled = (
                wsem(n) for n in ("scal_in", "lora_in", "qk_in", "ki_in", "vo_in", "vi_in", "ctx_in", "x0_in", "x_in", "spilled"))
            zeroed, ident0, ident_ok, veps_ok, rstd_ok = (wsem(n) for n in ("zeroed", "ident_zeroed", "ident_ok", "veps0_ok", "rstd0_ok"))
            chunk_mm, fold_mm, ipa_mm, vipa_mm, turn_mm = (wsem(n) for n in ("chunk_mm", "fold_mm", "ipa_mm", "vipa_mm", "turn0_mm"))
            gated, split, fold_hi, fold_f32, ipa_hi, vipa_ok, xn_hi_ok = (
                wsem(n) for n in ("gated", "ctx_hi_ok", "fold_hi", "fold_f32", "ipa_hi", "vipa_ok", "xn_hi_ok"))
            lora_ok, chunk_ok, fold_lo, gathered, stat_ok, var_ok, xn_ok, bias_ok = (
                wsem(n) for n in ("lora_ok", "chunk_ok", "fold_lo", "ctx_ipa_ok", "stat0_ok", "var0_ok", "xn0_ok", "bias_ok"))

            def chunks(name):
                return d[name].rearrange("(c p) d -> p c d", p=P)

            FACTORS = [("q_up", "q_downT", DIM), ("k_up", "k_downT", CDIM), ("o_downT", "o_up", DIM), ("v_up", "v_downT", CDIM)]
            COLUMN = [0, DIM, DIM + CDIM, 2 * DIM + CDIM]
            scalars = [d["q_alpha"], d["k_alpha"], d["o_alpha"], d["v_alpha"], d["g_xattn"][0:1]]
            FBANKS = HEADS // 4

            with nc.Block() as block:
                @block.sync
                def _(sp):
                    for i, (up, _, _) in enumerate(FACTORS):
                        sp.dma_start(ups[i * RANK:(i + 1) * RANK, :], d[up]).then_inc(lora_in, 16)
                    for i, s in enumerate(scalars):
                        sp.dma_start(scal[:, i:i + 1], s.partition_broadcast(P)).then_inc(scal_in, 16)
                    sp.dma_start(wqT[:, :, :], chunks("wqT")).then_inc(qk_in, 16)
                    sp.dma_start(wkT[:, :, :], chunks("wkT")).then_inc(qk_in, 16)
                    sp.dma_start(wkiT[:, :, :], chunks("wkiT")).then_inc(ki_in, 16)
                    sp.dma_start(wo[:, :, :], chunks("wo")).then_inc(vo_in, 16)
                    sp.dma_start(wvT[:, :, :], chunks("wvT")).then_inc(vo_in, 16)
                    sp.dma_start(bo[:, :], d["bo"].rearrange("(a n) -> a n", a=1)).then_inc(vo_in, 16)
                    sp.dma_start(ctx_raw[:, :, :], d["ctxT"].rearrange("c (b t) -> c b t", b=BATCH)).then_inc(ctx_in, 16)
                    sp.dma_start(wviT[:, :, :], chunks("wviT")).then_inc(vi_in, 16)
                    xs = d["x"].rearrange("b t d -> t b d")
                    sp.dma_start(x[:, 0:GB, :], xs[:, 0:GB, :]).then_inc(x0_in, 16)
                    sp.dma_start(x[:, GB:BATCH, :], xs[:, GB:BATCH, :]).then_inc(x_in, 16)
                    for i in range(4):
                        sp.wait_ge(vipa_ok, i + 1)
                        sp.dma_start(vipa_dram[:, i * 512:i * 512 + 512],
                                     vipa[:, i * 512:i * 512 + 512]).then_inc(spilled, 16)
                    sp.wait_ge(spilled, 64)
                    sp.wait_ge(x_in, 16)

                @block.scalar
                def _(act):
                    act.wait_ge(zeroed, 1)
                    for i, (_, down, n) in enumerate(FACTORS):
                        act.dma_start(downs[i * RANK:(i + 1) * RANK, COLUMN[i]:COLUMN[i] + n], d[down]).then_inc(lora_in, 16)
                    act.wait_ge(scal_in, 16 * len(scalars))
                    nc.scalar.activation(gate[:, :], scal[:, 4:5], ACT.Tanh).then_inc(gated, 1)

                    def whole(out, k, n, scale):
                        act.wait_ge(fold_mm, n + 1)
                        nc.scalar.activation(out[:, k * 512:k * 512 + 512], (first, second)[out is b_ipa][k][0:CDIM, :],
                                             ACT.Copy, scale=scale).then_inc(fold_f32, 1)

                    def high(out, k, n, scale):
                        act.wait_ge(fold_mm, n + 1)
                        nc.scalar.activation(out[:, k * 512:k * 512 + 512], first[k][0:CDIM, :],
                                             ACT.Copy, scale=scale).then_inc(fold_hi, 1)

                    for k in range(FBANKS):
                        high(a_hi, k, k, SCALE)
                    for k in range(FBANKS):
                        whole(a_ipa, k, FBANKS + k, SCALE)
                    act.wait_ge(ctx_in, 16)
                    nc.scalar.activation(ctx_hi[:, :, :], ctx_raw[:, :, :], ACT.Copy).then_inc(split, 1)
                    act.wait_ge(gated, 1)
                    for k in range(FBANKS):
                        whole(b_ipa, k, 2 * FBANKS + k, gate[0:CDIM, 0:1])
                    for k in range(FBANKS):
                        high(b_hi, k, 3 * FBANKS + k, gate[0:CDIM, 0:1])
                    for i in range(4):
                        act.wait_ge(vipa_mm, i + 1)
                        nc.scalar.activation(vipa[:, i * 512:i * 512 + 512], second[i][:, :], ACT.Copy).then_inc(vipa_ok, 1)
                    for i in range(4):
                        act.wait_ge(ipa_mm, i + 1)
                        nc.scalar.activation(kipa_hi[:, 4 * i:4 * i + 4, :, :].rearrange("p h b t -> p (h b t)"),
                                             first[i][:, :], ACT.Copy).then_inc(ipa_hi, 1)
                    act.wait_ge(turn_mm, 1)
                    nc.scalar.activation(xn_hi[:, :], second[0][:, :], ACT.Copy).then_inc(xn_hi_ok, 1)

                @block.gpsimd
                def _(pool):
                    nc.gpsimd.memset(downs[:, :], 0.0).then_inc(zeroed, 1)
                    nc.gpsimd.memset(neg_half[:, :], -0.5)
                    nc.gpsimd.memset(ident[:, :], 0.0).then_inc(ident0, 1)
                    pool.wait_ge(ident0, 1)
                    nc.gpsimd.affine_select(out=ident[:, :], in_=ident[:, :], compare_op=ALU.not_equal, fill=1.0,
                                            base=0, pattern=[[-1, P]], channel_multiplier=1).then_inc(ident_ok, 1)
                    pool.wait_ge(var_ok, 1)
                    nc.gpsimd.tensor_scalar(veps[:, :], mv[:, :, 1], EPS, None, ALU.add).then_inc(veps_ok, 1)
                    pool.wait_ge(veps_ok, 1)
                    nc.gpsimd.tensor_tensor(rstd[:, :], veps[:, :], neg_half[:, :], ALU.pow).then_inc(rstd_ok, 1)

                @block.tensor
                def _(pe):
                    def fold(bank, left, right, k):
                        for c in range(2):
                            mm = nc.tensor.matmul(bank[k][0:CDIM, c * 2 * P:(c + 1) * 2 * P], left[:, 2 * k + c, :],
                                                  right[:, 2 * k + c, :, :].rearrange("p two d -> p (two d)"),
                                                  start=True, stop=True)
                        mm.then_inc(fold_mm, 1)

                    pe.wait_ge(lora_in, 16 * 2 * len(FACTORS))

                    def lora_products(i):
                        n = FACTORS[i][2]
                        for k in range(2):
                            for c in range(4):
                                mm = nc.tensor.matmul(banks[2 * i + k][:, c * n:(c + 1) * n],
                                                      ups[:, (4 * k + c) * P:(4 * k + c + 1) * P],
                                                      downs[:, COLUMN[i]:COLUMN[i] + n], start=True, stop=True)
                            mm.then_inc(chunk_mm, 1)

                    for i in range(3):
                        lora_products(i)
                    pe.wait_ge(chunk_ok, 4)
                    for k in range(FBANKS):
                        fold(first, wkT, wq2, k)
                    lora_products(3)
                    pe.wait_ge(ki_in, 16)
                    for k in range(FBANKS):
                        pe.wait_ge(fold_lo, k + 1)
                        fold(first, wkiT, wq2, k)
                    pe.wait_ge(vi_in, 16)
                    pe.wait_ge(chunk_ok, 8)
                    for k in range(FBANKS):
                        fold(second, wviT, wo2, k)
                    for k in range(FBANKS):
                        pe.wait_ge(fold_f32, k + 1)
                        fold(first, wvT, wo2, k)
                    pe.wait_ge(gathered, 1)
                    for i in range(4):
                        pe.wait_ge(fold_f32, FBANKS + i + 1)
                        nc.tensor.matmul(second[i][:, :], ctx_ipa[:, :, :].rearrange("c b t -> c (b t)"),
                                         b_ipa[:, i * 512:(i + 1) * 512], start=True, stop=True).then_inc(vipa_mm, 1)
                    for i in range(4):
                        pe.wait_ge(fold_lo, FBANKS + i + 1)
                        for h in range(4):
                            mm = nc.tensor.matmul(first[i][:, h * P:(h + 1) * P],
                                                  a_ipa[:, (4 * i + h) * P:(4 * i + h + 1) * P],
                                                  ctx_ipa[:, :, :].rearrange("c b t -> c (b t)"), start=True, stop=True)
                        mm.then_inc(ipa_mm, 1)
                    pe.wait_ge(ident_ok, 1)
                    pe.wait_ge(xn_ok, 1)
                    pe.wait_ge(vipa_ok, 1)
                    for b in range(GB):
                        mm = nc.tensor.transpose(second[0][:, b * TOK:(b + 1) * TOK], xn[:, b, :], ident[:, :])
                    mm.then_inc(turn_mm, 1)

                @block.vector
                def _(dve):
                    for t in (wq2, wo2):
                        nc.vector.memset(t[:, :, :, :], 0.0)
                    dve.wait_ge(scal_in, 16 * len(scalars))
                    nc.vector.tensor_scalar(lora[:, :], scal[:, 0:4], 1.0 / RANK, None, ALU.mult).then_inc(lora_ok, 1)
                    dve.wait_ge(lora_ok, 1)

                    def merge(i, w, out2):
                        n = FACTORS[i][2]
                        for k in range(2):
                            dve.wait_ge(chunk_mm, 2 * i + k + 1)
                            c4 = slice(4 * k, 4 * k + 4)
                            for r in ((slice(0, P),) if out2 is None else (slice(0, 64), slice(64, P))):
                                out = w[r, c4, :] if out2 is None else out2[r, c4, r.start // 64, :]
                                op = nc.vector.scalar_tensor_tensor(
                                    out=out, in0=banks[2 * i + k][r, 0:4 * n].rearrange("p (c d) -> p c d", c=4),
                                    scalar=lora[r, i:i + 1], in1=w[r, c4, :], op0=ALU.mult, op1=ALU.add)
                            op.then_inc(chunk_ok, 1)

                    def low(hi, lo, n, scale):
                        for k in range(FBANKS):
                            dve.wait_ge(fold_hi, n + k + 1)
                            cols = slice(k * 512, k * 512 + 512)
                            nc.vector.scalar_tensor_tensor(out=lo[:, cols], in0=first[k][0:CDIM, :], scalar=scale,
                                                           in1=hi[:, cols], op0=ALU.mult, op1=ALU.subtract).then_inc(fold_lo, 1)

                    dve.wait_ge(qk_in, 32)
                    merge(0, wqT, wq2)
                    merge(1, wkT, None)
                    low(a_hi, a_lo, 0, SCALE)
                    dve.wait_ge(vo_in, 48)
                    merge(2, wo, wo2)
                    merge(3, wvT, None)
                    dve.wait_ge(ctx_in, 16)
                    nc.vector.tensor_copy(ctx_ipa[:, :, :], ctx_raw[:, :, ORG:CTX]).then_inc(gathered, 1)
                    dve.wait_ge(split, 1)
                    nc.vector.tensor_tensor(ctx_lo[:, :, :], ctx_raw[:, :, :], ctx_hi[:, :, :], ALU.subtract)
                    low(b_hi, b_lo, FBANKS, gate[0:CDIM, 0:1])
                    dve.wait_ge(x0_in, 16)
                    for b in range(GB):
                        op = nc.vector.bn_stats(stats[:, b, :], x[:, b, :])
                    op.then_inc(stat_ok, 1)
                    dve.wait_ge(stat_ok, 1)
                    for b in range(GB):
                        op = nc.vector.bn_aggr(mv[:, b, :], stats[:, b, :])
                    op.then_inc(var_ok, 1)
                    dve.wait_ge(gated, 1)
                    nc.vector.tensor_scalar(bog[:, :], bo[:, :], gate[0:1, 0:1], None, ALU.mult).then_inc(bias_ok, 1)
                    nc.vector.memset(ones[:, :].bitcast(F32), 1.0)
                    dve.wait_ge(bias_ok, 1)
                    for b in range(GB):
                        op = nc.vector.tensor_copy(bias_hi[:, b, :], bog[:, :])
                    op.then_inc(bias_ok, 1)
                    dve.wait_ge(rstd_ok, 1)
                    for b in range(GB):
                        op = nc.vector.tensor_scalar(xn[:, b, :], x[:, b, :], mv[:, b, 0:1], rstd[:, b:b + 1],
                                                     ALU.subtract, ALU.mult)
                    op.then_inc(xn_ok, 1)
                    dve.wait_ge(bias_ok, 2)
                    for b in range(GB):
                        nc.vector.tensor_tensor(bias_lo[:, b, :], bog[:, :], bias_hi[:, b, :], ALU.subtract)
                    for i in range(4):
                        dve.wait_ge(ipa_hi, i + 1)
                        out = kipa_lo[:, 4 * i:4 * i + 4, :, :].rearrange("p h b t -> p (h b t)")
                        hi = kipa_hi[:, 4 * i:4 * i + 4, :, :].rearrange("p h b t -> p (h b t)")
                        nc.vector.tensor_tensor(out, first[i][:, :], hi, ALU.subtract)
                    dve.wait_ge(xn_hi_ok, 1)
                    nc.vector.tensor_tensor(xn_lo[:, :], second[0][:, :], xn_hi[:, :], ALU.subtract)

        def raw_and_low(name, shape):
            raw = keep.enter_context(nc.sbuf_tensor(name + "_raw", shape, F32, side="right"))
            return raw, nc.alloc_sbuf_tensor_at(name + "_lo", shape, F32R, offset=nc.sbuf_top)

        experts = raw_and_low("w1", [P, EXPERTS, FFN]) + raw_and_low("w2", [P, EXPERTS, FCH, DIM])
        w1_raw, _, w2_raw, _ = experts

        def pb(name, shape=(P, 512)):
            return ctx.enter_context(nc.psum_tensor(name, list(shape), F32))

        ctxg_hi, ctxg_lo = (sb(n, [CDIM, GB, CTX], F32R) for n in ("ctxg_hi", "ctxg_lo"))
        keys_hi = [sb(f"keys_hi{i}", [P, GB, QH, CTX], F32R) for i in range(2)]
        keys_lo = [sb(f"keys_lo{i}", [P, GB, QH, CTX], F32R) for i in range(2)]
        vals = [sb(f"vals{i}", [CTX, QH * DIM]) for i in range(2)]
        shifted = [sb(f"shifted{i}", [P, QH, CTX]) for i in range(2)]
        expd = [sb(f"expd{i}", [P, QH, CTX]) for i in range(2)]
        prob = [sb(f"prob{i}", [P, QH, CTX]) for i in range(2)]
        probT = sb("probT", [CTX, QH * TOK])
        top = sb("top", [P, 2, 2, QH])
        total = sb("total", [P, 2, 2, QH])
        inv = sb("inv", [P, 2, 2, QH])

        score_ps = [pb(f"score_ps{i}") for i in range(2)]
        key_ps, val_ps, probT_ps, xnT_ps, acc = (pb(n) for n in ("key_ps", "val_ps", "probT_ps", "xnT_ps", "acc"))

        norm_ready = sem("norm_ready")
        probT_ready = sem("probT_ready")
        vals_ready = sem("vals_ready")
        keys_lo_ready = sem("keys_lo_ready")
        xn_ready = sem("xn_ready")
        xnT_ready = sem("xnT_ready")
        ctxg_ready = sem("ctxg_ready")
        vipa_in = [sem(f"vipa_in{i}") for i in range(2)]
        acc_free = sem("acc_free")
        ipa_keys_first = sem("ipa_keys_first")
        probT_mm, vals_mm, keys_mm, xnT_mm = (sem(n) for n in ("probT_mm", "vals_mm", "keys_mm", "xnT_mm"))
        shift_ready = sem("shift_ready")
        score_mm, acc_mm = sem("score_mm"), sem("acc_mm")
        keys_hi_ready, exp_ready, xn_hi_ready = (sem(n) for n in ("keys_hi_ready", "exp_ready", "xn_hi_ready"))
        rstd_ready = sem("rstd_ready")
        d_max, d_sum, d_stat = (sem(n) for n in ("d_max", "d_sum", "d_stat"))
        inv_ready, var_ready = sem("inv_ready"), sem("var_ready")
        p_var = sem("p_var")
        vals_slot = sem("vals_slot")

        def key_bank(s):
            return key_ps if s >= 0 else (key_ps, xnT_ps, probT_ps, acc, key_ps, xnT_ps, acc)[s + 7]

        def segs(t):
            return [(t[:, :, 0:ORG], ORG, 0), (t[:, :, ORG:CTX], IPA, 1)]

        with nc.Block() as block:
            @block.tensor
            def _(pe):
                taken = Taken(pe)

                KEYS_SEEN = {-3: 1, -1: 2}

                def transpose_x():
                    pe.wait_ge(xn_ready, taken.next(xn_ready))
                    for b in range(GB):
                        mm = nc.tensor.transpose(xnT_ps[:, b * TOK:(b + 1) * TOK], xn[:, b, :], ident[:, :])
                    mm.then_inc(xnT_mm, 1)

                def three(out, a, b):
                    nc.tensor.matmul(out, a[0], b[0], start=True, stop=False)
                    nc.tensor.matmul(out, a[0], b[1], start=False, stop=False)
                    return nc.tensor.matmul(out, a[1], b[0], start=False, stop=True)

                def step(s, g, last):
                    if s >= 0:
                        pe.wait_ge(norm_ready, taken.next(norm_ready))
                        for h in range(QH):
                            mm = nc.tensor.transpose(probT_ps[0:CTX, h * TOK:(h + 1) * TOK], prob[s % 2][:, h, :], ident[:, :])
                            if h == 0:
                                mm.then_inc(vals_slot, 1)
                        mm.then_inc(probT_mm, 1)
                    if it := item(s, 2, last):
                        _, u = it
                        q, b = divmod(u, GB)
                        if u == 0:
                            if s < 0 and g == 0 and not last:
                                pe.wait_ge(ipa_keys_first, 1)
                                for _ in range(3):
                                    pe.wait_ge(keys_lo_ready, taken.next(keys_lo_ready))
                            pe.wait_ge(xnT_ready, taken.next(xnT_ready))
                        rhs = [t[q % 2][:, b, :, :].rearrange("p h k -> p (h k)") for t in (keys_hi, keys_lo)]
                        three(score_ps[u % 2][:, 0:QCOLS], [t[:, b * TOK:(b + 1) * TOK] for t in (xn_hi, xn_lo)], rhs)\
                            .then_inc(score_mm, 1)
                    if s >= 0:
                        pe.wait_ge(vals_ready, taken.next(vals_ready))
                    if it := item(s, 1, last):
                        dg, u = it
                        q, b = divmod(u, GB)
                        if u == 0:
                            pe.wait_ge(ctxg_ready, taken.next(ctxg_ready))
                        three(val_ps[0:CTX, :], [t[:, b, :] for t in (ctxg_hi, ctxg_lo)],
                              [t[:, q * QH * DIM:(q + 1) * QH * DIM] for t in (b_hi, b_lo)]).then_inc(vals_mm, 1)
                    for _ in range(KEYS_SEEN.get(s, 0) if s < 0 else item(s, 6, last) is not None):
                        pe.wait_ge(keys_lo_ready, taken.next(keys_lo_ready))
                    if it := item(s, 7, last):
                        dg, h = it
                        grp = bass.ds(g * GB + dg * GB, GB) if not isinstance(g, int) else slice((g + dg) * GB, (g + dg + 1) * GB)
                        three(key_bank(s)[:, 0:GB * ORG].rearrange("p (b k) -> p b k", b=GB),
                              [t[:, h * P:(h + 1) * P] for t in (a_hi, a_lo)],
                              [t[:, grp, 0:ORG] for t in (ctx_hi, ctx_lo)]).then_inc(keys_mm, 1)
                    if s >= 0:
                        q, b = divmod(s, GB)
                        if s == 0:
                            pe.wait_ge(acc_free, taken.next(acc_free))
                            for n, part in enumerate((bias_hi, bias_lo)):
                                nc.tensor.matmul(acc[:, :], ones[:, :], part[:, :, :].rearrange("p b d -> p (b d)"),
                                                 start=(n == 0), stop=False, skip_group_check=True)
                        pe.wait_ge(probT_ready, taken.next(probT_ready))
                        pe.wait_ge(vipa_in[s % 2], taken.next(vipa_in[s % 2], 16))
                        for h in range(QH):
                            mm = nc.tensor.matmul(acc[:, b * DIM:(b + 1) * DIM], probT[:, h * TOK:(h + 1) * TOK],
                                                  vals[s % 2][:, h * DIM:(h + 1) * DIM],
                                                  start=False, stop=(q == QUADS - 1 and h == QH - 1), skip_group_check=True)
                        if s == UNITS - 1:
                            mm.then_inc(acc_mm, 1)
                        if s == 9 and not last:
                            transpose_x()

                for s in range(-7, 0):
                    step(s, 0, False)
                taken.give_back()
                with pe.Fori(0, GROUPS - 1) as g:
                    for s in range(UNITS):
                        step(s, g, False)
                    taken.give_back()
                for s in range(UNITS):
                    step(s, GROUPS - 1, True)

            @block.scalar
            def _(act):
                taken = Taken(act)

                def copy_ctx(grp):
                    nc.scalar.activation(ctxg_hi[:, :, :], ctx_hi[:, grp, :], ACT.Copy)
                    nc.scalar.activation(ctxg_lo[:, :, :], ctx_lo[:, grp, :], ACT.Copy).then_inc(ctxg_ready, 1)

                def split_x():
                    act.wait_ge(xnT_mm, taken.next(xnT_mm))
                    nc.scalar.activation(xn_hi[:, :], xnT_ps[:, :], ACT.Copy).then_inc(xn_hi_ready, 1)

                def step(s, g, last):
                    if s >= 0:
                        act.wait_ge(probT_mm, taken.next(probT_mm))
                        nc.scalar.activation(probT[:, :], probT_ps[0:CTX, :], ACT.Copy).then_inc(probT_ready, 1)
                    if it := item(s, 1, last):
                        _, u = it
                        act.wait_ge(vals_mm, taken.next(vals_mm))
                        nc.scalar.activation(vals[u % 2][0:ORG, :], val_ps[0:ORG, :], ACT.Copy).then_inc(vals_ready, 1)
                    if s == 13 and not last:
                        split_x()
                    if s == 14 and not last:
                        copy_ctx(bass.ds(g * GB + GB, GB))
                    if it := item(s, 7, last):
                        _, k = it
                        q, h = divmod(k, QH)
                        act.wait_ge(keys_mm, taken.next(keys_mm))
                        nc.scalar.activation(keys_hi[q % 2][:, :, h, 0:ORG],
                                             key_bank(s)[:, 0:GB * ORG].rearrange("p (b k) -> p b k", b=GB),
                                             ACT.Copy).then_inc(keys_hi_ready, 1)
                    if it := item(s, 2, last):
                        _, u = it
                        act.wait_ge(shift_ready, taken.next(shift_ready))
                        nc.scalar.activation(expd[u % 2][:, :, :], shifted[u % 2][:, :, :], ACT.Exp).then_inc(exp_ready, 1)

                act.dma_start(w1_raw[:, :, :], d["w1T"].rearrange("e h f -> h e f")).then_inc(raw_in, 16)
                act.dma_start(w2_raw[:, :, :, :], d["w2T"].rearrange("e (c p) h -> p e c h", p=P)).then_inc(raw_in, 16)
                copy_ctx(slice(0, GB))
                for s in range(-7, 0):
                    step(s, 0, False)
                taken.give_back()
                with act.Fori(0, GROUPS - 1) as g:
                    for s in range(UNITS):
                        step(s, g, False)
                    taken.give_back()
                for s in range(UNITS):
                    step(s, GROUPS - 1, True)

            @block.vector
            def _(dve):
                taken = Taken(dve)

                def stat(b, xb, last_one):
                    op = nc.vector.bn_stats(stats[:, b, :], xb)
                    if last_one:
                        op.then_inc(d_stat, 1)

                def aggregate():
                    dve.wait_ge(d_stat, taken.next(d_stat))
                    for b in range(GB):
                        op = nc.vector.bn_aggr(mv[:, b, :], stats[:, b, :])
                    op.then_inc(var_ready, 1)

                def normalise(xg):
                    dve.wait_ge(rstd_ready, taken.next(rstd_ready))
                    for b in range(GB):
                        op = nc.vector.tensor_scalar(xn[:, b, :], xg(b), mv[:, b, 0:1], rstd[:, b:b + 1],
                                                     ALU.subtract, ALU.mult)
                    op.then_inc(xn_ready, 1)

                def split_x():
                    dve.wait_ge(xn_hi_ready, taken.next(xn_hi_ready))
                    nc.vector.tensor_tensor(xn_lo[:, :], xnT_ps[:, :], xn_hi[:, :], ALU.subtract).then_inc(xnT_ready, 1)

                def step(s, g, last):
                    if it := item(s, 1, last):
                        _, u = it
                        dve.wait_ge(exp_ready, taken.next(exp_ready))
                        for part, _, seg in segs(expd[u % 2]):
                            op = nc.vector.tensor_reduce(total[:, u % 2, seg, :], part, AX.X, ALU.add)
                        op.then_inc(d_sum, 1)
                        dve.wait_ge(d_sum, taken.next(d_sum))
                        nc.vector.reciprocal(inv[:, u % 2, :, :], total[:, u % 2, :, :]).then_inc(inv_ready, 1)
                    if it := item(s, 2, last):
                        _, u = it
                        score = score_ps[u % 2][:, 0:QCOLS].rearrange("p (h k) -> p h k", h=QH)
                        dve.wait_ge(score_mm, taken.next(score_mm))
                        for part, _, seg in segs(score):
                            op = nc.vector.tensor_reduce(top[:, u % 2, seg, :], part, AX.X, ALU.max)
                        op.then_inc(d_max, 1)
                        dve.wait_ge(d_max, taken.next(d_max))
                        for (part, n, seg), (out, _, _) in zip(segs(score), segs(shifted[u % 2])):
                            op = nc.vector.tensor_tensor(out, part, bcast(top[:, u % 2, seg, :], n), ALU.subtract)
                        op.then_inc(shift_ready, 1)
                    if s == 13 and not last:
                        split_x()
                    if it := item(s, 7, last):
                        _, k = it
                        q, h = divmod(k, QH)
                        dve.wait_ge(keys_hi_ready, taken.next(keys_hi_ready))
                        nc.vector.tensor_tensor(keys_lo[q % 2][:, :, h, 0:ORG],
                                                key_bank(s)[:, 0:GB * ORG].rearrange("p (b k) -> p b k", b=GB),
                                                keys_hi[q % 2][:, :, h, 0:ORG], ALU.subtract).then_inc(keys_lo_ready, 1)
                    if s >= 0 and not last:
                        if s < GB:
                            stat(s, x[:, bass.ds(g * GB + GB + s, 1), :].rearrange("p a d -> p (a d)"), s == GB - 1)
                        if s == GB:
                            aggregate()
                        if s == 7:
                            normalise(lambda b: x[:, bass.ds(g * GB + GB + b, 1), :].rearrange("p a d -> p (a d)"))
                    if s == UNITS - 1:
                        xg = x[:, bass.ds(g * GB, GB), :] if not isinstance(g, int) else x[:, g * GB:(g + 1) * GB, :]
                        dve.wait_ge(acc_mm, taken.next(acc_mm))
                        nc.vector.tensor_tensor(xg, acc[:, :].rearrange("p (b d) -> p b d", b=GB), xg, ALU.add)\
                          .then_inc(acc_free, 1)

                dve.sem_inc(acc_free, 1)
                dve.sem_inc(xnT_ready, 1)
                for s in range(-7, 0):
                    step(s, 0, False)
                taken.give_back()
                with dve.Fori(0, GROUPS - 1) as g:
                    for s in range(UNITS):
                        step(s, g, False)
                    taken.give_back()
                for s in range(UNITS):
                    step(s, GROUPS - 1, True)

            @block.gpsimd
            def _(pool):
                taken = Taken(pool)

                def ipa_keys(q, grp):
                    for slot, src in ((keys_hi, kipa_hi), (keys_lo, kipa_lo)):
                        op = nc.gpsimd.tensor_copy(slot[q % 2][:, :, :, ORG:CTX].rearrange("p b h t -> p h b t"),
                                                   src[:, q * QH:(q + 1) * QH, grp, :])
                    return op

                def rstd_of_group():
                    pool.wait_ge(var_ready, taken.next(var_ready))
                    nc.gpsimd.tensor_scalar(veps[:, :], mv[:, :, 1], EPS, None, ALU.add).then_inc(p_var, 1)
                    pool.wait_ge(p_var, taken.next(p_var))
                    nc.gpsimd.tensor_tensor(rstd[:, :], veps[:, :], neg_half[:, :], ALU.pow).then_inc(rstd_ready, 1)

                def step(s, g, last):
                    if it := item(s, 1, last):
                        _, u = it
                        pool.wait_ge(inv_ready, taken.next(inv_ready))
                        for (part, n, seg), (out, _, _) in zip(segs(expd[u % 2]), segs(prob[u % 2])):
                            op = nc.gpsimd.tensor_tensor(out, part, bcast(inv[:, u % 2, seg, :], n), ALU.mult)
                        op.then_inc(norm_ready, 1)
                    if s >= 0 and (s + 1) % GB == GB - 1 and item(s, 6, last):
                        dg, u = item(s, 6, last)
                        q = u // GB
                        ipa_keys(q, bass.ds(g * GB + dg * GB, GB) if not isinstance(g, int) else
                                 slice((g + dg) * GB, (g + dg + 1) * GB))
                    if s == 5 and not last:
                        rstd_of_group()

                ipa_keys(0, slice(0, GB))
                ipa_keys(1, slice(0, GB)).then_inc(ipa_keys_first, 1)
                for s in range(-7, 0):
                    step(s, 0, False)
                taken.give_back()
                with pool.Fori(0, GROUPS - 1) as g:
                    for s in range(UNITS):
                        step(s, g, False)
                    taken.give_back()
                for s in range(UNITS):
                    step(s, GROUPS - 1, True)

            @block.sync
            def _(sp):
                taken = Taken(sp)

                def fetch(u, row):
                    q = u // GB
                    sp.dma_start(vals[u % 2][ORG:CTX, :], vipa_dram[row, q * QH * DIM:(q + 1) * QH * DIM])\
                      .then_inc(vipa_in[u % 2], 16)

                def step(s, g, last):
                    sp.wait_ge(vals_slot, taken.next(vals_slot))
                    if it := item(s, 1, last):
                        dg, u = it
                        b = u % GB
                        start = (g * GB + dg * GB + b) * IPA
                        fetch(u, slice(start, start + IPA) if isinstance(g, int) else bass.ds(start, IPA))

                fetch(0, slice(0, IPA))
                with sp.Fori(0, GROUPS - 1) as g:
                    for s in range(UNITS):
                        step(s, g, False)
                    taken.give_back()
                for s in range(UNITS):
                    step(s, GROUPS - 1, True)
    return experts


EXPERTS, FFN = 8, 512
FCH = FFN // P
LORA_R = 16
LORA_SCALING = 2.0
QMAX = 127.0
ROUND = 1.5 * 2.0 ** 23
ISCALE = DIM ** -0.5
MLP = 7
PARTS = EXPERTS + 1
SLOTS = PARTS * FCH
AHEAD = 3


class At:
    KEYS = 2
    MOE_OUT = 4
    MOE_ADD = 3
    ATT_STATS = 3
    VALUES = 4
    COMB_KEEP = 4
    ATT_NORM = 5
    ATT_TURN = 8
    ATT_LOW = 8
    QUERIES = 10
    SCORES = 14
    MAX = 13
    EXP = 14
    TOTAL = 16
    PROB_TURN = 19
    ATT_OUT = 20
    ATT_ADD = 21
    MLP_STATS = 21
    MLP_NORM = 22
    MLP_TURN = 24
    MLP_LOW = 24
    MLP_COPY = 31
    MLP_OUT = 34
    MLP_ADD = 34
    ROUTE_STATS = 8
    ROUTE_NORM = 11
    ROUTE_TURN = 13
    LOGITS = 16
    TOP_TWO = 15
    MOE_SPLIT = 16
    TANH = 16
    COMBINE = 17
    COMB_TURN = 21

    PREPARE = (4, 8, 20, 21, 23, 24, 27, 28, 31)


def lo_from_pool(u):
    return u % 4 == 2


def hi_from_act(u):
    return u % 2 == 1 or lo_from_pool(u)


def expert_of(part):
    return EXPERTS - 1 if part == EXPERTS else part


def rest(nc, d, x, experts, raw_in, out):
    with ExitStack() as ctx:
        def sb(name, shape, dt=F32):
            return ctx.enter_context(nc.sbuf_tensor(name, shape, dt))

        def sem(name):
            return ctx.enter_context(nc.semaphore(name))

        ident = sb("ident2", [P, P])
        w1_hi = sb("w1_hi", [P, EXPERTS, FFN], F32R)
        w2_hi = sb("w2_hi", [P, EXPERTS, FCH, DIM], F32R)
        w1_raw, w1_lo, w2_raw, w2_lo = experts
        fc_hi, fc_lo = (sb(n, [P, FFN], F32R) for n in ("fc_hi", "fc_lo"))
        pj_hi, pj_lo = (sb(n, [P, FCH, DIM], F32R) for n in ("pj_hi", "pj_lo"))
        q_hi, q_lo = (sb(n, [DIM, DIM], F32R) for n in ("wq1_hi", "wq1_lo"))
        wk, wv = (sb(n, [CDIM, DIM]) for n in ("wk1", "wv1"))
        b1 = sb("b1", [P, EXPERTS, FCH])
        b_fc = sb("b_fc", [P, FCH])
        bq, bk, b_pj = (sb(n, [P, 1]) for n in ("bq", "bk", "b_pj"))
        b2 = sb("b2", [EXPERTS, DIM])
        routerT = sb("routerT", [DIM, EXPERTS])
        gates = sb("gates", [P, 4])
        neg_gate = sb("neg_gate", [P, 1])
        bv_hi, bv_lo = (sb(n, [1, GB, DIM], F32R) for n in ("bv_hi", "bv_lo"))
        ones = sb("ones1", [1, P], F32R)
        neg_half = sb("neg_half1", [P, GB])
        iota = sb("iota8", [P, EXPERTS])
        comb_dram = nc.dram_tensor("comb_scratch", [GROUPS, EXPERTS, GTOK], F32, kind="Internal").ap()

        quant = sb("quant", [P, 2, FFN])
        work = sb("work", [P, 2, FFN])
        most, most_all, qscale, qinv = (sb(n, [P, 2]) for n in ("most", "most_all", "qscale", "qinv"))
        a_fc, bT_fc = sb("a_fc", [LORA_R, DIM]), sb("bT_fc", [LORA_R, FFN])
        a_pj, bT_pj = sb("a_pj", [LORA_R, FFN]), sb("bT_pj", [LORA_R, DIM])
        wq = sb("wq1", [DIM, DIM])
        bv, bvg = sb("bv", [1, DIM]), sb("bvg", [1, DIM])
        scal = sb("scal1", [P, 3])
        first_in, small_in, quant_in = (sem(n) for n in ("first_in", "small_in", "quant_in"))
        ident0, ident_ok = sem("ident2_zeroed"), sem("ident2_ok")
        w_hi_ok, q_hi_ok, gates_ok = (sem(n) for n in ("w_hi_ok", "q_hi_ok", "gates_ok"))
        w_lo_ok, most_ok, prepared = sem("w_lo_ok"), sem("most_ok"), sem("prepared")
        all_ok, lora_mm = sem("all_ok"), sem("lora_mm")
        firsts = [
            (routerT[:, :], d["routerT"]),
            (scal[:, 0:1], d["g_ffn"][0:1].partition_broadcast(P)), (scal[:, 1:2], d["g_xattn"][1:2].partition_broadcast(P)),
            (scal[:, 2:3], d["g_ffn"][1:2].partition_broadcast(P)),
            (b1[:, :, :].rearrange("p e c -> p (e c)"), d["b1"]), (b2[:, :], d["b2"]),
        ]
        smalls = [
            (a_fc[:, :], d["a_fc"]), (bT_fc[:, :], d["b_fcT"]), (a_pj[:, :], d["a_pj"]), (bT_pj[:, :], d["b_pjT"]),
            (wq[:, :], d["wq1"]), (wk[:, :], d["wk1"]), (wv[:, :], d["wv1"]), (b_fc[:, :], d["b_fc"]),
            (bq[:, :], d["bq1"].rearrange("(p a) -> p a", a=1)), (bk[:, :], d["bk1"].rearrange("(p a) -> p a", a=1)),
            (b_pj[:, :], d["b_proj"].rearrange("(p a) -> p a", a=1)), (bv[:, :], d["bv1"].rearrange("(a n) -> a n", a=1)),
        ]

        def pb(name):
            return ctx.enter_context(nc.psum_tensor(name, [P, 512], F32))

        hid_ps = [pb(f"hid_ps{i}") for i in range(AHEAD)]
        y_ps = [pb(f"y_ps{i}") for i in range(2)]
        turn_ps, att_ps, out_ps = pb("turn_ps"), pb("att_ps"), pb("out_ps")

        hid = [sb(f"hid{i}", [P, GTOK]) for i in range(AHEAD)]
        hid_hi = [sb(f"hid_hi{i}", [P, GTOK], F32R) for i in range(AHEAD)]
        hid_lo = [sb(f"hid_lo{i}", [P, GTOK], F32R) for i in range(AHEAD)]
        part = [sb(f"part{i}", [P, GTOK]) for i in range(2)]
        y_sum = sb("y_sum", [P, GTOK])
        comb_all = sb("comb_all", [P, EXPERTS, GTOK])
        moe_hi, moe_lo = (sb(n, [P, 2, GTOK], F32R) for n in ("moe_hi", "moe_lo"))
        two_hi, two_lo = (sb(n, [P, GTOK], F32R) for n in ("two_hi", "two_lo"))
        xnT = sb("xnT_route", [P, GTOK])
        xn = sb("xn_rest", [P, GB, DIM])
        stats, mv = sb("stats1", [P, GB, 6]), sb("mean_var1", [P, GB, 2])
        veps, rstd = sb("var_eps1", [P, GB]), sb("rstd1", [P, GB])
        best = sb("best", [P, GB, 8])
        best_at = sb("best_at", [P, GB, 8], mybir.dt.uint32)
        best_f = sb("best_f", [P, GB, 2])
        lead, lead_t = sb("lead", [P, GB]), sb("lead_tanh", [P, GB])
        weight = sb("weight", [P, 2, GB])
        hot = sb("hot", [P, 2, GB, EXPERTS])
        comb = sb("comb", [P, GB, EXPERTS])
        combT_next, combT = sb("combT_next", [EXPERTS, GTOK]), sb("combT", [EXPERTS, GTOK])
        ctxg = sb("ctxg1", [CDIM, GB, CTX])
        k1 = sb("k1", [DIM, GB, CTX])
        v1 = sb("v1", [CTX, GB, DIM])
        q1 = sb("q1", [DIM, GTOK])
        s1, e1, p1 = (sb(n, [P, GB, CTX]) for n in ("att_shifted", "att_expd", "att_probs"))
        p1T = sb("att_probsT", [CTX, GTOK])
        top1, total1, inv1 = (sb(n, [P, GB]) for n in ("top1", "total1", "inv1"))
        yT = sb("mlp_outT", [P, GTOK])

        hid_ready, hid_ready_pool = sem("hid_ready"), sem("hid_ready_pool")
        route_x, att_x, mlp_x = (sem(n) for n in ("route_x", "att_x", "mlp_x"))
        routeT_ready = sem("routeT_ready")
        moeT_ready, attT_ready, mlpT_ready = (sem(n) for n in ("moeT_ready", "attT_ready", "mlpT_ready"))
        comb_ready = sem("comb_ready")
        y_ready = sem("y_ready")
        ctxg_in = sem("ctxg_in")
        att_act = sem("att_act")
        att_prob = sem("att_prob")
        mlp_out = sem("mlp_out")
        hid_mm, turn_mm, att_mm, mlp_mm = (sem(n) for n in ("hid_mm", "turn_mm", "att_mm", "mlp_mm"))
        att_shift, lead_ok = sem("att_shift"), sem("lead_ok")
        gelu_ready, two_hi_ok, tanh_ready, att_exp = (sem(n) for n in ("gelu_ready", "two_hi_ok", "tanh_ready", "att_exp"))
        y_mm, out_mm, logit_mm, score_mm = (sem(n) for n in ("y_mm", "out_mm", "logit_mm", "score1_mm"))
        rstd_ok, summed = sem("rstd1_ok"), sem("summed")
        comb_in = [sem(f"comb_in{e}") for e in range(EXPERTS)]
        own = sem("dve_own")
        var_ok, part_ok, inv_ok, p_own = (sem(n) for n in ("var_ok", "part_ok", "inv_ok", "pool_own"))
        gelu_for_pool = sem("gelu_for_pool")
        comb_free, combT_ok, comb_out, ctxg_free, x_done = (sem(n) for n in ("comb_free", "combT_ok", "comb_out", "ctxg_free", "x_done"))
        stored = sem("stored")

        class Round:

            def __init__(self, r, experts, two, route):
                self.r, self.experts, self.two, self.route = r, experts, two, route
                self.loop = not isinstance(r, int)
                self.first = not self.loop and r == 0

            def has(self, u):
                if u < 0:
                    return False
                if u >= SLOTS:
                    return self.route
                return self.two if u // FCH == MLP else self.experts

            def group(self, off):
                g = self.r + off
                return bass.ds(g, 1) if self.loop else slice(g, g + 1)

            def batches(self, off):
                g = (self.r + off) * GB
                return bass.ds(g, GB) if self.loop else slice(g, g + GB)

            def batch(self, off, b):
                g = (self.r + off) * GB + b
                return bass.ds(g, 1) if self.loop else slice(g, g + 1)

            def parity(self, off):
                p = (self.r + off) % 2
                return bass.ds(p, 1) if self.loop else slice(p, p + 1)

        def rounds(eng, taken, body):
            body(Round(0, True, False, True))
            taken.give_back()
            with eng.Fori(1, GROUPS - 1) as r:
                body(Round(r, True, True, True))
                taken.give_back()
            body(Round(GROUPS - 1, True, True, False))
            taken.give_back()
            body(Round(GROUPS, False, True, False))

        def flat(ap):
            return ap.rearrange("p a b -> p (a b)")

        with nc.Block() as block:
            @block.tensor
            def _(pe):
                taken = Taken(pe)

                def three(out_, a, b):
                    nc.tensor.matmul(out_, a[0], b[0], start=True, stop=False)
                    nc.tensor.matmul(out_, a[0], b[1], start=False, stop=False)
                    return nc.tensor.matmul(out_, a[1], b[0], start=False, stop=True)

                def turn(ready):
                    pe.wait_ge(ready, taken.next(ready))
                    for b in range(GB):
                        mm = nc.tensor.transpose(turn_ps[:, b * TOK:(b + 1) * TOK], xn[:, b, :], ident[:, :])
                    mm.then_inc(turn_mm, 1)

                def up(R, u):
                    if not R.has(u):
                        return
                    k, c = divmod(u % SLOTS, FCH)
                    if k == MLP:
                        if c == 0:
                            pe.wait_ge(mlpT_ready, taken.next(mlpT_ready))
                        w, rhs = [t[:, c * P:(c + 1) * P] for t in (fc_hi, fc_lo)], [t[:, :] for t in (two_hi, two_lo)]
                    else:
                        if u % SLOTS == 0:
                            pe.wait_ge(moeT_ready, taken.next(moeT_ready))
                        e = expert_of(k)
                        if R.first and u < SLOTS and c == 0:
                            pe.wait_ge(w_lo_ok, e + 1)
                        w = [t[:, e, c * P:(c + 1) * P] for t in (w1_hi, w1_lo)]
                        rhs = [flat(t[:, R.parity(u // SLOTS), :]) for t in (moe_hi, moe_lo)]
                    three(hid_ps[u % AHEAD][:, :], w, rhs).then_inc(hid_mm, 1)

                def down(R, u):
                    if not R.has(u):
                        return
                    k, c = divmod(u, FCH)
                    ready = hid_ready_pool if lo_from_pool(u) else hid_ready
                    pe.wait_ge(ready, taken.next(ready))
                    if k == MLP:
                        w = [t[:, c, :] for t in (pj_hi, pj_lo)]
                    else:
                        w = [t[:, expert_of(k), c, :] for t in (w2_hi, w2_lo)]
                    h = [t[u % AHEAD][:, :] for t in (hid_hi, hid_lo)]
                    y = (att_ps if k == MLP else y_ps[expert_of(k) % 2])[:, :]
                    nc.tensor.matmul(y, w[0], h[0], start=(c == 0), stop=False)
                    nc.tensor.matmul(y, w[1], h[0], start=False, stop=False)
                    mm = nc.tensor.matmul(y, w[0], h[1], start=False, stop=(c == FCH - 1))
                    if c == FCH - 1:
                        mm.then_inc(mlp_mm if k == MLP else y_mm, 1)

                def body(R):
                    for s in range(SLOTS):
                        down(R, s)
                        up(R, s + AHEAD)
                        if R.first:
                            prepare(s)
                        if R.two and s == At.KEYS:
                            pe.wait_ge(ctxg_in, taken.next(ctxg_in, 16))
                            nc.tensor.matmul(att_ps[:, 0:GB * CTX], wk[:, :], flat(ctxg[:, :, :]), start=True, stop=True)\
                              .then_inc(att_mm, 1)
                        if R.two and s == At.MOE_OUT:
                            pe.wait_ge(y_ready, taken.next(y_ready))
                            for b in range(GB):
                                nc.tensor.matmul(out_ps[:, b * DIM:(b + 1) * DIM], combT[:, b * TOK:(b + 1) * TOK], b2[:, :],
                                                 start=(b == 0), stop=False, skip_group_check=True)
                            for b in range(GB):
                                mm = nc.tensor.matmul(out_ps[:, b * DIM:(b + 1) * DIM], y_sum[:, b * TOK:(b + 1) * TOK],
                                                      ident[:, :], start=False, stop=True, skip_group_check=True)
                            mm.then_inc(out_mm, 1)
                        if R.two and s == At.VALUES:
                            pe.wait_ge(att_act, taken.next(att_act))
                            for b in range(GB):
                                mm = nc.tensor.matmul(att_ps[0:CTX, b * DIM:(b + 1) * DIM], ctxg[:, b, :], wv[:, :],
                                                      start=True, stop=True)
                            mm.then_inc(att_mm, 1)
                        if R.two and s == At.ATT_TURN:
                            turn(att_x)
                        if R.two and s == At.QUERIES:
                            pe.wait_ge(attT_ready, taken.next(attT_ready))
                            pe.wait_ge(att_act, taken.next(att_act))
                            three(att_ps[:, :], [q_hi[:, :], q_lo[:, :]], [two_hi[:, :], two_lo[:, :]]).then_inc(att_mm, 1)
                        if R.two and s == At.SCORES:
                            pe.wait_ge(att_act, taken.next(att_act))
                            for b in range(GB):
                                mm = nc.tensor.matmul(att_ps[:, b * CTX:(b + 1) * CTX], q1[:, b * TOK:(b + 1) * TOK],
                                                      k1[:, b, :], start=True, stop=True)
                            mm.then_inc(score_mm, 1)
                        if R.route and s == At.ROUTE_TURN:
                            turn(route_x)
                        if R.route and s == At.LOGITS:
                            pe.wait_ge(routeT_ready, taken.next(routeT_ready))
                            for b in range(GB):
                                mm = nc.tensor.matmul(turn_ps[:, b * EXPERTS:(b + 1) * EXPERTS], xnT[:, b * TOK:(b + 1) * TOK],
                                                      routerT[:, :], start=True, stop=True)
                            mm.then_inc(logit_mm, 1)
                        if R.two and s == At.PROB_TURN:
                            pe.wait_ge(att_prob, taken.next(att_prob))
                            for b in range(GB):
                                mm = nc.tensor.transpose(att_ps[0:CTX, b * TOK:(b + 1) * TOK], p1[:, b, :], ident[:, :])
                            mm.then_inc(att_mm, 1)
                        if R.two and s == At.ATT_OUT:
                            pe.wait_ge(att_act, taken.next(att_act))
                            for n, t in enumerate((bv_hi, bv_lo)):
                                nc.tensor.matmul(out_ps[:, :], ones[:, :], flat(t[:, :, :]), start=(n == 0), stop=False,
                                                 skip_group_check=True)
                            for b in range(GB):
                                mm = nc.tensor.matmul(out_ps[:, b * DIM:(b + 1) * DIM], p1T[:, b * TOK:(b + 1) * TOK],
                                                      v1[:, b, :], start=False, stop=True, skip_group_check=True)
                            mm.then_inc(out_mm, 1)
                        if R.route and s == At.COMB_TURN:
                            pe.wait_ge(comb_ready, taken.next(comb_ready))
                            for b in range(GB):
                                mm = nc.tensor.transpose(turn_ps[0:EXPERTS, b * TOK:(b + 1) * TOK], comb[:, b, :], ident[:, :])
                            mm.then_inc(turn_mm, 1)
                        if R.two and s == At.MLP_TURN:
                            turn(mlp_x)
                        if R.two and s == At.MLP_OUT:
                            pe.wait_ge(mlp_out, taken.next(mlp_out))
                            for b in range(GB):
                                mm = nc.tensor.transpose(out_ps[:, b * DIM:(b + 1) * DIM], yT[:, b * TOK:(b + 1) * TOK], ident[:, :])
                            mm.then_inc(out_mm, 1)

                def prepare(s):
                    if s == At.PREPARE[0]:
                        pe.wait_ge(small_in, 16 * len(smalls))
                        nc.tensor.matmul(att_ps[:, :], a_fc[:, :], bT_fc[:, :], start=True, stop=True)
                        for c in range(FCH):
                            mm = nc.tensor.matmul(out_ps[:, c * DIM:(c + 1) * DIM], a_pj[:, c * P:(c + 1) * P], bT_pj[:, :],
                                                  start=True, stop=True)
                        mm.then_inc(lora_mm, 1)
                    if s == SLOTS - 1:
                        pe.wait_ge(prepared, 1)

                pe.wait_ge(ident_ok, 1)
                pe.wait_ge(first_in, 16 * len(firsts))
                turn(route_x)
                pe.wait_ge(routeT_ready, taken.next(routeT_ready))
                for b in range(GB):
                    mm = nc.tensor.matmul(turn_ps[:, b * EXPERTS:(b + 1) * EXPERTS], xnT[:, b * TOK:(b + 1) * TOK],
                                          routerT[:, :], start=True, stop=True)
                mm.then_inc(logit_mm, 1)
                R0 = Round(0, True, False, True)
                for u in range(AHEAD):
                    up(R0, u)
                pe.wait_ge(comb_ready, taken.next(comb_ready))
                for b in range(GB):
                    mm = nc.tensor.transpose(turn_ps[0:EXPERTS, b * TOK:(b + 1) * TOK], comb[:, b, :], ident[:, :])
                mm.then_inc(turn_mm, 1)
                taken.give_back()
                rounds(pe, taken, body)

            @block.scalar
            def _(act):
                taken = Taken(act)

                def gelu(R, u):
                    if not R.has(u):
                        return
                    k, c = divmod(u % SLOTS, FCH)
                    bias = b_fc[:, c:c + 1] if k == MLP else b1[:, expert_of(k), c:c + 1]
                    act.wait_ge(hid_mm, taken.next(hid_mm))
                    op = nc.scalar.activation(hid[u % AHEAD][:, :], hid_ps[u % AHEAD][:, :], ACT.Gelu, bias=bias)
                    if hi_from_act(u):
                        op = nc.scalar.activation(hid_hi[u % AHEAD][:, :], hid_ps[u % AHEAD][:, :], ACT.Gelu, bias=bias)
                    op.then_inc(gelu_for_pool if lo_from_pool(u) else gelu_ready, 1)

                def turned(out_):
                    act.wait_ge(turn_mm, taken.next(turn_mm))
                    return nc.scalar.activation(out_, turn_ps[0:out_.shape[0], :], ACT.Copy)

                def weights():
                    act.wait_ge(lead_ok, taken.next(lead_ok))
                    nc.scalar.activation(lead_t[:, :], lead[:, :], ACT.Tanh, scale=0.5).then_inc(tanh_ready, 1)

                def expert_hi(e):
                    nc.scalar.activation(w1_hi[:, e, :], w1_raw[:, e, :], ACT.Copy)
                    nc.scalar.activation(w2_hi[:, e, :, :], w2_raw[:, e, :, :], ACT.Copy).then_inc(w_hi_ok, 1)

                def prepare(s):
                    if s % FCH == 0 and s // FCH + 2 < EXPERTS:
                        expert_hi(s // FCH + 2)
                    if s == At.PREPARE[0]:
                        act.wait_ge(small_in, 16 * len(smalls))
                        nc.scalar.activation(q_hi[:, :], wq[:, :], ACT.Copy).then_inc(q_hi_ok, 1)
                    if s == SLOTS - 1:
                        act.wait_ge(prepared, 1)

                def body(R):
                    for s in range(SLOTS):
                        gelu(R, s + AHEAD)
                        if R.first:
                            prepare(s)
                        if R.two:
                            if s == At.KEYS:
                                act.wait_ge(att_mm, taken.next(att_mm))
                                nc.scalar.activation(flat(k1[:, :, :]), att_ps[:, 0:GB * CTX], ACT.Identity, bias=bk[:, 0:1])\
                                  .then_inc(att_act, 1)
                            if s == At.VALUES:
                                act.wait_ge(att_mm, taken.next(att_mm))
                                nc.scalar.activation(flat(v1[:, :, :]), att_ps[0:CTX, :], ACT.Copy, scale=gates[0:CTX, 1:2])\
                                  .then_inc(att_act, 1)
                            if s == At.ATT_TURN:
                                turned(two_hi[:, :]).then_inc(two_hi_ok, 1)
                            if s == At.QUERIES:
                                act.wait_ge(att_mm, taken.next(att_mm))
                                nc.scalar.activation(q1[:, :], att_ps[:, :], ACT.Identity, bias=bq[:, 0:1], scale=ISCALE)\
                                  .then_inc(att_act, 1)
                            if s == At.EXP:
                                act.wait_ge(att_shift, taken.next(att_shift))
                                nc.scalar.activation(e1[:, :, :], s1[:, :, :], ACT.Exp).then_inc(att_exp, 1)
                            if s == At.PROB_TURN:
                                act.wait_ge(att_mm, taken.next(att_mm))
                                nc.scalar.activation(p1T[:, :], att_ps[0:CTX, :], ACT.Copy).then_inc(att_act, 1)
                            if s == At.MLP_TURN:
                                turned(two_hi[:, :]).then_inc(two_hi_ok, 1)
                            if s == At.MLP_COPY:
                                act.wait_ge(mlp_mm, taken.next(mlp_mm))
                                nc.scalar.activation(yT[:, :], att_ps[:, :], ACT.Identity, bias=b_pj[:, 0:1],
                                                     scale=gates[:, 2:3]).then_inc(mlp_out, 1)
                        if R.experts and s == At.COMB_KEEP:
                            nc.scalar.activation(combT[:, :], combT_next[:, :], ACT.Copy)
                        if R.route:
                            if s == At.ROUTE_TURN:
                                turned(xnT[:, :]).then_inc(routeT_ready, 1)
                            if s == At.TANH:
                                weights()
                            if s == At.COMB_TURN:
                                turned(combT_next[:, :]).then_inc(combT_ok, 1)

                act.wait_ge(raw_in, 32)
                expert_hi(0)
                turned(xnT[:, :]).then_inc(routeT_ready, 1)
                act.wait_ge(first_in, 16 * len(firsts))
                nc.scalar.activation(gates[:, 0:3], scal[:, :], ACT.Tanh).then_inc(gates_ok, 1)
                weights()
                expert_hi(1)
                R0 = Round(0, True, False, True)
                for u in range(AHEAD):
                    gelu(R0, u)
                turned(combT_next[:, :]).then_inc(combT_ok, 1)
                taken.give_back()
                rounds(act, taken, body)

            @block.vector
            def _(dve):
                taken = Taken(dve)

                def done(op):
                    op.then_inc(own, 1)
                    dve.wait_ge(own, taken.next(own))

                def split(R, u):
                    if not R.has(u) or lo_from_pool(u):
                        return
                    i = u % AHEAD
                    dve.wait_ge(gelu_ready, taken.next(gelu_ready))
                    if not hi_from_act(u):
                        done(nc.vector.tensor_copy(hid_hi[i][:, :], hid[i][:, :]))
                    nc.vector.tensor_tensor(hid_lo[i][:, :], hid[i][:, :], hid_hi[i][:, :], ALU.subtract).then_inc(hid_ready, 1)

                def statistics(xb):
                    for b in range(GB):
                        op = nc.vector.bn_stats(stats[:, b, :], flat(xb(b)))
                    done(op)
                    for b in range(GB):
                        op = nc.vector.bn_aggr(mv[:, b, :], stats[:, b, :])
                    op.then_inc(var_ok, 1)

                def normalise(xb, ready):
                    dve.wait_ge(rstd_ok, taken.next(rstd_ok))
                    for b in range(GB):
                        op = nc.vector.tensor_scalar(xn[:, b, :], flat(xb(b)), mv[:, b, 0:1], rstd[:, b:b + 1],
                                                     ALU.subtract, ALU.mult)
                    op.then_inc(ready, 1)

                def two_low(ready):
                    dve.wait_ge(two_hi_ok, taken.next(two_hi_ok))
                    nc.vector.tensor_tensor(two_lo[:, :], turn_ps[:, :], two_hi[:, :], ALU.subtract).then_inc(ready, 1)

                def add_out(R, off, after=None):
                    xg = x[:, R.batches(off), :]
                    dve.wait_ge(out_mm, taken.next(out_mm))
                    op = nc.vector.tensor_tensor(xg, out_ps[:, :].rearrange("p (b d) -> p b d", b=GB), xg, ALU.add)
                    if after is None:
                        done(op)
                    else:
                        op.then_inc(after, 1)

                def top_two():
                    dve.wait_ge(logit_mm, taken.next(logit_mm))
                    logits = turn_ps[:, 0:GB * EXPERTS].rearrange("p (b e) -> p b e", b=GB)
                    for b in range(GB):
                        op = nc.vector.max(best[:, b, :], logits[:, b, :])
                    done(op)
                    nc.vector.tensor_tensor(lead[:, :], best[:, :, 0], best[:, :, 1], ALU.subtract).then_inc(lead_ok, 1)
                    for b in range(GB):
                        op = nc.vector.max_index(best_at[:, b, :], best[:, b, :], logits[:, b, :])
                    done(op)
                    done(nc.vector.tensor_copy(best_f[:, :, :], best_at[:, :, 0:2]))
                    for n in range(2):
                        op = nc.vector.tensor_tensor(hot[:, n, :, :], iota[:, :].unsqueeze(1).to_broadcast([P, GB, EXPERTS]),
                                                     bcast(best_f[:, :, n], EXPERTS), ALU.is_equal)

                def combine():
                    dve.wait_ge(tanh_ready, taken.next(tanh_ready))
                    nc.vector.tensor_scalar(weight[:, 0, :], lead_t[:, :], gates[:, 3:4], gates[:, 3:4], ALU.mult, ALU.add)
                    done(nc.vector.tensor_scalar(weight[:, 1, :], lead_t[:, :], neg_gate[:, 0:1], gates[:, 3:4], ALU.mult, ALU.add))
                    for n in range(2):
                        op = nc.vector.tensor_tensor(hot[:, n, :, :], hot[:, n, :, :], bcast(weight[:, n, :], EXPERTS), ALU.mult)
                    done(op)
                    nc.vector.tensor_tensor(comb[:, :, :], hot[:, 0, :, :], hot[:, 1, :, :], ALU.add).then_inc(comb_ready, 1)

                def moe_split(par):
                    done(nc.vector.tensor_copy(flat(moe_hi[:, par, :]), xnT[:, :]))
                    nc.vector.tensor_tensor(flat(moe_lo[:, par, :]), xnT[:, :], flat(moe_hi[:, par, :]), ALU.subtract)\
                      .then_inc(moeT_ready, 1)

                def expert_lo(e):
                    dve.wait_ge(w_hi_ok, e + 1)
                    nc.vector.tensor_tensor(w1_lo[:, e, :], w1_raw[:, e, :], w1_hi[:, e, :], ALU.subtract)
                    nc.vector.tensor_tensor(w2_lo[:, e, :, :], w2_raw[:, e, :, :], w2_hi[:, e, :, :], ALU.subtract)\
                      .then_inc(w_lo_ok, 1)

                def prepare(s):
                    if s % FCH == 1 and s // FCH + 2 < EXPERTS:
                        expert_lo(s // FCH + 2)
                    at = At.PREPARE
                    if s == at[0]:
                        dve.wait_ge(quant_in, 32)
                        nc.vector.tensor_reduce(most[:, :], quant[:, :, :], AX.X, ALU.max,
                                                apply_absolute_value=True).then_inc(most_ok, 1)
                    if s == at[1]:
                        dve.wait_ge(all_ok, 1)
                        done(nc.vector.tensor_scalar(qscale[:, :], most_all[:, :], 1.0 / QMAX, None, ALU.mult))
                        done(nc.vector.reciprocal(qinv[:, :], qscale[:, :]))
                    for i in range(2):
                        if s == at[2 + i]:
                            w = work[:, i, :]
                            done(nc.vector.tensor_scalar(w, quant[:, i, :], qinv[:, i:i + 1], ROUND, ALU.mult, ALU.add))
                            done(nc.vector.tensor_scalar(w, w, ROUND, QMAX, ALU.subtract, ALU.min))
                            done(nc.vector.tensor_scalar(w, w, -QMAX - 1, qscale[:, i:i + 1], ALU.max, ALU.mult))
                    for i in range(2):
                        if s == at[4 + i]:
                            w = work[:, i, :]
                            done(nc.vector.tensor_tensor(w, w, quant[:, i, :], ALU.subtract))
                            done(nc.vector.tensor_tensor(w, w, quant[:, i, :], ALU.add))
                            if i == 0:
                                dve.wait_ge(lora_mm, 1)
                            done(nc.vector.scalar_tensor_tensor(out=w, in0=(att_ps, out_ps)[i][:, :], scalar=LORA_SCALING,
                                                                in1=w, op0=ALU.mult, op1=ALU.add))
                    for i, (hi, lo) in enumerate(((fc_hi[:, :], fc_lo[:, :]), (flat(pj_hi[:, :, :]), flat(pj_lo[:, :, :])))):
                        if s == at[6 + i]:
                            done(nc.vector.tensor_copy(hi, work[:, i, :]))
                            nc.vector.tensor_tensor(lo, work[:, i, :], hi, ALU.subtract)
                    if s == at[8]:
                        dve.wait_ge(q_hi_ok, 1)
                        nc.vector.tensor_tensor(q_lo[:, :], wq[:, :], q_hi[:, :], ALU.subtract)
                        nc.vector.memset(ones[:, :].bitcast(F32), 1.0)
                        nc.vector.tensor_scalar(bq[:, :], bq[:, :], ISCALE, None, ALU.mult)
                        nc.vector.tensor_scalar(b_pj[:, :], b_pj[:, :], gates[:, 2:3], None, ALU.mult)
                        done(nc.vector.tensor_scalar(bvg[:, :], bv[:, :], gates[0:1, 1:2], None, ALU.mult))
                        for b in range(GB):
                            op = nc.vector.tensor_copy(bv_hi[:, b, :], bvg[:, :])
                        done(op)
                        for b in range(GB):
                            op = nc.vector.tensor_tensor(bv_lo[:, b, :], bvg[:, :], bv_hi[:, b, :], ALU.subtract)
                        op.then_inc(prepared, 1)

                def body(R):
                    for s in range(SLOTS):
                        if R.first:
                            prepare(s)
                        if R.experts and s % FCH == FCH - 1 and s // FCH != MLP:
                            e = expert_of(s // FCH)
                            dve.wait_ge(y_mm, taken.next(y_mm))
                            dve.wait_ge(comb_in[e], taken.next(comb_in[e], 16))
                            if e >= 2:
                                dve.wait_ge(summed, taken.next(summed))
                            nc.vector.tensor_tensor(part[e % 2][:, :], y_ps[e % 2][:, :], comb_all[:, e, :],
                                                    ALU.mult).then_inc(part_ok, 1)
                        split(R, s + AHEAD)
                        if R.two:
                            if s == At.MOE_ADD:
                                add_out(R, -1)
                            if s == At.ATT_STATS:
                                statistics(lambda b: x[:, R.batch(-1, b), :])
                            if s == At.ATT_NORM:
                                normalise(lambda b: x[:, R.batch(-1, b), :], att_x)
                            if s == At.ATT_LOW:
                                two_low(attT_ready)
                            if s == At.MAX:
                                dve.wait_ge(score_mm, taken.next(score_mm))
                                scores = att_ps[:, 0:GB * CTX].rearrange("p (b k) -> p b k", b=GB)
                                done(nc.vector.tensor_reduce(top1[:, :], scores, AX.X, ALU.max))
                                nc.vector.tensor_tensor(s1[:, :, :], scores, bcast(top1[:, :], CTX), ALU.subtract)\
                                  .then_inc(att_shift, 1)
                            if s == At.TOTAL:
                                dve.wait_ge(att_exp, taken.next(att_exp))
                                done(nc.vector.tensor_reduce(total1[:, :], e1[:, :, :], AX.X, ALU.add))
                                nc.vector.reciprocal(inv1[:, :], total1[:, :]).then_inc(inv_ok, 1)
                            if s == At.ATT_ADD:
                                add_out(R, -1)
                            if s == At.MLP_STATS:
                                statistics(lambda b: x[:, R.batch(-1, b), :])
                            if s == At.MLP_NORM:
                                normalise(lambda b: x[:, R.batch(-1, b), :], mlp_x)
                            if s == At.MLP_LOW:
                                two_low(mlpT_ready)
                            if s == At.MLP_ADD:
                                add_out(R, -1, x_done)
                        if R.route:
                            if s == At.ROUTE_STATS:
                                statistics(lambda b: x[:, R.batch(1, b), :])
                            if s == At.ROUTE_NORM:
                                normalise(lambda b: x[:, R.batch(1, b), :], route_x)
                            if s == At.TOP_TWO:
                                top_two()
                            if s == At.MOE_SPLIT:
                                moe_split(R.parity(1))
                            if s == At.COMBINE:
                                combine()

                statistics(lambda b: x[:, b:b + 1, :])
                normalise(lambda b: x[:, b:b + 1, :], route_x)
                expert_lo(0)
                top_two()
                moe_split(slice(0, 1))
                dve.wait_ge(gates_ok, 1)
                nc.vector.tensor_scalar(gates[:, 3:4], gates[:, 0:1], 0.5, None, ALU.mult)
                done(nc.vector.tensor_scalar(neg_gate[:, :], gates[:, 0:1], -0.5, None, ALU.mult))
                combine()
                expert_lo(1)
                R0 = Round(0, True, False, True)
                for u in range(AHEAD):
                    split(R0, u)
                taken.give_back()
                rounds(dve, taken, body)

            @block.gpsimd
            def _(pool):
                taken = Taken(pool)

                def root():
                    pool.wait_ge(var_ok, taken.next(var_ok))
                    nc.gpsimd.tensor_scalar(veps[:, :], mv[:, :, 1], EPS, None, ALU.add).then_inc(p_own, 1)
                    pool.wait_ge(p_own, taken.next(p_own))
                    nc.gpsimd.tensor_tensor(rstd[:, :], veps[:, :], neg_half[:, :], ALU.pow).then_inc(rstd_ok, 1)

                def split(R, u):
                    if not R.has(u) or not lo_from_pool(u):
                        return
                    i = u % AHEAD
                    pool.wait_ge(gelu_for_pool, taken.next(gelu_for_pool))
                    nc.gpsimd.tensor_tensor(hid_lo[i][:, :], hid[i][:, :], hid_hi[i][:, :], ALU.subtract)\
                      .then_inc(hid_ready_pool, 1)

                def body(R):
                    for s in range(SLOTS):
                        split(R, s + AHEAD)
                        if R.first and s == At.PREPARE[0]:
                            pool.wait_ge(most_ok, 1)
                            nc.gpsimd.partition_all_reduce(most_all[:, :], most[:, :], P, bass.bass_isa.ReduceOp.max).then_inc(all_ok, 1)
                        if R.experts and s % FCH == FCH - 1 and s // FCH != MLP:
                            e = expert_of(s // FCH)
                            pool.wait_ge(part_ok, taken.next(part_ok))
                            pool.sem_inc(comb_free, 1)
                            if e == 1:
                                nc.gpsimd.tensor_tensor(y_sum[:, :], part[0][:, :], part[1][:, :], ALU.add).then_inc(summed, 1)
                            elif 1 < e < EXPERTS - 1:
                                nc.gpsimd.tensor_tensor(y_sum[:, :], y_sum[:, :], part[e % 2][:, :], ALU.add).then_inc(summed, 1)
                            elif e == EXPERTS - 1:
                                nc.gpsimd.tensor_tensor(y_sum[:, :], y_sum[:, :], part[e % 2][:, :], ALU.add).then_inc(y_ready, 1)
                        if R.two and s == At.ATT_STATS:
                            root()
                        if R.two and s == At.TOTAL:
                            pool.wait_ge(inv_ok, taken.next(inv_ok))
                            nc.gpsimd.tensor_tensor(p1[:, :, :], e1[:, :, :], bcast(inv1[:, :], CTX), ALU.mult).then_inc(att_prob, 1)
                        if R.two and s == At.MLP_STATS:
                            root()
                        if R.route and s == At.ROUTE_STATS:
                            root()

                nc.gpsimd.memset(neg_half[:, :], -0.5).then_inc(ident0, 1)
                pool.wait_ge(ident0, 1)
                root()
                nc.gpsimd.memset(ident[:, :], 0.0).then_inc(ident0, 1)
                nc.gpsimd.iota(iota[:, :], [[1, EXPERTS]], base=0, channel_multiplier=0, allow_small_or_imprecise_dtypes=True)
                pool.wait_ge(ident0, 2)
                nc.gpsimd.affine_select(out=ident[:, :], in_=ident[:, :], compare_op=ALU.not_equal, fill=1.0,
                                        base=0, pattern=[[-1, P]], channel_multiplier=1).then_inc(ident_ok, 1)
                R0 = Round(0, True, False, True)
                for u in range(AHEAD):
                    split(R0, u)
                taken.give_back()
                rounds(pool, taken, body)

            @block.sync
            def _(sp):
                taken = Taken(sp)

                def context(g):
                    sp.dma_start(ctxg[:, :, :], d["ctxT"].rearrange("c (b t) -> c b t", b=BATCH)[:, g, :]).then_inc(ctxg_in, 16)

                def spill(R, off):
                    sp.wait_ge(combT_ok, taken.next(combT_ok))
                    sp.dma_start(comb_dram[R.group(off), :, :].rearrange("a e t -> (a e) t"), combT_next[:, :]).then_inc(comb_out, 16)
                    sp.wait_ge(comb_out, taken.next(comb_out, 16))

                def fetch(R, off, e):
                    sp.dma_start(comb_all[:, e, :], comb_dram[R.group(off), e, :].rearrange("a t -> (a t)").partition_broadcast(P))\
                      .then_inc(comb_in[e], 16)

                def body(R):
                    if R.two and R.experts:
                        sp.wait_ge(comb_free, taken.next(comb_free))
                        fetch(R, 0, EXPERTS - 1)
                    if R.route:
                        spill(R, 1)
                        for e in range(EXPERTS - 1):
                            sp.wait_ge(comb_free, taken.next(comb_free))
                            fetch(R, 1, e)
                    if R.two:
                        sp.wait_ge(x_done, taken.next(x_done))
                        sp.dma_start(out.rearrange("b t d -> t b d")[:, R.batches(-1), :], x[:, R.batches(-1), :]).then_inc(stored, 16)
                    if R.experts:
                        context(R.batches(0))

                for out_, in_ in firsts:
                    sp.dma_start(out_, in_).then_inc(first_in, 16)
                sp.dma_start(quant[:, 0, :], d["w_fcT"]).then_inc(quant_in, 16)
                sp.dma_start(quant[:, 1, :].rearrange("p (c d) -> p c d", c=FCH),
                             d["w_pjT"].rearrange("(c p) d -> p c d", p=P)).then_inc(quant_in, 16)
                for out_, in_ in smalls:
                    sp.dma_start(out_, in_).then_inc(small_in, 16)
                R0 = Round(0, True, False, True)
                spill(R0, 0)
                for e in range(EXPERTS):
                    fetch(R0, 0, e)
                taken.give_back()
                rounds(sp, taken, body)
                sp.wait_ge(stored, 16 * GROUPS)


def program(nc, d, out):
    with ExitStack() as ctx:
        x = ctx.enter_context(nc.sbuf_tensor("x_sb", [P, BATCH, DIM], F32))
        raw_in = ctx.enter_context(nc.semaphore("experts_in"))
        experts = head_attention(nc, d, x, raw_in, ctx)
        rest(nc, d, x, experts, raw_in, out)


_L0 = "L0_xattn_"
_PLAIN = {"x": "x", "g_xattn": "g_xattn", "g_ffn": "g_ffn", "q_up": _L0 + "q_up", "k_up": _L0 + "k_up", "v_up": _L0 + "v_up",
          "o_up": _L0 + "o_up", "wo": _L0 + "Wo", "bo": _L0 + "bo", "q_alpha": _L0 + "q_alpha",
          "k_alpha": _L0 + "k_alpha", "v_alpha": _L0 + "v_alpha", "o_alpha": _L0 + "o_alpha",
          "b2": "L0_ffn_b2", "wq1": "L1_xattn_Wq", "bq1": "L1_xattn_bq", "wk1": "L1_xattn_Wk", "bk1": "L1_xattn_bk",
          "wv1": "L1_xattn_Wv", "bv1": "L1_xattn_bv", "a_fc": "L1_ffn_A_fc", "a_pj": "L1_ffn_A_proj", "b_proj": "L1_ffn_b_proj"}
_TURNED = {"q_downT": _L0 + "q_down", "k_downT": _L0 + "k_down", "v_downT": _L0 + "v_down", "o_downT": _L0 + "o_down",
           "routerT": "L0_ffn_router_w", "w_fcT": "L1_ffn_W_fc", "b_fcT": "L1_ffn_B_fc", "w_pjT": "L1_ffn_W_proj",
           "b_pjT": "L1_ffn_B_proj", "wqT": _L0 + "Wq", "wkT": _L0 + "Wk", "wvT": _L0 + "Wv", "wkiT": _L0 + "Wk_ipa", "wviT": _L0 + "Wv_ipa"}


def kernel(**inputs):
    import numpy as _np
    import concourse.bacc as _bacc
    from concourse import mybir as _mybir
    from concourse.bass_utils import run_bass_kernel_spmd as _run

    given = {n: _np.ascontiguousarray(inputs[src]) for n, src in _PLAIN.items()}
    given |= {n: _np.ascontiguousarray(_np.asarray(inputs[src]).T) for n, src in _TURNED.items()}
    c = _np.asarray(inputs["ctx_768"])
    given["ctxT"] = _np.ascontiguousarray(c.reshape(-1, c.shape[-1]).T)
    for n, src in (("w1T", "L0_ffn_w1"), ("w2T", "L0_ffn_w2")):
        given[n] = _np.ascontiguousarray(_np.asarray(inputs[src]).transpose(0, 2, 1))
    for n, src in (("b1", "L0_ffn_b1"), ("b_fc", "L1_ffn_b_fc")):
        given[n] = _np.ascontiguousarray(_np.asarray(inputs[src]).reshape(-1, P).T)
    nc = _bacc.Bacc("TRN2", target_bir_lowering=False, num_devices=1)
    dram, arrays = {}, {}
    for n, a in given.items():
        arrays[f"in_{n}"] = a
        dram[n] = nc.dram_tensor(f"in_{n}", a.shape, _mybir.dt.from_np(a.dtype), kind="ExternalInput").ap()
    out = nc.dram_tensor("out_x", (BATCH, TOK, DIM), F32, kind="ExternalOutput").ap()
    program(nc, dram, out)
    r = _run(nc, [arrays], core_ids=[0])
    return r.results[0]["out_x"]
```

```python
from contextlib import ExitStack

import concourse.bass as bass
from concourse import mybir

F32 = mybir.dt.float32
F32R = mybir.dt.float32r
ALU = mybir.AluOpType
ACT = mybir.ActivationFunctionType
AX = mybir.AxisListType

P = 128
BATCH, TOK, DIM = 32, 128, 128
CTX, CDIM = 120, 96
HEADS, DHEAD = 16, 64
INNER = HEADS * DHEAD
RANK = 32
IPA = 4
ORG = CTX - IPA
GB = 4
GROUPS = BATCH // GB
GTOK = GB * TOK
QH = 4
QUADS = HEADS // QH
UNITS = QUADS * GB
QCOLS = QH * CTX
CHUNKS = INNER // P
EPS = 1e-5
SCALE = DHEAD ** -0.5


class Taken:

    def __init__(self, eng):
        self.eng, self.count = eng, {}

    def next(self, sem, n=1):
        self.count[sem.name] = (sem, self.count.get(sem.name, (sem, 0))[1] + n)
        return self.count[sem.name][1]

    def give_back(self):
        for sem, n in self.count.values():
            self.eng.sem_inc(sem, -n)
        self.count = {}


def bcast(ap, n):
    return ap.unsqueeze(2).to_broadcast([ap.shape[0], ap.shape[1], n])


def item(step, ahead, last, count=UNITS):
    i = step + ahead
    if i < 0 or (last and i >= count):
        return None
    return i // count, i % count


def head_attention(nc, d, x, raw_in, keep):
    with ExitStack() as ctx:
        def sb(name, shape, dt=F32):
            return ctx.enter_context(nc.sbuf_tensor(name, shape, dt))

        def sem(name):
            return ctx.enter_context(nc.semaphore(name))

        ident = sb("ident", [P, P])
        ctx_hi, ctx_lo = (sb(n, [CDIM, BATCH, CTX], F32R) for n in ("ctx_hi", "ctx_lo"))
        a_hi, a_lo, b_hi, b_lo = (sb(n, [CDIM, HEADS * P], F32R) for n in ("a_hi", "a_lo", "b_hi", "b_lo"))
        kipa_hi, kipa_lo = (sb(n, [P, HEADS, BATCH, IPA], F32R) for n in ("kipa_hi", "kipa_lo"))
        bias = sb("bias", [P, DIM])
        xn = sb("xn", [P, GB, DIM])
        xn_hi, xn_lo = (sb(n, [P, GTOK], F32R) for n in ("xnT_hi", "xnT_lo"))
        stats = sb("stats", [P, GB, 6])
        mv = sb("mean_var", [P, GB, 2])
        veps = sb("var_eps", [P, GB])
        rstd = sb("rstd", [P, GB])
        neg_half = sb("neg_half", [P, GB])
        vipa_dram = nc.dram_tensor("vipa_scratch", [BATCH * IPA, HEADS * DIM], F32, kind="Internal").ap()

        with ExitStack() as ws:
            def st(name, shape, dt=F32):
                return ws.enter_context(nc.sbuf_tensor(name, shape, dt, side="right"))

            def ps(name):
                return ws.enter_context(nc.psum_tensor(name, [P, 512], F32))

            wqT, wo = (st(n, [P, CHUNKS, DIM]) for n in ("wqT", "wo"))
            wkT, wvT, wkiT, wviT = (st(n, [P, CHUNKS, CDIM]) for n in ("wkT", "wvT", "wkiT", "wviT"))
            ups, downs = st("lora_ups", [P, INNER]), st("lora_downs", [P, 2 * DIM + 2 * CDIM])
            scal = st("scal", [P, 5])
            lora = st("lora", [P, 4])
            gate = st("gate", [P, 1])
            bo = st("bo", [P, DIM])
            ctx_raw = st("ctx_raw", [CDIM, BATCH, CTX])
            ctx_ipa = st("ctx_ipa", [CDIM, BATCH, IPA])
            vipa = st("vipa", [P, HEADS * DIM])
            a_ipa, b_ipa = (st(n, [CDIM, HEADS * P]) for n in ("a_ipa", "b_ipa"))
            wq2, wo2 = (st(n, [P, CHUNKS, 2, DIM]) for n in ("wq2", "wo2"))
            banks = [ps(f"setup{i}") for i in range(8)]
            first, second = banks[0:4], banks[4:8]

            def wsem(name):
                return ws.enter_context(nc.semaphore(name))

            scal_in, lora_in, qk_in, ki_in, vo_in, vi_in, ctx_in, x0_in, x_in, spilled = (
                wsem(n) for n in ("scal_in", "lora_in", "qk_in", "ki_in", "vo_in", "vi_in", "ctx_in", "x0_in", "x_in", "spilled"))
            zeroed, ident0, ident_ok, veps_ok, rstd_ok = (wsem(n) for n in ("zeroed", "ident_zeroed", "ident_ok", "veps0_ok", "rstd0_ok"))
            chunk_mm, fold_mm, ipa_mm, vipa_mm, turn_mm = (wsem(n) for n in ("chunk_mm", "fold_mm", "ipa_mm", "vipa_mm", "turn0_mm"))
            gated, split, fold_hi, fold_f32, ipa_hi, vipa_ok, xn_hi_ok = (
                wsem(n) for n in ("gated", "ctx_hi_ok", "fold_hi", "fold_f32", "ipa_hi", "vipa_ok", "xn_hi_ok"))
            lora_ok, chunk_ok, fold_lo, gathered, stat_ok, var_ok, xn_ok = (
                wsem(n) for n in ("lora_ok", "chunk_ok", "fold_lo", "ctx_ipa_ok", "stat0_ok", "var0_ok", "xn0_ok"))

            def chunks(name):
                return d[name].rearrange("(c p) d -> p c d", p=P)

            FACTORS = [("q_up", "q_downT", DIM), ("k_up", "k_downT", CDIM), ("o_downT", "o_up", DIM), ("v_up", "v_downT", CDIM)]
            COLUMN = [0, DIM, DIM + CDIM, 2 * DIM + CDIM]
            scalars = [d["q_alpha"], d["k_alpha"], d["o_alpha"], d["v_alpha"], d["g_xattn"][0:1]]
            FBANKS = HEADS // 4

            with nc.Block() as block:
                @block.sync
                def _(sp):
                    for i, (up, _, _) in enumerate(FACTORS):
                        sp.dma_start(ups[i * RANK:(i + 1) * RANK, :], d[up]).then_inc(lora_in, 16)
                    for i, s in enumerate(scalars):
                        sp.dma_start(scal[:, i:i + 1], s.partition_broadcast(P)).then_inc(scal_in, 16)
                    sp.dma_start(wqT[:, :, :], chunks("wqT")).then_inc(qk_in, 16)
                    sp.dma_start(wkT[:, :, :], chunks("wkT")).then_inc(qk_in, 16)
                    sp.dma_start(wkiT[:, :, :], chunks("wkiT")).then_inc(ki_in, 16)
                    sp.dma_start(wo[:, :, :], chunks("wo")).then_inc(vo_in, 16)
                    sp.dma_start(wvT[:, :, :], chunks("wvT")).then_inc(vo_in, 16)
                    sp.dma_start(bo[:, :], d["bo"].partition_broadcast(P)).then_inc(vo_in, 16)
                    sp.dma_start(ctx_raw[:, :, :], d["ctxT"].rearrange("c (b t) -> c b t", b=BATCH)).then_inc(ctx_in, 16)
                    sp.dma_start(wviT[:, :, :], chunks("wviT")).then_inc(vi_in, 16)
                    xs = d["x"].rearrange("b t d -> t b d")
                    sp.dma_start(x[:, 0:GB, :], xs[:, 0:GB, :]).then_inc(x0_in, 16)
                    sp.dma_start(x[:, GB:BATCH, :], xs[:, GB:BATCH, :]).then_inc(x_in, 16)
                    for i in range(4):
                        sp.wait_ge(vipa_ok, i + 1)
                        sp.dma_start(vipa_dram[:, i * 512:i * 512 + 512],
                                     vipa[:, i * 512:i * 512 + 512]).then_inc(spilled, 16)
                    sp.wait_ge(spilled, 64)
                    sp.wait_ge(x_in, 16)

                @block.scalar
                def _(act):
                    act.wait_ge(zeroed, 1)
                    for i, (_, down, n) in enumerate(FACTORS):
                        act.dma_start(downs[i * RANK:(i + 1) * RANK, COLUMN[i]:COLUMN[i] + n], d[down]).then_inc(lora_in, 16)
                    act.wait_ge(scal_in, 16 * len(scalars))
                    nc.scalar.activation(gate[:, :], scal[:, 4:5], ACT.Tanh).then_inc(gated, 1)

                    def whole(out, k, n, scale):
                        act.wait_ge(fold_mm, n + 1)
                        nc.scalar.activation(out[:, k * 512:k * 512 + 512], (first, second)[out is b_ipa][k][0:CDIM, :],
                                             ACT.Copy, scale=scale).then_inc(fold_f32, 1)

                    def high(out, k, n, scale):
                        act.wait_ge(fold_mm, n + 1)
                        nc.scalar.activation(out[:, k * 512:k * 512 + 512], first[k][0:CDIM, :],
                                             ACT.Copy, scale=scale).then_inc(fold_hi, 1)

                    for k in range(FBANKS):
                        high(a_hi, k, k, SCALE)
                    for k in range(FBANKS):
                        whole(a_ipa, k, FBANKS + k, SCALE)
                    act.wait_ge(ctx_in, 16)
                    nc.scalar.activation(ctx_hi[:, :, :], ctx_raw[:, :, :], ACT.Copy).then_inc(split, 1)
                    act.wait_ge(gated, 1)
                    for k in range(FBANKS):
                        whole(b_ipa, k, 2 * FBANKS + k, gate[0:CDIM, 0:1])
                    for k in range(FBANKS):
                        high(b_hi, k, 3 * FBANKS + k, gate[0:CDIM, 0:1])
                    for i in range(4):
                        act.wait_ge(vipa_mm, i + 1)
                        nc.scalar.activation(vipa[:, i * 512:i * 512 + 512], second[i][:, :], ACT.Copy).then_inc(vipa_ok, 1)
                    for i in range(4):
                        act.wait_ge(ipa_mm, i + 1)
                        nc.scalar.activation(kipa_hi[:, 4 * i:4 * i + 4, :, :].rearrange("p h b t -> p (h b t)"),
                                             first[i][:, :], ACT.Copy).then_inc(ipa_hi, 1)
                    act.wait_ge(turn_mm, 1)
                    nc.scalar.activation(xn_hi[:, :], second[0][:, :], ACT.Copy).then_inc(xn_hi_ok, 1)

                @block.gpsimd
                def _(pool):
                    nc.gpsimd.memset(downs[:, :], 0.0).then_inc(zeroed, 1)
                    nc.gpsimd.memset(neg_half[:, :], -0.5)
                    nc.gpsimd.memset(ident[:, :], 0.0).then_inc(ident0, 1)
                    pool.wait_ge(ident0, 1)
                    nc.gpsimd.affine_select(out=ident[:, :], in_=ident[:, :], compare_op=ALU.not_equal, fill=1.0,
                                            base=0, pattern=[[-1, P]], channel_multiplier=1).then_inc(ident_ok, 1)
                    pool.wait_ge(var_ok, 1)
                    nc.gpsimd.tensor_scalar(veps[:, :], mv[:, :, 1], EPS, None, ALU.add).then_inc(veps_ok, 1)
                    pool.wait_ge(veps_ok, 1)
                    nc.gpsimd.tensor_tensor(rstd[:, :], veps[:, :], neg_half[:, :], ALU.pow).then_inc(rstd_ok, 1)

                @block.tensor
                def _(pe):
                    def fold(bank, left, right, k):
                        for c in range(2):
                            mm = nc.tensor.matmul(bank[k][0:CDIM, c * 2 * P:(c + 1) * 2 * P], left[:, 2 * k + c, :],
                                                  right[:, 2 * k + c, :, :].rearrange("p two d -> p (two d)"),
                                                  start=True, stop=True)
                        mm.then_inc(fold_mm, 1)

                    pe.wait_ge(lora_in, 16 * 2 * len(FACTORS))

                    def lora_products(i):
                        n = FACTORS[i][2]
                        for k in range(2):
                            for c in range(4):
                                mm = nc.tensor.matmul(banks[2 * i + k][:, c * n:(c + 1) * n],
                                                      ups[:, (4 * k + c) * P:(4 * k + c + 1) * P],
                                                      downs[:, COLUMN[i]:COLUMN[i] + n], start=True, stop=True)
                            mm.then_inc(chunk_mm, 1)

                    for i in range(3):
                        lora_products(i)
                    pe.wait_ge(chunk_ok, 4)
                    for k in range(FBANKS):
                        fold(first, wkT, wq2, k)
                    lora_products(3)
                    pe.wait_ge(ki_in, 16)
                    for k in range(FBANKS):
                        pe.wait_ge(fold_lo, k + 1)
                        fold(first, wkiT, wq2, k)
                    pe.wait_ge(vi_in, 16)
                    pe.wait_ge(chunk_ok, 8)
                    for k in range(FBANKS):
                        fold(second, wviT, wo2, k)
                    for k in range(FBANKS):
                        pe.wait_ge(fold_f32, k + 1)
                        fold(first, wvT, wo2, k)
                    pe.wait_ge(gathered, 1)
                    for i in range(4):
                        pe.wait_ge(fold_f32, FBANKS + i + 1)
                        nc.tensor.matmul(second[i][:, :], ctx_ipa[:, :, :].rearrange("c b t -> c (b t)"),
                                         b_ipa[:, i * 512:(i + 1) * 512], start=True, stop=True).then_inc(vipa_mm, 1)
                    for i in range(4):
                        pe.wait_ge(fold_lo, FBANKS + i + 1)
                        for h in range(4):
                            mm = nc.tensor.matmul(first[i][:, h * P:(h + 1) * P],
                                                  a_ipa[:, (4 * i + h) * P:(4 * i + h + 1) * P],
                                                  ctx_ipa[:, :, :].rearrange("c b t -> c (b t)"), start=True, stop=True)
                        mm.then_inc(ipa_mm, 1)
                    pe.wait_ge(ident_ok, 1)
                    pe.wait_ge(xn_ok, 1)
                    pe.wait_ge(vipa_ok, 1)
                    for b in range(GB):
                        mm = nc.tensor.transpose(second[0][:, b * TOK:(b + 1) * TOK], xn[:, b, :], ident[:, :])
                    mm.then_inc(turn_mm, 1)

                @block.vector
                def _(dve):
                    for t in (wq2, wo2):
                        nc.vector.memset(t[:, :, :, :], 0.0)
                    dve.wait_ge(scal_in, 16 * len(scalars))
                    nc.vector.tensor_scalar(lora[:, :], scal[:, 0:4], 1.0 / RANK, None, ALU.mult).then_inc(lora_ok, 1)
                    dve.wait_ge(lora_ok, 1)

                    def merge(i, w, out2):
                        n = FACTORS[i][2]
                        for k in range(2):
                            dve.wait_ge(chunk_mm, 2 * i + k + 1)
                            c4 = slice(4 * k, 4 * k + 4)
                            for r in ((slice(0, P),) if out2 is None else (slice(0, 64), slice(64, P))):
                                out = w[r, c4, :] if out2 is None else out2[r, c4, r.start // 64, :]
                                op = nc.vector.scalar_tensor_tensor(
                                    out=out, in0=banks[2 * i + k][r, 0:4 * n].rearrange("p (c d) -> p c d", c=4),
                                    scalar=lora[r, i:i + 1], in1=w[r, c4, :], op0=ALU.mult, op1=ALU.add)
                            op.then_inc(chunk_ok, 1)

                    def low(hi, lo, n, scale):
                        for k in range(FBANKS):
                            dve.wait_ge(fold_hi, n + k + 1)
                            cols = slice(k * 512, k * 512 + 512)
                            nc.vector.scalar_tensor_tensor(out=lo[:, cols], in0=first[k][0:CDIM, :], scalar=scale,
                                                           in1=hi[:, cols], op0=ALU.mult, op1=ALU.subtract).then_inc(fold_lo, 1)

                    dve.wait_ge(qk_in, 32)
                    merge(0, wqT, wq2)
                    merge(1, wkT, None)
                    low(a_hi, a_lo, 0, SCALE)
                    dve.wait_ge(vo_in, 48)
                    merge(2, wo, wo2)
                    merge(3, wvT, None)
                    dve.wait_ge(ctx_in, 16)
                    nc.vector.tensor_copy(ctx_ipa[:, :, :], ctx_raw[:, :, ORG:CTX]).then_inc(gathered, 1)
                    dve.wait_ge(split, 1)
                    nc.vector.tensor_tensor(ctx_lo[:, :, :], ctx_raw[:, :, :], ctx_hi[:, :, :], ALU.subtract)
                    low(b_hi, b_lo, FBANKS, gate[0:CDIM, 0:1])
                    dve.wait_ge(x0_in, 16)
                    for b in range(GB):
                        op = nc.vector.bn_stats(stats[:, b, :], x[:, b, :])
                    op.then_inc(stat_ok, 1)
                    dve.wait_ge(stat_ok, 1)
                    for b in range(GB):
                        op = nc.vector.bn_aggr(mv[:, b, :], stats[:, b, :])
                    op.then_inc(var_ok, 1)
                    dve.wait_ge(gated, 1)
                    nc.vector.tensor_scalar(bias[:, :], bo[:, :], gate[:, 0:1], None, ALU.mult)
                    dve.wait_ge(rstd_ok, 1)
                    for b in range(GB):
                        op = nc.vector.tensor_scalar(xn[:, b, :], x[:, b, :], mv[:, b, 0:1], rstd[:, b:b + 1],
                                                     ALU.subtract, ALU.mult)
                    op.then_inc(xn_ok, 1)
                    for i in range(4):
                        dve.wait_ge(ipa_hi, i + 1)
                        out = kipa_lo[:, 4 * i:4 * i + 4, :, :].rearrange("p h b t -> p (h b t)")
                        hi = kipa_hi[:, 4 * i:4 * i + 4, :, :].rearrange("p h b t -> p (h b t)")
                        nc.vector.tensor_tensor(out, first[i][:, :], hi, ALU.subtract)
                    dve.wait_ge(xn_hi_ok, 1)
                    nc.vector.tensor_tensor(xn_lo[:, :], second[0][:, :], xn_hi[:, :], ALU.subtract)

        def raw_and_low(name, shape):
            raw = keep.enter_context(nc.sbuf_tensor(name + "_raw", shape, F32, side="right"))
            return raw, nc.alloc_sbuf_tensor_at(name + "_lo", shape, F32R, offset=nc.sbuf_top)

        def kept(name, shape, dt=F32):
            return keep.enter_context(nc.sbuf_tensor(name, shape, dt, side="right"))

        experts = raw_and_low("w1", [P, EXPERTS, FFN]) + raw_and_low("w2", [P, EXPERTS, FCH, DIM])
        w1_raw, _, w2_raw, _ = experts
        routerT = kept("routerT", [DIM, EXPERTS])
        scal2 = kept("scal1", [P, 3])
        b1, b2 = kept("b1", [P, EXPERTS, FCH]), kept("b2", [DIM, EXPERTS])
        firsts = [
            (routerT[:, :], d["routerT"]),
            (scal2[:, 0:1], d["g_ffn"][0:1].partition_broadcast(P)), (scal2[:, 1:2], d["g_xattn"][1:2].partition_broadcast(P)),
            (scal2[:, 2:3], d["g_ffn"][1:2].partition_broadcast(P)),
            (b1[:, :, :].rearrange("p e c -> p (e c)"), d["b1"]), (b2[:, :], d["b2"]),
        ]
        xnT = kept("xnT_route", [P, GTOK])
        moe_hi, moe_lo = (kept(n, [P, 2, GTOK], F32R) for n in ("moe_hi", "moe_lo"))

        def pb(name, shape=(P, 512)):
            return ctx.enter_context(nc.psum_tensor(name, list(shape), F32))

        ctxg_hi, ctxg_lo = (sb(n, [CDIM, GB, CTX], F32R) for n in ("ctxg_hi", "ctxg_lo"))
        keys_hi = [sb(f"keys_hi{i}", [P, GB, QH, CTX], F32R) for i in range(2)]
        keys_lo = [sb(f"keys_lo{i}", [P, GB, QH, CTX], F32R) for i in range(2)]
        vals = [sb(f"vals{i}", [CTX, QH * DIM]) for i in range(2)]
        shifted = [sb(f"shifted{i}", [P, QH, CTX]) for i in range(2)]
        expd = [sb(f"expd{i}", [P, QH, CTX]) for i in range(2)]
        prob = [sb(f"prob{i}", [P, QH, CTX]) for i in range(2)]
        probT = sb("probT", [CTX, QH * TOK])
        top = sb("top", [P, 2, 2, QH])
        total = sb("total", [P, 2, 2, QH])
        inv = sb("inv", [P, 2, 2, QH])

        score_ps = [pb(f"score_ps{i}") for i in range(2)]
        key_ps, val_ps, probT_ps, xnT_ps, acc = (pb(n) for n in ("key_ps", "val_ps", "probT_ps", "xnT_ps", "acc"))

        norm_ready = sem("norm_ready")
        probT_ready = sem("probT_ready")
        vals_ready = sem("vals_ready")
        keys_lo_ready = sem("keys_lo_ready")
        xn_ready = sem("xn_ready")
        xnT_ready = sem("xnT_ready")
        ctxg_ready = sem("ctxg_ready")
        vipa_in = [sem(f"vipa_in{i}") for i in range(2)]
        acc_free = sem("acc_free")
        ipa_keys_first = sem("ipa_keys_first")
        probT_mm, vals_mm, keys_mm, xnT_mm = (sem(n) for n in ("probT_mm", "vals_mm", "keys_mm", "xnT_mm"))
        shift_ready = sem("shift_ready")
        score_mm, acc_mm = sem("score_mm"), sem("acc_mm")
        keys_hi_ready, exp_ready, xn_hi_ready = (sem(n) for n in ("keys_hi_ready", "exp_ready", "xn_hi_ready"))
        rstd_ready, bias_added = sem("rstd_ready"), sem("bias_added")
        d_max, d_sum, d_stat = (sem(n) for n in ("d_max", "d_sum", "d_stat"))
        inv_ready, var_ready = sem("inv_ready"), sem("var_ready")
        p_var = sem("p_var")
        vals_slot = sem("vals_slot")

        def key_bank(s):
            return key_ps if s >= 0 else (key_ps, xnT_ps, probT_ps, acc, key_ps, xnT_ps, acc)[s + 7]

        NORM, TURN = 7, 12

        def segs(t):
            return [(t[:, :, 0:ORG], ORG, 0), (t[:, :, ORG:CTX], IPA, 1)]

        with nc.Block() as block:
            @block.tensor
            def _(pe):
                taken = Taken(pe)

                KEYS_SEEN = {-3: 1, -1: 2}

                def transpose_x():
                    pe.wait_ge(xn_ready, taken.next(xn_ready))
                    for b in range(GB):
                        mm = nc.tensor.transpose(xnT_ps[:, b * TOK:(b + 1) * TOK], xn[:, b, :], ident[:, :])
                    mm.then_inc(xnT_mm, 1)

                def three(out, a, b):
                    nc.tensor.matmul(out, a[0], b[0], start=True, stop=False)
                    nc.tensor.matmul(out, a[0], b[1], start=False, stop=False)
                    return nc.tensor.matmul(out, a[1], b[0], start=False, stop=True)

                def step(s, g, last):
                    if s >= 0:
                        pe.wait_ge(norm_ready, taken.next(norm_ready))
                        for h in range(QH):
                            mm = nc.tensor.transpose(probT_ps[0:CTX, h * TOK:(h + 1) * TOK], prob[s % 2][:, h, :], ident[:, :])
                            if h == 0:
                                mm.then_inc(vals_slot, 1)
                        mm.then_inc(probT_mm, 1)
                    if it := item(s, 2, last):
                        _, u = it
                        q, b = divmod(u, GB)
                        if u == 0:
                            if s < 0 and g == 0 and not last:
                                pe.wait_ge(ipa_keys_first, 1)
                                for _ in range(3):
                                    pe.wait_ge(keys_lo_ready, taken.next(keys_lo_ready))
                            pe.wait_ge(xnT_ready, taken.next(xnT_ready))
                        rhs = [t[q % 2][:, b, :, :].rearrange("p h k -> p (h k)") for t in (keys_hi, keys_lo)]
                        three(score_ps[u % 2][:, 0:QCOLS], [t[:, b * TOK:(b + 1) * TOK] for t in (xn_hi, xn_lo)], rhs)\
                            .then_inc(score_mm, 1)
                    if s >= 0:
                        pe.wait_ge(vals_ready, taken.next(vals_ready))
                    if it := item(s, 1, last):
                        dg, u = it
                        q, b = divmod(u, GB)
                        if u == 0:
                            pe.wait_ge(ctxg_ready, taken.next(ctxg_ready))
                        three(val_ps[0:CTX, :], [t[:, b, :] for t in (ctxg_hi, ctxg_lo)],
                              [t[:, q * QH * DIM:(q + 1) * QH * DIM] for t in (b_hi, b_lo)]).then_inc(vals_mm, 1)
                    for _ in range(KEYS_SEEN.get(s, 0) if s < 0 else item(s, 6, last) is not None):
                        pe.wait_ge(keys_lo_ready, taken.next(keys_lo_ready))
                    if it := item(s, 7, last):
                        dg, h = it
                        grp = bass.ds(g * GB + dg * GB, GB) if not isinstance(g, int) else slice((g + dg) * GB, (g + dg + 1) * GB)
                        three(key_bank(s)[:, 0:GB * ORG].rearrange("p (b k) -> p b k", b=GB),
                              [t[:, h * P:(h + 1) * P] for t in (a_hi, a_lo)],
                              [t[:, grp, 0:ORG] for t in (ctx_hi, ctx_lo)]).then_inc(keys_mm, 1)
                    if s >= 0:
                        q, b = divmod(s, GB)
                        if s == 0:
                            pe.wait_ge(acc_free, taken.next(acc_free))
                        pe.wait_ge(probT_ready, taken.next(probT_ready))
                        pe.wait_ge(vipa_in[s % 2], taken.next(vipa_in[s % 2], 16))
                        for h in range(QH):
                            mm = nc.tensor.matmul(acc[:, b * DIM:(b + 1) * DIM], probT[:, h * TOK:(h + 1) * TOK],
                                                  vals[s % 2][:, h * DIM:(h + 1) * DIM],
                                                  start=(s == 0 and h == 0), stop=(q == QUADS - 1 and h == QH - 1),
                                                  skip_group_check=True)
                        if s == UNITS - 1:
                            mm.then_inc(acc_mm, 1)
                        if s == TURN:
                            transpose_x()

                for s in range(-7, 0):
                    step(s, 0, False)
                taken.give_back()
                with pe.Fori(0, GROUPS - 1) as g:
                    for s in range(UNITS):
                        step(s, g, False)
                    taken.give_back()
                for s in range(UNITS):
                    step(s, GROUPS - 1, True)

            @block.scalar
            def _(act):
                taken = Taken(act)

                def copy_ctx(grp):
                    nc.scalar.activation(ctxg_hi[:, :, :], ctx_hi[:, grp, :], ACT.Copy)
                    nc.scalar.activation(ctxg_lo[:, :, :], ctx_lo[:, grp, :], ACT.Copy).then_inc(ctxg_ready, 1)

                def split_x(hi, whole=None):
                    act.wait_ge(xnT_mm, taken.next(xnT_mm))
                    if whole is not None:
                        nc.scalar.activation(whole, xnT_ps[:, :], ACT.Copy)
                    nc.scalar.activation(hi, xnT_ps[:, :], ACT.Copy).then_inc(xn_hi_ready, 1)

                def step(s, g, last):
                    if s >= 0:
                        act.wait_ge(probT_mm, taken.next(probT_mm))
                        nc.scalar.activation(probT[:, :], probT_ps[0:CTX, :], ACT.Copy).then_inc(probT_ready, 1)
                    if it := item(s, 1, last):
                        _, u = it
                        act.wait_ge(vals_mm, taken.next(vals_mm))
                        nc.scalar.activation(vals[u % 2][0:ORG, :], val_ps[0:ORG, :], ACT.Copy).then_inc(vals_ready, 1)
                    if s == 13 and not last:
                        split_x(xn_hi[:, :])
                    if s == 13 and last:
                        split_x(moe_hi[:, 0, :], xnT[:, :])
                    if s == 14 and not last:
                        copy_ctx(bass.ds(g * GB + GB, GB))
                    if it := item(s, 7, last):
                        _, k = it
                        q, h = divmod(k, QH)
                        act.wait_ge(keys_mm, taken.next(keys_mm))
                        nc.scalar.activation(keys_hi[q % 2][:, :, h, 0:ORG],
                                             key_bank(s)[:, 0:GB * ORG].rearrange("p (b k) -> p b k", b=GB),
                                             ACT.Copy).then_inc(keys_hi_ready, 1)
                    if it := item(s, 2, last):
                        _, u = it
                        act.wait_ge(shift_ready, taken.next(shift_ready))
                        nc.scalar.activation(expd[u % 2][:, :, :], shifted[u % 2][:, :, :], ACT.Exp).then_inc(exp_ready, 1)

                copy_ctx(slice(0, GB))
                for s in range(-7, 0):
                    step(s, 0, False)
                taken.give_back()
                with act.Fori(0, GROUPS - 1) as g:
                    for s in range(UNITS):
                        step(s, g, False)
                    taken.give_back()
                for s in range(UNITS):
                    step(s, GROUPS - 1, True)
                act.wait_ge(raw_in, 16 * (2 + len(firsts)))

            @block.vector
            def _(dve):
                taken = Taken(dve)

                def stat(b, xb, last_one):
                    op = nc.vector.bn_stats(stats[:, b, :], xb)
                    if last_one:
                        op.then_inc(d_stat, 1)

                def aggregate():
                    dve.wait_ge(d_stat, taken.next(d_stat))
                    for b in range(GB):
                        op = nc.vector.bn_aggr(mv[:, b, :], stats[:, b, :])
                    op.then_inc(var_ready, 1)

                def normalise(b, xb):
                    if b == 0:
                        dve.wait_ge(rstd_ready, taken.next(rstd_ready))
                    op = nc.vector.tensor_scalar(xn[:, b, :], xb, mv[:, b, 0:1], rstd[:, b:b + 1],
                                                 ALU.subtract, ALU.mult)
                    if b == GB - 1:
                        op.then_inc(xn_ready, 1)

                def split_x(hi, lo):
                    dve.wait_ge(xn_hi_ready, taken.next(xn_hi_ready))
                    nc.vector.tensor_tensor(lo, xnT_ps[:, :], hi, ALU.subtract).then_inc(xnT_ready, 1)

                def step(s, g, last):
                    if it := item(s, 1, last):
                        _, u = it
                        dve.wait_ge(exp_ready, taken.next(exp_ready))
                        for part, _, seg in segs(expd[u % 2]):
                            op = nc.vector.tensor_reduce(total[:, u % 2, seg, :], part, AX.X, ALU.add)
                        op.then_inc(d_sum, 1)
                        dve.wait_ge(d_sum, taken.next(d_sum))
                        nc.vector.reciprocal(inv[:, u % 2, :, :], total[:, u % 2, :, :]).then_inc(inv_ready, 1)
                    if it := item(s, 2, last):
                        _, u = it
                        score = score_ps[u % 2][:, 0:QCOLS].rearrange("p (h k) -> p h k", h=QH)
                        dve.wait_ge(score_mm, taken.next(score_mm))
                        for part, _, seg in segs(score):
                            op = nc.vector.tensor_reduce(top[:, u % 2, seg, :], part, AX.X, ALU.max)
                        op.then_inc(d_max, 1)
                        dve.wait_ge(d_max, taken.next(d_max))
                        for (part, n, seg), (out, _, _) in zip(segs(score), segs(shifted[u % 2])):
                            op = nc.vector.tensor_tensor(out, part, bcast(top[:, u % 2, seg, :], n), ALU.subtract)
                        op.then_inc(shift_ready, 1)
                    if s == 13 and not last:
                        split_x(xn_hi[:, :], xn_lo[:, :])
                    if s == 13 and last:
                        split_x(moe_hi[:, 0, :], moe_lo[:, 0, :])
                    if it := item(s, 7, last):
                        _, k = it
                        q, h = divmod(k, QH)
                        dve.wait_ge(keys_hi_ready, taken.next(keys_hi_ready))
                        nc.vector.tensor_tensor(keys_lo[q % 2][:, :, h, 0:ORG],
                                                key_bank(s)[:, 0:GB * ORG].rearrange("p (b k) -> p b k", b=GB),
                                                keys_hi[q % 2][:, :, h, 0:ORG], ALU.subtract).then_inc(keys_lo_ready, 1)
                    if s >= 0:
                        def row(b):
                            return x[:, b, :] if last else x[:, bass.ds(g * GB + GB + b, 1), :].rearrange("p a d -> p (a d)")

                        if s < GB:
                            stat(s, row(s), s == GB - 1)
                        if s == GB:
                            aggregate()
                        if NORM <= s < NORM + GB:
                            normalise(s - NORM, row(s - NORM))
                    if s == UNITS - 1:
                        xg = x[:, bass.ds(g * GB, GB), :] if not isinstance(g, int) else x[:, g * GB:(g + 1) * GB, :]
                        dve.wait_ge(bias_added, taken.next(bias_added))
                        dve.wait_ge(acc_mm, taken.next(acc_mm))
                        nc.vector.tensor_tensor(xg, acc[:, :].rearrange("p (b d) -> p b d", b=GB), xg, ALU.add)\
                          .then_inc(acc_free, 1)

                dve.sem_inc(acc_free, 1)
                dve.sem_inc(xnT_ready, 1)
                for s in range(-7, 0):
                    step(s, 0, False)
                taken.give_back()
                with dve.Fori(0, GROUPS - 1) as g:
                    for s in range(UNITS):
                        step(s, g, False)
                    taken.give_back()
                for s in range(UNITS):
                    step(s, GROUPS - 1, True)

            @block.gpsimd
            def _(pool):
                taken = Taken(pool)

                def ipa_keys(q, grp):
                    for slot, src in ((keys_hi, kipa_hi), (keys_lo, kipa_lo)):
                        op = nc.gpsimd.tensor_copy(slot[q % 2][:, :, :, ORG:CTX].rearrange("p b h t -> p h b t"),
                                                   src[:, q * QH:(q + 1) * QH, grp, :])
                    return op

                def rstd_of_group():
                    pool.wait_ge(var_ready, taken.next(var_ready))
                    nc.gpsimd.tensor_scalar(veps[:, :], mv[:, :, 1], EPS, None, ALU.add).then_inc(p_var, 1)
                    pool.wait_ge(p_var, taken.next(p_var))
                    nc.gpsimd.tensor_tensor(rstd[:, :], veps[:, :], neg_half[:, :], ALU.pow).then_inc(rstd_ready, 1)

                def step(s, g, last):
                    if it := item(s, 1, last):
                        _, u = it
                        pool.wait_ge(inv_ready, taken.next(inv_ready))
                        for (part, n, seg), (out, _, _) in zip(segs(expd[u % 2]), segs(prob[u % 2])):
                            op = nc.gpsimd.tensor_tensor(out, part, bcast(inv[:, u % 2, seg, :], n), ALU.mult)
                        op.then_inc(norm_ready, 1)
                    if s >= 0 and (s + 1) % GB == GB - 1 and item(s, 6, last):
                        dg, u = item(s, 6, last)
                        q = u // GB
                        ipa_keys(q, bass.ds(g * GB + dg * GB, GB) if not isinstance(g, int) else
                                 slice((g + dg) * GB, (g + dg + 1) * GB))
                    if s == 5:
                        rstd_of_group()
                    if s == 9:
                        xg = x[:, bass.ds(g * GB, GB), :] if not isinstance(g, int) else x[:, g * GB:(g + 1) * GB, :]
                        nc.gpsimd.tensor_tensor(xg, xg, bias[:, :].unsqueeze(1).to_broadcast([P, GB, DIM]), ALU.add)\
                          .then_inc(bias_added, 1)

                ipa_keys(0, slice(0, GB))
                ipa_keys(1, slice(0, GB)).then_inc(ipa_keys_first, 1)
                for s in range(-7, 0):
                    step(s, 0, False)
                taken.give_back()
                with pool.Fori(0, GROUPS - 1) as g:
                    for s in range(UNITS):
                        step(s, g, False)
                    taken.give_back()
                for s in range(UNITS):
                    step(s, GROUPS - 1, True)

            @block.sync
            def _(sp):
                taken = Taken(sp)

                def fetch(u, row):
                    q = u // GB
                    sp.dma_start(vals[u % 2][ORG:CTX, :], vipa_dram[row, q * QH * DIM:(q + 1) * QH * DIM])\
                      .then_inc(vipa_in[u % 2], 16)

                def step(s, g, last):
                    sp.wait_ge(vals_slot, taken.next(vals_slot))
                    if it := item(s, 1, last):
                        dg, u = it
                        b = u % GB
                        start = (g * GB + dg * GB + b) * IPA
                        fetch(u, slice(start, start + IPA) if isinstance(g, int) else bass.ds(start, IPA))

                fetch(0, slice(0, IPA))
                for out_, in_ in firsts:
                    sp.dma_start(out_, in_).then_inc(raw_in, 16)
                sp.dma_start(w1_raw[:, :, :], d["w1T"].rearrange("e h f -> h e f")).then_inc(raw_in, 16)
                sp.dma_start(w2_raw[:, :, :, :], d["w2T"].rearrange("e (c p) h -> p e c h", p=P)).then_inc(raw_in, 16)
                with sp.Fori(0, GROUPS - 1) as g:
                    for s in range(UNITS):
                        step(s, g, False)
                    taken.give_back()
                for s in range(UNITS):
                    step(s, GROUPS - 1, True)
    return experts, (routerT, scal2, b1, b2), (xnT, moe_hi, moe_lo)


EXPERTS, FFN = 8, 512
FCH = FFN // P
LORA_R = 16
LORA_SCALING = 2.0
QMAX = 127.0
ROUND = 1.5 * 2.0 ** 23
ISCALE = DIM ** -0.5
MLP = 7
PARTS = EXPERTS + 1
SLOTS = PARTS * FCH
AHEAD = 3


class At:
    KEYS = 1
    MOE_OUT = 3
    MOE_ADD = 2
    ATT_STATS = 3
    VALUES = 5
    ATT_NORM = 5
    ATT_TURN = 8
    ATT_LOW = 8
    QUERIES = 11
    SCORES = 15
    MAX = 14
    EXP = 15
    TOTAL = 16
    PROB_TURN = 20
    ATT_OUT = 21
    ATT_ADD = 21
    MLP_STATS = 21
    MLP_NORM = 22
    MLP_TURN = 24
    MLP_LOW = 24
    MLP_COPY = 30
    MLP_OUT = 32
    MLP_ADD = 30
    ROUTE_STATS = 7
    ROUTE_NORM = 11
    ROUTE_TURN = 13
    LOGITS = 15
    TOP_TWO = 15
    MOE_SPLIT = 18
    TANH = 16
    COMBINE = 17
    COMB_TURN = 21

    EXPERT = (1, 1, 2)
    PREPARE = (4, 8, 20, 21, 23, 24, 27, 28, 31)


class Late(At):
    MLP_COPY = MLP_OUT = MLP_ADD = SLOTS - 1


class Tail:
    KEYS = 0
    MOE_OUT = 0
    MOE_ADD = 2
    ATT_STATS = 2
    VALUES = 3
    ATT_NORM = 5
    ATT_TURN = 5
    ATT_LOW = 7
    QUERIES = 10
    SCORES = 15
    MAX = 13
    EXP = 15
    TOTAL = 15
    PROB_TURN = 17
    ATT_OUT = 21
    ATT_ADD = 21
    MLP_STATS = 21
    MLP_NORM = 22
    MLP_TURN = 24
    MLP_LOW = 24
    MLP_COPY = 31
    MLP_OUT = 33
    MLP_ADD = 33


def lo_from_pool(u):
    return u % 4 == 2


def rest(nc, d, x, experts, firsts, rows, raw_in, out):
    with ExitStack() as ctx:
        def sb(name, shape, dt=F32):
            return ctx.enter_context(nc.sbuf_tensor(name, shape, dt))

        def sem(name):
            return ctx.enter_context(nc.semaphore(name))

        ident = sb("ident2", [P, P])
        w1_hi = sb("w1_hi", [P, EXPERTS, FFN], F32R)
        w2_hi = sb("w2_hi", [P, EXPERTS, FCH, DIM], F32R)
        w1_raw, w1_lo, w2_raw, w2_lo = experts
        routerT, scal, b1, b2 = firsts
        xnT, moe_hi, moe_lo = rows
        fc_hi, fc_lo = (sb(n, [P, FFN], F32R) for n in ("fc_hi", "fc_lo"))
        pj_hi, pj_lo = (sb(n, [P, FCH, DIM], F32R) for n in ("pj_hi", "pj_lo"))
        q_hi, q_lo = (sb(n, [DIM, DIM], F32R) for n in ("wq1_hi", "wq1_lo"))
        wk, wv = (sb(n, [CDIM, DIM]) for n in ("wk1", "wv1"))
        b_fc = sb("b_fc", [P, FCH])
        bq, bk, b_pj = (sb(n, [P, 1]) for n in ("bq", "bk", "b_pj"))
        gates = sb("gates", [P, 4])
        neg_gate = sb("neg_gate", [P, 1])
        neg_half = sb("neg_half1", [P, GB])
        iota = sb("iota8", [P, EXPERTS])
        comb_dram = nc.dram_tensor("comb_scratch", [GROUPS, EXPERTS, GTOK], F32, kind="Internal").ap()

        quant = sb("quant", [P, 2, FFN])
        work = sb("work", [P, 2, FFN])
        most, most_all, qscale, qinv = (sb(n, [P, 2]) for n in ("most", "most_all", "qscale", "qinv"))
        a_fc, bT_fc = sb("a_fc", [LORA_R, DIM]), sb("bT_fc", [LORA_R, FFN])
        a_pj, bT_pj = sb("a_pj", [LORA_R, FFN]), sb("bT_pj", [LORA_R, DIM])
        wq = sb("wq1", [DIM, DIM])
        bv = sb("bv", [P, DIM])
        small_in, quant_in = sem("small_in"), sem("quant_in")
        ident0, ident_ok, iota_ok = (sem(n) for n in ("ident2_zeroed", "ident2_ok", "iota_ok"))
        w_hi_ok, q_hi_ok, gates_ok = (sem(n) for n in ("w_hi_ok", "q_hi_ok", "gates_ok"))
        w2_ok, most_ok, prepared = (sem(n) for n in ("w2_ok", "most_ok", "prepared"))
        w1_ok, all_ok, lora_mm = (sem(n) for n in ("w1_ok", "all_ok", "lora_mm"))
        smalls = [
            (a_fc[:, :], d["a_fc"]), (bT_fc[:, :], d["b_fcT"]), (a_pj[:, :], d["a_pj"]), (bT_pj[:, :], d["b_pjT"]),
            (wq[:, :], d["wq1"]), (wk[:, :], d["wk1"]), (wv[:, :], d["wv1"]), (b_fc[:, :], d["b_fc"]),
            (bq[:, :], d["bq1"].rearrange("(p a) -> p a", a=1)), (bk[:, :], d["bk1"].rearrange("(p a) -> p a", a=1)),
            (b_pj[:, :], d["b_proj"].rearrange("(p a) -> p a", a=1)), (bv[:, :], d["bv1"].partition_broadcast(P)),
        ]

        def pb(name):
            return ctx.enter_context(nc.psum_tensor(name, [P, 512], F32))

        hid_ps = [pb(f"hid_ps{i}") for i in range(AHEAD)]
        y_ps = [pb(f"y_ps{i}") for i in range(2)]
        turn_ps, att_ps, out_ps = pb("turn_ps"), pb("att_ps"), pb("out_ps")

        hid = [sb(f"hid{i}", [P, GTOK]) for i in range(AHEAD)]
        hid_hi = [sb(f"hid_hi{i}", [P, GTOK], F32R) for i in range(AHEAD)]
        hid_lo = [sb(f"hid_lo{i}", [P, GTOK], F32R) for i in range(AHEAD)]
        part = [sb(f"part{i}", [P, GTOK]) for i in range(2)]
        y_sum = sb("y_sum", [P, GTOK])
        comb_all = sb("comb_all", [P, EXPERTS, GTOK])
        two_hi, two_lo = (sb(n, [P, GTOK], F32R) for n in ("two_hi", "two_lo"))
        xn = sb("xn_rest", [P, GB, DIM])
        stats, mv = sb("stats1", [P, GB, 6]), sb("mean_var1", [P, GB, 2])
        veps, rstd = sb("var_eps1", [P, GB]), sb("rstd1", [P, GB])
        best = sb("best", [P, GB, 8])
        best_at = sb("best_at", [P, GB, 8], mybir.dt.uint32)
        best_f = sb("best_f", [P, GB, 2])
        lead, lead_t = sb("lead", [P, GB]), sb("lead_tanh", [P, GB])
        weight = sb("weight", [P, 2, GB])
        hot = sb("hot", [P, 2, GB, EXPERTS])
        comb = sb("comb", [P, GB, EXPERTS])
        combT = sb("combT", [EXPERTS, GTOK])
        ctxg = sb("ctxg1", [CDIM, GB, CTX])
        k1 = sb("k1", [DIM, GB, CTX])
        v1 = sb("v1", [CTX, GB, DIM])
        q1 = sb("q1", [DIM, GTOK])
        s1, e1, p1 = (sb(n, [P, GB, CTX]) for n in ("att_shifted", "att_expd", "att_probs"))
        p1T = sb("att_probsT", [CTX, GTOK])
        top1, total1, inv1 = (sb(n, [P, GB]) for n in ("top1", "total1", "inv1"))
        yT = sb("mlp_outT", [P, GTOK])

        hid_ready, hid_ready_pool = sem("hid_ready"), sem("hid_ready_pool")
        route_x, att_x, mlp_x = (sem(n) for n in ("route_x", "att_x", "mlp_x"))
        routeT_ready = sem("routeT_ready")
        moeT_ready, attT_ready, mlpT_ready = (sem(n) for n in ("moeT_ready", "attT_ready", "mlpT_ready"))
        comb_ready = sem("comb_ready")
        y_ready = sem("y_ready")
        ctxg_in = sem("ctxg_in")
        att_act = sem("att_act")
        vals_ok = sem("vals_ok")
        att_prob = sem("att_prob")
        mlp_out = sem("mlp_out")
        hid_mm, turn_mm, att_mm, mlp_mm = (sem(n) for n in ("hid_mm", "turn_mm", "att_mm", "mlp_mm"))
        att_shift, lead_ok = sem("att_shift"), sem("lead_ok")
        gelu_ready, two_hi_ok, tanh_ready, att_exp = (sem(n) for n in ("gelu_ready", "two_hi_ok", "tanh_ready", "att_exp"))
        y_mm, out_mm, logit_mm, score_mm, val_mm = (sem(n) for n in ("y_mm", "out_mm", "logit_mm", "score1_mm", "val_mm"))
        rstd_ok, summed = sem("rstd1_ok"), sem("summed")
        comb_in = [sem(f"comb_in{e}") for e in range(EXPERTS)]
        own = sem("dve_own")
        var_ok, part_ok, inv_ok, p_own = (sem(n) for n in ("var_ok", "part_ok", "inv_ok", "pool_own"))
        gelu_for_pool = sem("gelu_for_pool")
        comb_free, combT_ok, comb_out, x_done = (sem(n) for n in ("comb_free", "combT_ok", "comb_out", "x_done"))
        stored = sem("stored")

        class Round:

            def __init__(self, r, experts, two, route):
                self.r, self.experts, self.two, self.route = r, experts, two, route
                self.loop = not isinstance(r, int)
                self.first = not self.loop and r == 0
                self.late = experts and not route
                self.mlp = PARTS - 1 if self.late else MLP
                self.at = At if route else Late if self.late else Tail

            def has(self, u):
                if u < 0:
                    return False
                if u >= SLOTS:
                    return self.route
                return self.two if u // FCH == self.mlp else self.experts

            def expert(self, part):
                return part if part < self.mlp else part - 1

            def ahead(self, s):
                mlp = MLP * FCH
                if self.first and mlp - AHEAD <= s < mlp:
                    return s + AHEAD + FCH
                if self.first and mlp <= s < mlp + FCH:
                    return -1
                return s + AHEAD

            def buffer(self, u):
                return (u + 1 if self.first and u < MLP * FCH else u) % AHEAD

            def mlp_bank(self):
                return turn_ps if self.late else out_ps

            def group(self, off):
                g = self.r + off
                return bass.ds(g, 1) if self.loop else slice(g, g + 1)

            def batches(self, off):
                g = (self.r + off) * GB
                return bass.ds(g, GB) if self.loop else slice(g, g + GB)

            def batch(self, off, b):
                g = (self.r + off) * GB + b
                return bass.ds(g, 1) if self.loop else slice(g, g + 1)

            def parity(self, off):
                p = (self.r + off) % 2
                return bass.ds(p, 1) if self.loop else slice(p, p + 1)

        def rounds(eng, taken, body):
            body(Round(0, True, False, True))
            taken.give_back()
            with eng.Fori(1, GROUPS - 1) as r:
                body(Round(r, True, True, True))
                taken.give_back()
            body(Round(GROUPS - 1, True, True, False))
            taken.give_back()
            body(Round(GROUPS, False, True, False))

        def flat(ap):
            return ap.rearrange("p a b -> p (a b)")

        with nc.Block() as block:
            @block.tensor
            def _(pe):
                taken = Taken(pe)

                def three(out_, a, b):
                    nc.tensor.matmul(out_, a[0], b[0], start=True, stop=False)
                    nc.tensor.matmul(out_, a[0], b[1], start=False, stop=False)
                    return nc.tensor.matmul(out_, a[1], b[0], start=False, stop=True)

                def turn(ready):
                    pe.wait_ge(ready, taken.next(ready))
                    for b in range(GB):
                        mm = nc.tensor.transpose(turn_ps[:, b * TOK:(b + 1) * TOK], xn[:, b, :], ident[:, :])
                    mm.then_inc(turn_mm, 1)

                def up(R, u):
                    if not R.has(u):
                        return
                    k, c = divmod(u % SLOTS, FCH)
                    if k == R.mlp:
                        if c == 0:
                            pe.wait_ge(mlpT_ready, taken.next(mlpT_ready))
                        w, rhs = [t[:, c * P:(c + 1) * P] for t in (fc_hi, fc_lo)], [t[:, :] for t in (two_hi, two_lo)]
                    else:
                        if u % SLOTS == 0 and not (R.first and u == 0):
                            pe.wait_ge(moeT_ready, taken.next(moeT_ready))
                        e = R.expert(k)
                        if R.first and u < SLOTS and c == 0:
                            pe.wait_ge(w1_ok, e + 1)
                        w = [t[:, e, c * P:(c + 1) * P] for t in (w1_hi, w1_lo)]
                        rhs = [flat(t[:, R.parity(u // SLOTS), :]) for t in (moe_hi, moe_lo)]
                    three(hid_ps[R.buffer(u)][:, :], w, rhs).then_inc(hid_mm, 1)

                def down(R, u):
                    if not R.has(u):
                        return
                    k, c = divmod(u, FCH)
                    ready = hid_ready_pool if lo_from_pool(u) else hid_ready
                    pe.wait_ge(ready, taken.next(ready))
                    if k == R.mlp:
                        w = [t[:, c, :] for t in (pj_hi, pj_lo)]
                    else:
                        if R.first and c == 0:
                            pe.wait_ge(w2_ok, R.expert(k) + 1)
                        w = [t[:, R.expert(k), c, :] for t in (w2_hi, w2_lo)]
                    h = [t[R.buffer(u)][:, :] for t in (hid_hi, hid_lo)]
                    y = (att_ps if k == R.mlp else y_ps[R.expert(k) % 2])[:, :]
                    nc.tensor.matmul(y, w[0], h[0], start=(c == 0), stop=False)
                    nc.tensor.matmul(y, w[1], h[0], start=False, stop=False)
                    mm = nc.tensor.matmul(y, w[0], h[1], start=False, stop=(c == FCH - 1))
                    if c == FCH - 1:
                        mm.then_inc(mlp_mm if k == R.mlp else y_mm, 1)

                def body(R):
                    for s in range(SLOTS):
                        down(R, s)
                        up(R, R.ahead(s))
                        if R.first:
                            prepare(s)
                        if R.two and s == R.at.KEYS:
                            pe.wait_ge(ctxg_in, taken.next(ctxg_in, 16))
                            nc.tensor.matmul(att_ps[:, 0:GB * CTX], wk[:, :], flat(ctxg[:, :, :]), start=True, stop=True)\
                              .then_inc(att_mm, 1)
                        if R.two and s == R.at.MOE_OUT:
                            pe.wait_ge(y_ready, taken.next(y_ready))
                            for b in range(GB):
                                mm = nc.tensor.transpose(out_ps[:, b * DIM:(b + 1) * DIM], y_sum[:, b * TOK:(b + 1) * TOK],
                                                         ident[:, :])
                            mm.then_inc(out_mm, 1)
                        if R.two and s == R.at.VALUES:
                            pe.wait_ge(att_act, taken.next(att_act))
                            for b in range(GB):
                                mm = nc.tensor.matmul(att_ps[0:CTX, b * DIM:(b + 1) * DIM], ctxg[:, b, :], wv[:, :],
                                                      start=True, stop=True)
                            mm.then_inc(val_mm, 1)
                        if R.two and s == R.at.ATT_TURN:
                            turn(att_x)
                        if R.two and s == R.at.QUERIES:
                            pe.wait_ge(attT_ready, taken.next(attT_ready))
                            pe.wait_ge(vals_ok, taken.next(vals_ok))
                            three(att_ps[:, :], [q_hi[:, :], q_lo[:, :]], [two_hi[:, :], two_lo[:, :]]).then_inc(att_mm, 1)
                        if R.two and s == R.at.SCORES:
                            pe.wait_ge(att_act, taken.next(att_act))
                            for b in range(GB):
                                mm = nc.tensor.matmul(att_ps[:, b * CTX:(b + 1) * CTX], q1[:, b * TOK:(b + 1) * TOK],
                                                      k1[:, b, :], start=True, stop=True)
                            mm.then_inc(score_mm, 1)
                        if R.route and s == R.at.ROUTE_TURN:
                            turn(route_x)
                        if R.route and s == R.at.LOGITS:
                            pe.wait_ge(routeT_ready, taken.next(routeT_ready))
                            for b in range(GB):
                                mm = nc.tensor.matmul(turn_ps[:, b * EXPERTS:(b + 1) * EXPERTS], xnT[:, b * TOK:(b + 1) * TOK],
                                                      routerT[:, :], start=True, stop=True)
                            mm.then_inc(logit_mm, 1)
                        if R.two and s == R.at.PROB_TURN:
                            pe.wait_ge(att_prob, taken.next(att_prob))
                            for b in range(GB):
                                mm = nc.tensor.transpose(att_ps[0:CTX, b * TOK:(b + 1) * TOK], p1[:, b, :], ident[:, :])
                            mm.then_inc(att_mm, 1)
                        if R.two and s == R.at.ATT_OUT:
                            pe.wait_ge(att_act, taken.next(att_act))
                            for b in range(GB):
                                mm = nc.tensor.matmul(out_ps[:, b * DIM:(b + 1) * DIM], p1T[:, b * TOK:(b + 1) * TOK],
                                                      v1[:, b, :], start=True, stop=True)
                            mm.then_inc(out_mm, 1)
                        if R.route and s == R.at.COMB_TURN:
                            pe.wait_ge(comb_ready, taken.next(comb_ready))
                            for b in range(GB):
                                mm = nc.tensor.transpose(turn_ps[0:EXPERTS, b * TOK:(b + 1) * TOK], comb[:, b, :], ident[:, :])
                            mm.then_inc(turn_mm, 1)
                        if R.two and s == R.at.MLP_TURN:
                            turn(mlp_x)
                        if R.two and s == R.at.MLP_OUT:
                            pe.wait_ge(mlp_out, taken.next(mlp_out))
                            for b in range(GB):
                                mm = nc.tensor.transpose(R.mlp_bank()[:, b * DIM:(b + 1) * DIM], yT[:, b * TOK:(b + 1) * TOK], ident[:, :])
                            mm.then_inc(out_mm, 1)

                def prepare(s):
                    if s == At.PREPARE[0]:
                        pe.wait_ge(small_in, 16 * len(smalls))
                        nc.tensor.matmul(att_ps[:, :], a_fc[:, :], bT_fc[:, :], start=True, stop=True)
                        for c in range(FCH):
                            mm = nc.tensor.matmul(out_ps[:, c * DIM:(c + 1) * DIM], a_pj[:, c * P:(c + 1) * P], bT_pj[:, :],
                                                  start=True, stop=True)
                        mm.then_inc(lora_mm, 1)
                    if s == SLOTS - 1:
                        pe.wait_ge(prepared, 1)

                R0 = Round(0, True, False, True)
                up(R0, 0)
                for b in range(GB):
                    mm = nc.tensor.matmul(turn_ps[:, b * EXPERTS:(b + 1) * EXPERTS], xnT[:, b * TOK:(b + 1) * TOK],
                                          routerT[:, :], start=True, stop=True)
                mm.then_inc(logit_mm, 1)
                for u in range(1, AHEAD):
                    up(R0, u)
                pe.wait_ge(ident_ok, 1)
                pe.wait_ge(comb_ready, taken.next(comb_ready))
                for b in range(GB):
                    mm = nc.tensor.transpose(turn_ps[0:EXPERTS, b * TOK:(b + 1) * TOK], comb[:, b, :], ident[:, :])
                mm.then_inc(turn_mm, 1)
                taken.give_back()
                rounds(pe, taken, body)

            @block.scalar
            def _(act):
                taken = Taken(act)

                def gelu(R, u):
                    if not R.has(u):
                        return
                    k, c = divmod(u % SLOTS, FCH)
                    bias = b_fc[:, c:c + 1] if k == R.mlp else b1[:, R.expert(k), c:c + 1]
                    act.wait_ge(hid_mm, taken.next(hid_mm))
                    nc.scalar.activation(hid[R.buffer(u)][:, :], hid_ps[R.buffer(u)][:, :], ACT.Gelu, bias=bias)
                    op = nc.scalar.activation(hid_hi[R.buffer(u)][:, :], hid_ps[R.buffer(u)][:, :], ACT.Gelu, bias=bias)
                    op.then_inc(gelu_for_pool if lo_from_pool(u) else gelu_ready, 1)

                def turned(out_):
                    act.wait_ge(turn_mm, taken.next(turn_mm))
                    return nc.scalar.activation(out_, turn_ps[0:out_.shape[0], :], ACT.Copy)

                def weights():
                    act.wait_ge(lead_ok, taken.next(lead_ok))
                    nc.scalar.activation(lead_t[:, :], lead[:, :], ACT.Tanh, scale=0.5).then_inc(tanh_ready, 1)

                def expert_hi(e):
                    nc.scalar.activation(w1_hi[:, e, :], w1_raw[:, e, :], ACT.Copy).then_inc(w_hi_ok, 1)

                def prepare(s):
                    if s % FCH == At.EXPERT[0] and s // FCH + 2 < EXPERTS:
                        expert_hi(s // FCH + 2)
                    if s == At.PREPARE[0]:
                        act.wait_ge(small_in, 16 * len(smalls))
                        nc.scalar.activation(q_hi[:, :], wq[:, :], ACT.Copy).then_inc(q_hi_ok, 1)
                    if s == SLOTS - 1:
                        act.wait_ge(prepared, 1)

                def body(R):
                    for s in range(SLOTS):
                        gelu(R, R.ahead(s))
                        if R.first:
                            prepare(s)
                        if R.two:
                            if s == R.at.KEYS:
                                act.wait_ge(att_mm, taken.next(att_mm))
                                nc.scalar.activation(flat(k1[:, :, :]), att_ps[:, 0:GB * CTX], ACT.Identity, bias=bk[:, 0:1])\
                                  .then_inc(att_act, 1)
                            if s == R.at.ATT_TURN:
                                turned(two_hi[:, :]).then_inc(two_hi_ok, 1)
                            if s == R.at.QUERIES:
                                act.wait_ge(att_mm, taken.next(att_mm))
                                nc.scalar.activation(q1[:, :], att_ps[:, :], ACT.Identity, bias=bq[:, 0:1], scale=ISCALE)\
                                  .then_inc(att_act, 1)
                            if s == R.at.EXP:
                                act.wait_ge(att_shift, taken.next(att_shift))
                                nc.scalar.activation(e1[:, :, :], s1[:, :, :], ACT.Exp).then_inc(att_exp, 1)
                            if s == R.at.PROB_TURN:
                                act.wait_ge(att_mm, taken.next(att_mm))
                                nc.scalar.activation(p1T[:, :], att_ps[0:CTX, :], ACT.Copy).then_inc(att_act, 1)
                            if s == R.at.MLP_TURN:
                                turned(two_hi[:, :]).then_inc(two_hi_ok, 1)
                            if s == R.at.MLP_COPY:
                                act.wait_ge(mlp_mm, taken.next(mlp_mm))
                                nc.scalar.activation(yT[:, :], att_ps[:, :], ACT.Identity, bias=b_pj[:, 0:1],
                                                     scale=gates[:, 2:3]).then_inc(mlp_out, 1)
                        if R.route:
                            if s == R.at.ROUTE_TURN:
                                turned(xnT[:, :]).then_inc(routeT_ready, 1)
                            if s == R.at.TANH:
                                weights()
                            if s == R.at.COMB_TURN:
                                turned(combT[:, :]).then_inc(combT_ok, 1)

                R0 = Round(0, True, False, True)
                expert_hi(0)
                nc.scalar.activation(gates[:, 0:3], scal[:, :], ACT.Tanh).then_inc(gates_ok, 1)
                gelu(R0, 0)
                weights()
                gelu(R0, 1)
                expert_hi(1)
                gelu(R0, 2)
                turned(combT[:, :]).then_inc(combT_ok, 1)
                taken.give_back()
                rounds(act, taken, body)

            @block.vector
            def _(dve):
                taken = Taken(dve)

                def done(op):
                    op.then_inc(own, 1)
                    dve.wait_ge(own, taken.next(own))

                def split(R, u):
                    if not R.has(u) or lo_from_pool(u):
                        return
                    i = R.buffer(u)
                    dve.wait_ge(gelu_ready, taken.next(gelu_ready))
                    nc.vector.tensor_tensor(hid_lo[i][:, :], hid[i][:, :], hid_hi[i][:, :], ALU.subtract).then_inc(hid_ready, 1)

                def statistics(xb):
                    for b in range(GB):
                        op = nc.vector.bn_stats(stats[:, b, :], flat(xb(b)))
                    done(op)
                    for b in range(GB):
                        op = nc.vector.bn_aggr(mv[:, b, :], stats[:, b, :])
                    op.then_inc(var_ok, 1)

                def normalise(xb, ready):
                    dve.wait_ge(rstd_ok, taken.next(rstd_ok))
                    for b in range(GB):
                        op = nc.vector.tensor_scalar(xn[:, b, :], flat(xb(b)), mv[:, b, 0:1], rstd[:, b:b + 1],
                                                     ALU.subtract, ALU.mult)
                    op.then_inc(ready, 1)

                def two_low(ready):
                    dve.wait_ge(two_hi_ok, taken.next(two_hi_ok))
                    nc.vector.tensor_tensor(two_lo[:, :], turn_ps[:, :], two_hi[:, :], ALU.subtract).then_inc(ready, 1)

                def add_out(R, off, after=None):
                    xg = x[:, R.batches(off), :]
                    dve.wait_ge(out_mm, taken.next(out_mm))
                    bank = out_ps if after is None else R.mlp_bank()
                    op = nc.vector.tensor_tensor(xg, bank[:, :].rearrange("p (b d) -> p b d", b=GB), xg, ALU.add)
                    if after is None:
                        done(op)
                    else:
                        op.then_inc(after, 1)

                def top_two():
                    dve.wait_ge(logit_mm, taken.next(logit_mm))
                    logits = turn_ps[:, 0:GB * EXPERTS].rearrange("p (b e) -> p b e", b=GB)
                    for b in range(GB):
                        op = nc.vector.max(best[:, b, :], logits[:, b, :])
                    done(op)
                    nc.vector.tensor_tensor(lead[:, :], best[:, :, 0], best[:, :, 1], ALU.subtract).then_inc(lead_ok, 1)
                    for b in range(GB):
                        op = nc.vector.max_index(best_at[:, b, :], best[:, b, :], logits[:, b, :])
                    done(op)
                    done(nc.vector.tensor_copy(best_f[:, :, :], best_at[:, :, 0:2]))
                    for n in range(2):
                        op = nc.vector.tensor_tensor(hot[:, n, :, :], iota[:, :].unsqueeze(1).to_broadcast([P, GB, EXPERTS]),
                                                     bcast(best_f[:, :, n], EXPERTS), ALU.is_equal)

                def combine():
                    dve.wait_ge(tanh_ready, taken.next(tanh_ready))
                    nc.vector.tensor_scalar(weight[:, 0, :], lead_t[:, :], gates[:, 3:4], gates[:, 3:4], ALU.mult, ALU.add)
                    done(nc.vector.tensor_scalar(weight[:, 1, :], lead_t[:, :], neg_gate[:, 0:1], gates[:, 3:4], ALU.mult, ALU.add))
                    for n in range(2):
                        op = nc.vector.tensor_tensor(hot[:, n, :, :], hot[:, n, :, :], bcast(weight[:, n, :], EXPERTS), ALU.mult)
                    done(op)
                    nc.vector.tensor_tensor(comb[:, :, :], hot[:, 0, :, :], hot[:, 1, :, :], ALU.add).then_inc(comb_ready, 1)

                def moe_split(par):
                    done(nc.vector.tensor_copy(flat(moe_hi[:, par, :]), xnT[:, :]))
                    nc.vector.tensor_tensor(flat(moe_lo[:, par, :]), xnT[:, :], flat(moe_hi[:, par, :]), ALU.subtract)\
                      .then_inc(moeT_ready, 1)

                def expert_split(e):
                    done(nc.vector.tensor_copy(w2_hi[:, e, :, :], w2_raw[:, e, :, :]))
                    nc.vector.tensor_tensor(w2_lo[:, e, :, :], w2_raw[:, e, :, :], w2_hi[:, e, :, :], ALU.subtract)\
                      .then_inc(w2_ok, 1)

                def prepare(s):
                    if s % FCH == At.EXPERT[1] and s // FCH + 2 < EXPERTS:
                        expert_split(s // FCH + 2)
                    at = At.PREPARE
                    if s == at[0]:
                        dve.wait_ge(quant_in, 32)
                        nc.vector.tensor_reduce(most[:, :], quant[:, :, :], AX.X, ALU.max,
                                                apply_absolute_value=True).then_inc(most_ok, 1)
                    if s == at[1]:
                        dve.wait_ge(all_ok, 1)
                        done(nc.vector.tensor_scalar(qscale[:, :], most_all[:, :], 1.0 / QMAX, None, ALU.mult))
                        done(nc.vector.reciprocal(qinv[:, :], qscale[:, :]))
                    for i in range(2):
                        if s == at[2 + i]:
                            w = work[:, i, :]
                            done(nc.vector.tensor_scalar(w, quant[:, i, :], qinv[:, i:i + 1], ROUND, ALU.mult, ALU.add))
                            done(nc.vector.tensor_scalar(w, w, ROUND, QMAX, ALU.subtract, ALU.min))
                            done(nc.vector.tensor_scalar(w, w, -QMAX - 1, qscale[:, i:i + 1], ALU.max, ALU.mult))
                    for i in range(2):
                        if s == at[4 + i]:
                            w = work[:, i, :]
                            done(nc.vector.tensor_tensor(w, w, quant[:, i, :], ALU.subtract))
                            done(nc.vector.tensor_tensor(w, w, quant[:, i, :], ALU.add))
                            if i == 0:
                                dve.wait_ge(lora_mm, 1)
                            done(nc.vector.scalar_tensor_tensor(out=w, in0=(att_ps, out_ps)[i][:, :], scalar=LORA_SCALING,
                                                                in1=w, op0=ALU.mult, op1=ALU.add))
                    for i, (hi, lo) in enumerate(((fc_hi[:, :], fc_lo[:, :]), (flat(pj_hi[:, :, :]), flat(pj_lo[:, :, :])))):
                        if s == at[6 + i]:
                            done(nc.vector.tensor_copy(hi, work[:, i, :]))
                            nc.vector.tensor_tensor(lo, work[:, i, :], hi, ALU.subtract)
                    if s == at[8]:
                        dve.wait_ge(q_hi_ok, 1)
                        nc.vector.tensor_tensor(q_lo[:, :], wq[:, :], q_hi[:, :], ALU.subtract)
                        nc.vector.tensor_scalar(bq[:, :], bq[:, :], ISCALE, None, ALU.mult)
                        nc.vector.tensor_scalar(b_pj[:, :], b_pj[:, :], gates[:, 2:3], None, ALU.mult)
                        op = nc.vector.tensor_scalar(bv[:, :], bv[:, :], gates[:, 1:2], None, ALU.mult)
                        op.then_inc(prepared, 1)

                def body(R):
                    for s in range(SLOTS):
                        if R.first:
                            prepare(s)
                        if R.experts and s % FCH == FCH - 1 and s // FCH != R.mlp:
                            e = R.expert(s // FCH)
                            dve.wait_ge(y_mm, taken.next(y_mm))
                            dve.wait_ge(comb_in[e], taken.next(comb_in[e], 16))
                            if e >= 2:
                                dve.wait_ge(summed, taken.next(summed))
                            nc.vector.scalar_tensor_tensor(out=part[e % 2][:, :], in0=y_ps[e % 2][:, :], scalar=b2[:, e:e + 1],
                                                           in1=comb_all[:, e, :], op0=ALU.add, op1=ALU.mult).then_inc(part_ok, 1)
                        split(R, R.ahead(s))
                        if R.two:
                            if s == R.at.VALUES:
                                dve.wait_ge(val_mm, taken.next(val_mm))
                                nc.vector.scalar_tensor_tensor(
                                    out=v1[:, :, :], in0=att_ps[0:CTX, :].rearrange("p (b d) -> p b d", b=GB),
                                    scalar=gates[0:CTX, 1:2], in1=bv[0:CTX, :].unsqueeze(1).to_broadcast([CTX, GB, DIM]),
                                    op0=ALU.mult, op1=ALU.add).then_inc(vals_ok, 1)
                            if s == R.at.MOE_ADD:
                                add_out(R, -1)
                            if s == R.at.ATT_STATS:
                                statistics(lambda b: x[:, R.batch(-1, b), :])
                            if s == R.at.ATT_NORM:
                                normalise(lambda b: x[:, R.batch(-1, b), :], att_x)
                            if s == R.at.ATT_LOW:
                                two_low(attT_ready)
                            if s == R.at.MAX:
                                dve.wait_ge(score_mm, taken.next(score_mm))
                                scores = att_ps[:, 0:GB * CTX].rearrange("p (b k) -> p b k", b=GB)
                                done(nc.vector.tensor_reduce(top1[:, :], scores, AX.X, ALU.max))
                                nc.vector.tensor_tensor(s1[:, :, :], scores, bcast(top1[:, :], CTX), ALU.subtract)\
                                  .then_inc(att_shift, 1)
                            if s == R.at.TOTAL:
                                dve.wait_ge(att_exp, taken.next(att_exp))
                                done(nc.vector.tensor_reduce(total1[:, :], e1[:, :, :], AX.X, ALU.add))
                                nc.vector.reciprocal(inv1[:, :], total1[:, :]).then_inc(inv_ok, 1)
                            if s == R.at.ATT_ADD:
                                add_out(R, -1)
                            if s == R.at.MLP_STATS:
                                statistics(lambda b: x[:, R.batch(-1, b), :])
                            if s == R.at.MLP_NORM:
                                normalise(lambda b: x[:, R.batch(-1, b), :], mlp_x)
                            if s == R.at.MLP_LOW:
                                two_low(mlpT_ready)
                            if s == R.at.MLP_ADD:
                                add_out(R, -1, x_done)
                        if R.route:
                            if s == R.at.ROUTE_STATS:
                                statistics(lambda b: x[:, R.batch(1, b), :])
                            if s == R.at.ROUTE_NORM:
                                normalise(lambda b: x[:, R.batch(1, b), :], route_x)
                            if s == R.at.TOP_TWO:
                                top_two()
                            if s == R.at.MOE_SPLIT:
                                moe_split(R.parity(1))
                            if s == R.at.COMBINE:
                                combine()

                R0 = Round(0, True, False, True)
                expert_split(0)
                dve.wait_ge(iota_ok, 1)
                top_two()
                split(R0, 0)
                dve.wait_ge(gates_ok, 1)
                nc.vector.tensor_scalar(gates[:, 3:4], gates[:, 0:1], 0.5, None, ALU.mult)
                done(nc.vector.tensor_scalar(neg_gate[:, :], gates[:, 0:1], -0.5, None, ALU.mult))
                combine()
                split(R0, 1)
                expert_split(1)
                split(R0, 2)
                taken.give_back()
                rounds(dve, taken, body)

            @block.gpsimd
            def _(pool):
                taken = Taken(pool)

                def root():
                    pool.wait_ge(var_ok, taken.next(var_ok))
                    nc.gpsimd.tensor_scalar(veps[:, :], mv[:, :, 1], EPS, None, ALU.add).then_inc(p_own, 1)
                    pool.wait_ge(p_own, taken.next(p_own))
                    nc.gpsimd.tensor_tensor(rstd[:, :], veps[:, :], neg_half[:, :], ALU.pow).then_inc(rstd_ok, 1)

                def split(R, u):
                    if not R.has(u) or not lo_from_pool(u):
                        return
                    i = R.buffer(u)
                    pool.wait_ge(gelu_for_pool, taken.next(gelu_for_pool))
                    nc.gpsimd.tensor_tensor(hid_lo[i][:, :], hid[i][:, :], hid_hi[i][:, :], ALU.subtract)\
                      .then_inc(hid_ready_pool, 1)

                def expert_lo(e):
                    pool.wait_ge(w_hi_ok, e + 1)
                    nc.gpsimd.tensor_tensor(w1_lo[:, e, :], w1_raw[:, e, :], w1_hi[:, e, :], ALU.subtract).then_inc(w1_ok, 1)

                def body(R):
                    for s in range(SLOTS):
                        split(R, R.ahead(s))
                        if R.first and s % FCH == At.EXPERT[2] and s // FCH + 2 < EXPERTS:
                            expert_lo(s // FCH + 2)
                        if R.first and s == At.PREPARE[0]:
                            pool.wait_ge(most_ok, 1)
                            nc.gpsimd.partition_all_reduce(most_all[:, :], most[:, :], P, bass.bass_isa.ReduceOp.max).then_inc(all_ok, 1)
                        if R.experts and s % FCH == FCH - 1 and s // FCH != R.mlp:
                            e = R.expert(s // FCH)
                            pool.wait_ge(part_ok, taken.next(part_ok))
                            pool.sem_inc(comb_free, 1)
                            if e == 1:
                                nc.gpsimd.tensor_tensor(y_sum[:, :], part[0][:, :], part[1][:, :], ALU.add).then_inc(summed, 1)
                            elif 1 < e < EXPERTS - 1:
                                nc.gpsimd.tensor_tensor(y_sum[:, :], y_sum[:, :], part[e % 2][:, :], ALU.add).then_inc(summed, 1)
                            elif e == EXPERTS - 1:
                                nc.gpsimd.tensor_tensor(y_sum[:, :], y_sum[:, :], part[e % 2][:, :], ALU.add).then_inc(y_ready, 1)
                        if R.two and s == R.at.ATT_STATS:
                            root()
                        if R.two and s == R.at.TOTAL:
                            pool.wait_ge(inv_ok, taken.next(inv_ok))
                            nc.gpsimd.tensor_tensor(p1[:, :, :], e1[:, :, :], bcast(inv1[:, :], CTX), ALU.mult).then_inc(att_prob, 1)
                        if R.two and s == R.at.MLP_STATS:
                            root()
                        if R.route and s == R.at.ROUTE_STATS:
                            root()

                nc.gpsimd.memset(neg_half[:, :], -0.5)
                nc.gpsimd.iota(iota[:, :], [[1, EXPERTS]], base=0, channel_multiplier=0,
                               allow_small_or_imprecise_dtypes=True).then_inc(iota_ok, 1)
                nc.gpsimd.memset(ident[:, :], 0.0).then_inc(ident0, 1)
                pool.wait_ge(ident0, 1)
                nc.gpsimd.affine_select(out=ident[:, :], in_=ident[:, :], compare_op=ALU.not_equal, fill=1.0,
                                        base=0, pattern=[[-1, P]], channel_multiplier=1).then_inc(ident_ok, 1)
                expert_lo(0)
                expert_lo(1)
                R0 = Round(0, True, False, True)
                for u in range(AHEAD):
                    split(R0, u)
                taken.give_back()
                rounds(pool, taken, body)

            @block.sync
            def _(sp):
                taken = Taken(sp)

                def context(g):
                    sp.dma_start(ctxg[:, :, :], d["ctxT"].rearrange("c (b t) -> c b t", b=BATCH)[:, g, :]).then_inc(ctxg_in, 16)

                def spill(R, off):
                    sp.wait_ge(combT_ok, taken.next(combT_ok))
                    sp.dma_start(comb_dram[R.group(off), :, :].rearrange("a e t -> (a e) t"), combT[:, :]).then_inc(comb_out, 16)
                    sp.wait_ge(comb_out, taken.next(comb_out, 16))

                def fetch(R, off, e):
                    sp.dma_start(comb_all[:, e, :], comb_dram[R.group(off), e, :].rearrange("a t -> (a t)").partition_broadcast(P))\
                      .then_inc(comb_in[e], 16)

                def body(R):
                    if R.two and R.experts:
                        sp.wait_ge(comb_free, taken.next(comb_free))
                        fetch(R, 0, EXPERTS - 1)
                    if R.route:
                        spill(R, 1)
                        context(R.batches(0))
                        for e in range(EXPERTS - 1):
                            sp.wait_ge(comb_free, taken.next(comb_free))
                            fetch(R, 1, e)
                    elif R.experts:
                        for _ in range(2):
                            sp.wait_ge(comb_free, taken.next(comb_free))
                        context(R.batches(0))
                    if R.two:
                        sp.wait_ge(x_done, taken.next(x_done))
                        sp.dma_start(out.rearrange("b t d -> t b d")[:, R.batches(-1), :], x[:, R.batches(-1), :]).then_inc(stored, 16)

                sp.dma_start(quant[:, 0, :], d["w_fcT"]).then_inc(quant_in, 16)
                sp.dma_start(quant[:, 1, :].rearrange("p (c d) -> p c d", c=FCH),
                             d["w_pjT"].rearrange("(c p) d -> p c d", p=P)).then_inc(quant_in, 16)
                for out_, in_ in smalls:
                    sp.dma_start(out_, in_).then_inc(small_in, 16)
                R0 = Round(0, True, False, True)
                spill(R0, 0)
                for e in range(EXPERTS):
                    fetch(R0, 0, e)
                taken.give_back()
                rounds(sp, taken, body)
                sp.wait_ge(stored, 16 * GROUPS)


def program(nc, d, out):
    with ExitStack() as ctx:
        x = ctx.enter_context(nc.sbuf_tensor("x_sb", [P, BATCH, DIM], F32))
        raw_in = ctx.enter_context(nc.semaphore("experts_in"))
        experts, firsts, rows = head_attention(nc, d, x, raw_in, ctx)
        rest(nc, d, x, experts, firsts, rows, raw_in, out)


_L0 = "L0_xattn_"
_PLAIN = {"x": "x", "g_xattn": "g_xattn", "g_ffn": "g_ffn", "q_up": _L0 + "q_up", "k_up": _L0 + "k_up", "v_up": _L0 + "v_up",
          "o_up": _L0 + "o_up", "wo": _L0 + "Wo", "bo": _L0 + "bo", "q_alpha": _L0 + "q_alpha",
          "k_alpha": _L0 + "k_alpha", "v_alpha": _L0 + "v_alpha", "o_alpha": _L0 + "o_alpha",
          "wq1": "L1_xattn_Wq", "bq1": "L1_xattn_bq", "wk1": "L1_xattn_Wk", "bk1": "L1_xattn_bk",
          "wv1": "L1_xattn_Wv", "bv1": "L1_xattn_bv", "a_fc": "L1_ffn_A_fc", "a_pj": "L1_ffn_A_proj", "b_proj": "L1_ffn_b_proj"}
_TURNED = {"q_downT": _L0 + "q_down", "k_downT": _L0 + "k_down", "v_downT": _L0 + "v_down", "o_downT": _L0 + "o_down",
           "b2": "L0_ffn_b2", "routerT": "L0_ffn_router_w", "w_fcT": "L1_ffn_W_fc", "b_fcT": "L1_ffn_B_fc", "w_pjT": "L1_ffn_W_proj",
           "b_pjT": "L1_ffn_B_proj", "wqT": _L0 + "Wq", "wkT": _L0 + "Wk", "wvT": _L0 + "Wv", "wkiT": _L0 + "Wk_ipa", "wviT": _L0 + "Wv_ipa"}


def kernel(**inputs):
    import numpy as _np
    import concourse.bacc as _bacc
    from concourse import mybir as _mybir
    from concourse.bass_utils import run_bass_kernel_spmd as _run

    given = {n: _np.ascontiguousarray(inputs[src]) for n, src in _PLAIN.items()}
    given |= {n: _np.ascontiguousarray(_np.asarray(inputs[src]).T) for n, src in _TURNED.items()}
    c = _np.asarray(inputs["ctx_768"])
    given["ctxT"] = _np.ascontiguousarray(c.reshape(-1, c.shape[-1]).T)
    for n, src in (("w1T", "L0_ffn_w1"), ("w2T", "L0_ffn_w2")):
        given[n] = _np.ascontiguousarray(_np.asarray(inputs[src]).transpose(0, 2, 1))
    for n, src in (("b1", "L0_ffn_b1"), ("b_fc", "L1_ffn_b_fc")):
        given[n] = _np.ascontiguousarray(_np.asarray(inputs[src]).reshape(-1, P).T)
    nc = _bacc.Bacc("TRN2", target_bir_lowering=False, num_devices=1)
    dram, arrays = {}, {}
    for n, a in given.items():
        arrays[f"in_{n}"] = a
        dram[n] = nc.dram_tensor(f"in_{n}", a.shape, _mybir.dt.from_np(a.dtype), kind="ExternalInput").ap()
    out = nc.dram_tensor("out_x", (BATCH, TOK, DIM), F32, kind="ExternalOutput").ap()
    program(nc, dram, out)
    r = _run(nc, [arrays], core_ids=[0])
    return r.results[0]["out_x"]
```
